# Optimizing a Trainium2 kernel written in Bass

```python
import numpy as np
import jax
import jax.numpy as jnp

def _softmax(x, axis=-1):
    return jax.nn.softmax(x, axis=axis)

def _gelu(x):
    return jax.nn.gelu(x, approximate=True)

def _silu(x):
    return jax.nn.silu(x)

def _sigmoid(x):
    return jax.nn.sigmoid(x)

def _layernorm(x, axis=-1, eps=1e-05):
    m = jnp.mean(x, axis=axis, keepdims=True)
    v = jnp.var(x, axis=axis, keepdims=True)
    return (x - m) / jnp.sqrt(v + eps)

def _scatter_add(tgt, idx, src, axis=0):
    return tgt.at[idx].add(src)

def _segment_sum(src, seg, n):
    return jax.ops.segment_sum(src, seg, n)
kernel_name = 'mk_adj_resnorm_d4_adj_r2_4b4061'

def setup_inputs(seed: int=0):
    np.random.seed(seed)
    _w = jnp.asarray

    def _rec_inputs():
        import jax
        import jax.numpy as jnp
        _gk = jax.random.key(seed)
        x = -0.000125 + 0.9999 * jax.random.normal(jax.random.fold_in(_gk, 1), (128, 64, 256), jnp.float32)
        _a = jax.random.bernoulli(jax.random.fold_in(_gk, 2), 0.125, (64, 64))
        _af = _a.astype(jnp.float32)
        adj = _af
        return (x, adj)
    x, adj = _rec_inputs()

    def _L0_gnn_setup():
        import jax, jax.numpy as jnp
        import numpy as np
        ALPHA = 0.2
        key = jax.random.key(seed)
        k0, k1, k2, k3 = jax.random.split(key, 4)
        B, N, C, F = (64, 512, 256, 256)
        x = jax.random.normal(k0, (B, N, C), dtype=jnp.float32)
        W = jax.random.normal(k1, (C, F), dtype=jnp.float32) * (1.414 / np.sqrt(C + F))
        a = jax.random.normal(k2, (2 * F, 1), dtype=jnp.float32) * (1.414 / np.sqrt(2 * F + 1))
        beta = jnp.ones((1,), dtype=jnp.float32)
        mask = (jax.random.uniform(k3, (N, N)) < 0.3).astype(jnp.float32)
        return {'x': x, 'W': W, 'a': a, 'beta': beta, 'mask': mask}
    _L0_gnn_all = _L0_gnn_setup()
    _L0_gnn_in = {k: v for k, v in _L0_gnn_all.items() if k in ('W', 'a', 'beta')}
    del _L0_gnn_all

    def _L1_gnn_setup():
        import jax, jax.numpy as jnp
        import numpy as np
        B, N, D, O = (8, 2048, 256, 256)
        key = jax.random.key(seed)
        k1, k2, k3, k4 = jax.random.split(key, 4)
        x = jax.random.normal(k1, (B, N, D), dtype=jnp.float32)
        adj = jax.random.uniform(k2, (N, N), dtype=jnp.float32)
        weight = jax.random.normal(k3, (D, O), dtype=jnp.float32) * 0.02
        bias = jax.random.normal(k4, (O,), dtype=jnp.float32) * 0.02
        return {'x': x, 'adj': adj, 'weight': weight, 'bias': bias}
    _L1_gnn_all = _L1_gnn_setup()
    _L1_gnn_in = {k: v for k, v in _L1_gnn_all.items() if k in ('weight', 'bias')}
    del _L1_gnn_all

    def _L2_gnn_setup():
        import jax, jax.numpy as jnp
        import numpy as np
        B, N, D, H = (16, 1025, 256, 8)
        LN_EPS = 1e-05

        def _make_mask(key, n):
            n_proto = n - 1
            adj = jax.random.bernoulli(key, 0.03, (n_proto, n_proto)).astype(jnp.float32)
            adj = jnp.clip(adj + adj.T + jnp.eye(n_proto, dtype=jnp.float32), 0.0, 1.0)
            mask = jnp.zeros((n, n), dtype=jnp.float32)
            mask = mask.at[0, :].set(1.0).at[:, 0].set(1.0)
            mask = mask.at[1:, 1:].set(adj)
            return mask
        key = jax.random.key(seed)
        ks = jax.random.split(key, 7)
        s = 1.0 / np.sqrt(D)
        return {'x': jax.random.normal(ks[0], (B, N, D), dtype=jnp.float32), 'w_qkv': jax.random.uniform(ks[1], (D, 3 * D), dtype=jnp.float32, minval=-s, maxval=s), 'w_proj': jax.random.uniform(ks[2], (D, D), dtype=jnp.float32, minval=-s, maxval=s), 'b_proj': jnp.zeros((D,), dtype=jnp.float32), 'ln_gamma': jnp.ones((D,), dtype=jnp.float32), 'ln_beta': jnp.zeros((D,), dtype=jnp.float32), 'attn_mask': _make_mask(ks[3], N)}
    _L2_gnn_all = _L2_gnn_setup()
    _L2_gnn_in = {k: v for k, v in _L2_gnn_all.items() if k in ('w_qkv', 'w_proj', 'b_proj', 'ln_gamma', 'ln_beta')}
    del _L2_gnn_all

    def _L3_gnn_setup():
        import jax, jax.numpy as jnp
        import numpy as np
        B, N, D, T = (64, 128, 256, 3)

        def _lin(v, W, b):
            return jnp.einsum('...i,oi->...o', v, W) + b
        key = jax.random.key(seed)
        ks = jax.random.split(key, 12)
        s2 = 1.0 / np.sqrt(2 * D)
        s1 = 1.0 / np.sqrt(D)
        return {'x': jax.random.normal(ks[0], (B, N, D), jnp.float32), 'in_mat': jax.random.uniform(ks[1], (N, N), jnp.float32) / N, 'out_mat': jax.random.uniform(ks[2], (N, N), jnp.float32) / N, 'w3_w': jax.random.normal(ks[3], (D, 2 * D), jnp.float32) * s2, 'w3_b': jnp.zeros((D,), jnp.float32), 'u3_w': jax.random.normal(ks[4], (D, D), jnp.float32) * s1, 'u3_b': jnp.zeros((D,), jnp.float32), 'w4_w': jax.random.normal(ks[5], (D, 2 * D), jnp.float32) * s2, 'w4_b': jnp.zeros((D,), jnp.float32), 'w5_w': jax.random.normal(ks[6], (D, 2 * D), jnp.float32) * s2, 'w5_b': jnp.zeros((D,), jnp.float32), 'u5_w': jax.random.normal(ks[7], (D, D), jnp.float32) * s1, 'u5_b': jnp.zeros((D,), jnp.float32)}
    _L3_gnn_all = _L3_gnn_setup()
    _L3_gnn_in = {k: v for k, v in _L3_gnn_all.items() if k in ('w3_w', 'w3_b', 'u3_w', 'u3_b', 'w4_w', 'w4_b', 'w5_w', 'w5_b', 'u5_w', 'u5_b')}
    del _L3_gnn_all
    return {'x': x, 'adj': adj, 'L0_gnn_W': _L0_gnn_in['W'], 'L0_gnn_a': _L0_gnn_in['a'], 'L0_gnn_beta': _L0_gnn_in['beta'], 'L1_gnn_weight': _L1_gnn_in['weight'], 'L1_gnn_bias': _L1_gnn_in['bias'], 'L2_gnn_w_qkv': _L2_gnn_in['w_qkv'], 'L2_gnn_w_proj': _L2_gnn_in['w_proj'], 'L2_gnn_b_proj': _L2_gnn_in['b_proj'], 'L2_gnn_ln_gamma': _L2_gnn_in['ln_gamma'], 'L2_gnn_ln_beta': _L2_gnn_in['ln_beta'], 'L3_gnn_w3_w': _L3_gnn_in['w3_w'], 'L3_gnn_w3_b': _L3_gnn_in['w3_b'], 'L3_gnn_u3_w': _L3_gnn_in['u3_w'], 'L3_gnn_u3_b': _L3_gnn_in['u3_b'], 'L3_gnn_w4_w': _L3_gnn_in['w4_w'], 'L3_gnn_w4_b': _L3_gnn_in['w4_b'], 'L3_gnn_w5_w': _L3_gnn_in['w5_w'], 'L3_gnn_w5_b': _L3_gnn_in['w5_b'], 'L3_gnn_u5_w': _L3_gnn_in['u5_w'], 'L3_gnn_u5_b': _L3_gnn_in['u5_b']}

def reference(x, adj, L0_gnn_W, L0_gnn_a, L0_gnn_beta, L1_gnn_weight, L1_gnn_bias, L2_gnn_w_qkv, L2_gnn_w_proj, L2_gnn_b_proj, L2_gnn_ln_gamma, L2_gnn_ln_beta, L3_gnn_w3_w, L3_gnn_w3_b, L3_gnn_u3_w, L3_gnn_u3_b, L3_gnn_w4_w, L3_gnn_w4_b, L3_gnn_w5_w, L3_gnn_w5_b, L3_gnn_u5_w, L3_gnn_u5_b):
    import jax
    import jax.numpy as jnp

    def _L0_gnn_ref(x, W, a, beta, mask):
        import jax, jax.numpy as jnp
        import numpy as np
        ALPHA = 0.2
        F_ = W.shape[1]
        h = jnp.einsum('bnc,cf->bnf', x, W)
        a1, a2 = (a[:F_, 0], a[F_:, 0])
        s1 = jnp.einsum('bnf,f->bn', h, a1)
        s2 = jnp.einsum('bnf,f->bn', h, a2)
        e = jax.nn.leaky_relu(s1[:, :, None] + s2[:, None, :], negative_slope=ALPHA)
        e = e * mask[None, :, :]
        att = jax.nn.softmax(e, axis=2)
        h_prime = jnp.einsum('bij,bjf->bif', att, h)
        return jax.nn.elu(h_prime + beta * h)

    def _L1_gnn_ref(x, adj, weight, bias):
        import jax, jax.numpy as jnp
        import numpy as np
        B, N, D, O = (8, 2048, 256, 256)
        y = jnp.einsum('nm,bmd->bnd', adj, x)
        out = jnp.einsum('bnd,do->bno', y, weight) + bias
        return out

    def _L2_gnn_ref(x, w_qkv, w_proj, b_proj, ln_gamma, ln_beta, attn_mask):
        import jax, jax.numpy as jnp
        import numpy as np
        B, N, D, H = (16, 1025, 256, 8)
        LN_EPS = 1e-05

        def _make_mask(key, n):
            n_proto = n - 1
            adj = jax.random.bernoulli(key, 0.03, (n_proto, n_proto)).astype(jnp.float32)
            adj = jnp.clip(adj + adj.T + jnp.eye(n_proto, dtype=jnp.float32), 0.0, 1.0)
            mask = jnp.zeros((n, n), dtype=jnp.float32)
            mask = mask.at[0, :].set(1.0).at[:, 0].set(1.0)
            mask = mask.at[1:, 1:].set(adj)
            return mask
        b, n, d = x.shape
        hd = d // H
        scale = hd ** (-0.5)
        qkv = (x @ w_qkv).reshape(b, n, 3, H, hd).transpose(2, 0, 3, 1, 4)
        q, k, v = (qkv[0], qkv[1], qkv[2])
        attn = jnp.einsum('bhnd,bhmd->bhnm', q, k) * scale
        attn = jnp.where(attn_mask[None, None] == 0, -jnp.inf, attn)
        attn = jax.nn.softmax(attn, axis=-1)
        o = jnp.einsum('bhnm,bhmd->bhnd', attn, v).transpose(0, 2, 1, 3).reshape(b, n, d)
        o = o @ w_proj + b_proj
        mu = jnp.mean(o, axis=-1, keepdims=True)
        var = jnp.mean(jnp.square(o - mu), axis=-1, keepdims=True)
        ln = (o - mu) * jax.lax.rsqrt(var + LN_EPS) * ln_gamma + ln_beta
        return o + ln

    def _L3_gnn_ref(x, in_mat, out_mat, w3_w, w3_b, u3_w, u3_b, w4_w, w4_b, w5_w, w5_b, u5_w, u5_b):
        import jax, jax.numpy as jnp
        import numpy as np
        B, N, D, T = (64, 128, 256, 3)

        def _lin(v, W, b):
            return jnp.einsum('...i,oi->...o', v, W) + b
        h = x
        for _ in range(T):
            a_in = jnp.einsum('nm,bmd->bnd', in_mat, h)
            a_out = jnp.einsum('nm,bmd->bnd', out_mat, h)
            av = jnp.concatenate([a_in, a_out], axis=-1)
            z = jax.nn.sigmoid(_lin(av, w3_w, w3_b) + _lin(h, u3_w, u3_b))
            r = jax.nn.sigmoid(_lin(av, w4_w, w4_b) + _lin(h, u3_w, u3_b))
            hv = jnp.tanh(_lin(av, w5_w, w5_b) + _lin(r * h, u5_w, u5_b))
            h = (1.0 - z) * h + z * hv
        return h
    x = _layernorm(x + _L0_gnn_ref(x, L0_gnn_W, L0_gnn_a, L0_gnn_beta, adj), axis=-1)
    x = _layernorm(x + _L1_gnn_ref(x, adj, L1_gnn_weight, L1_gnn_bias), axis=-1)
    x = _layernorm(x + _L2_gnn_ref(x, L2_gnn_w_qkv, L2_gnn_w_proj, L2_gnn_b_proj, L2_gnn_ln_gamma, L2_gnn_ln_beta, adj), axis=-1)
    x = _layernorm(x + _L3_gnn_ref(x, adj, adj, L3_gnn_w3_w, L3_gnn_w3_b, L3_gnn_u3_w, L3_gnn_u3_b, L3_gnn_w4_w, L3_gnn_w4_b, L3_gnn_w5_w, L3_gnn_w5_b, L3_gnn_u5_w, L3_gnn_u5_b), axis=-1)
    return x

_drawn_inputs = setup_inputs


def setup_inputs(seed=0):
    import zlib

    import numpy as np

    out = dict(_drawn_inputs(seed))
    spreads = {'L2_gnn_b_proj': (0.0, 0.1),
     'L2_gnn_ln_gamma': (1.0, 0.2),
     'L2_gnn_ln_beta': (0.0, 0.1),
     'L3_gnn_w3_b': (0.0, 0.308),
     'L3_gnn_u3_b': (0.0, 0.303),
     'L3_gnn_w4_b': (0.0, 2.0),
     'L3_gnn_w5_b': (0.0, 0.1),
     'L3_gnn_u5_b': (0.0, 0.1)}
    factors = {}
    for name, (base, spread) in spreads.items():
        noise = np.random.default_rng([zlib.crc32(name.encode()), seed]).standard_normal(out[name].shape)
        drawn = base * np.exp(spread * noise) if base else spread * noise
        out[name] = jnp.asarray(drawn.astype(out[name].dtype))
    for name, factor in factors.items():
        out[name] = (out[name] * factor).astype(out[name].dtype)
    return out
```

```python
from contextlib import ExitStack

import concourse.bass as bass
from concourse import mybir

F32 = mybir.dt.float32
F32R = mybir.dt.float32r
BF16 = mybir.dt.bfloat16
ALU = mybir.AluOpType
ACT = mybir.ActivationFunctionType
AX = mybir.AxisListType

GRAPHS, NODES, DIM = 128, 64, 256
P = 128
PER_TILE = P // NODES
TILES = 4
GROUP = TILES * P
PAIRS = GRAPHS * NODES // (2 * GROUP)
CH = DIM // P
HEADS, HD = 8, 32
BANK = 512
EPS = 1e-5
SLOPE = 0.2
MASKED = -3.0e38
SLOTS = (0, 1)


class Signal:

    def __init__(self, sem, per, primed=0):
        self.sem, self.per, self.primed = sem, per, primed

    def at(self, it, n):
        return it * self.per + (n + self.primed)


class Chain:

    def __init__(self, sem, per):
        self.sem, self.per, self.n = sem, per, 0

    def start(self, eng, it):
        assert self.n in (0, self.per), (self.sem, self.n)
        self.eng, self.it, self.n = eng, it, 0

    def link(self, ins):
        self.n += 1
        ins.then_inc(self.sem, 1)
        self.eng.wait_ge(self.sem, self.it * self.per + self.n)


def staged(eng, front, mid, tail):
    front(0)
    with eng.Fori(0, PAIRS - 1) as it:
        mid(it)
        front(it + 1)
        tail(it)
    mid(PAIRS - 1)
    tail(PAIRS - 1)


class Program:
    def __init__(self, nc, a, out, stack):
        self.nc, self.a, self.out, self.stack = nc, a, out, stack
        self.taken = []
        self.ps = [stack.enter_context(nc.psum_tensor(f"banks{s}", [P, TILES, BANK], F32)) for s in SLOTS]
        sb = self.sb
        self.ident = sb("ident", [P, P])
        self.ident_bf = sb("ident_bf", [P, P], BF16)
        self.adj_t = sb("adj_t", [P, P])
        self.adj2 = sb("adj2", [P, NODES])
        self.mask_bias = sb("mask_bias", [P, NODES], BF16)
        self.nan_rows = sb("nan_rows", [P, 1])
        self.same_graph = sb("same_graph", [P, P])
        self.ident2 = sb("ident2", [P, NODES])
        self.eps = sb("eps", [P, TILES])
        self.minus_half = sb("minus_half", [P, TILES])
        self.minus_one = sb("minus_one", [P, 1])

    def sb(self, name, shape, dt=F32, stack=None):
        return (stack or self.stack).enter_context(self.nc.sbuf_tensor(name, shape, dt))

    def sem(self, name):
        self.taken.append(self.nc.alloc_semaphore(name=name))
        return self.taken[-1]

    def clear_semaphores(self):
        self.nc.all_engine_barrier()
        self.nc.clear_and_free_semaphores(self.taken)
        self.nc.all_engine_barrier()
        self.taken = []

    def signals(self, name, per, primed=0):
        return [Signal(self.sem(f"{name}{s}"), per, primed) for s in SLOTS]

    def view(self, x):
        return x.rearrange("(i s t p) d -> i s p t d", s=2, t=TILES, p=P)


def matmul3(nc, out, w, x, first, last):
    nc.tensor.matmul(out, w[0], x[0], start=first, stop=False, skip_group_check=True)
    nc.tensor.matmul(out, w[0], x[1], start=False, stop=False, skip_group_check=True)
    return nc.tensor.matmul(out, w[1], x[0], start=False, stop=last, skip_group_check=True)


def constants(p):
    nc = p.nc
    with ExitStack() as own:
        adj_blk = p.sb("adj_blk", [P, P], stack=own)
        hits = p.sb("hits", [P, NODES], stack=own)
        count = p.sb("count", [P, 1], stack=own)
        zeroed, made, loaded, turned, chain = (p.sem(n) for n in (
            "c_zeroed", "c_made", "c_loaded", "c_turned", "c_chain"))
        with nc.Block() as block:

            @block.gpsimd
            def _(pool):
                nc.gpsimd.memset(p.ident[:, :], 0.0).then_inc(zeroed, 1)
                nc.gpsimd.memset(adj_blk[:, :], 0.0).then_inc(zeroed, 1)
                nc.gpsimd.memset(p.same_graph[:, :], 0.0).then_inc(zeroed, 1)
                nc.gpsimd.memset(p.eps[:, :], EPS)
                nc.gpsimd.memset(p.minus_half[:, :], -0.5)
                nc.gpsimd.memset(p.minus_one[:, :], -1.0)
                pool.wait_ge(zeroed, 3)
                nc.gpsimd.affine_select(out=p.ident[:, :], in_=p.ident[:, :], compare_op=ALU.not_equal, fill=1.0,
                                        base=0, pattern=[[-1, P]], channel_multiplier=1).then_inc(made, 1)

            @block.sync
            def _(sp):
                sp.wait_ge(zeroed, 3)
                for b in range(PER_TILE):
                    q = slice(b * NODES, (b + 1) * NODES)
                    sp.dma_start(adj_blk[q, q], p.a["adj"]).then_inc(loaded, 16)
                    sp.dma_start(p.adj2[q, :], p.a["adj"]).then_inc(loaded, 16)
                sp.wait_ge(loaded, 64)

            @block.tensor
            def _(pe):
                pe.wait_ge(made, 1)
                pe.wait_ge(loaded, 64)
                nc.tensor.transpose(p.ps[0][:, 0, 0:P], adj_blk[:, :], p.ident[:, :]).then_inc(turned, 1)

            @block.vector
            def _(dve):
                links = Chain(chain, 7)
                links.start(dve, 0)
                dve.wait_ge(loaded, 64)
                dve.wait_ge(made, 1)
                for b in range(PER_TILE):
                    q = slice(b * NODES, (b + 1) * NODES)
                    nc.vector.memset(p.same_graph[q, q], 1.0)
                nc.vector.tensor_copy(p.ident_bf[:, :], p.ident[:, :])
                nc.vector.tensor_tensor(p.ident2[:, :], p.ident[:, 0:NODES], p.ident[:, NODES:P], ALU.add)
                nc.vector.tensor_scalar(p.mask_bias[:, :], p.adj2[:, :], 0.0, MASKED, ALU.is_equal, ALU.mult)
                links.link(nc.vector.tensor_scalar(hits[:, :], p.adj2[:, :], 0.0, None, ALU.not_equal))
                links.link(nc.vector.reduce_sum(count[:, :], hits[:, :], AX.X))
                links.link(nc.vector.tensor_scalar(count[:, :], count[:, :], 1.0, None, ALU.min))
                links.link(nc.vector.reciprocal(count[:, :], count[:, :]))
                links.link(nc.vector.tensor_scalar(p.nan_rows[:, :], count[:, :], 0.0, None, ALU.mult))
                dve.wait_ge(turned, 1)
                links.link(nc.vector.tensor_copy(p.adj_t[:, :], p.ps[0][:, 0, 0:P]))
                links.link(nc.vector.tensor_copy(hits[:, 0:1], p.nan_rows[:, :]))


class Norm:

    LINKS = 2

    def __init__(self, p, name, stack):
        self.p = p
        self.carrier = p.sb(f"{name}_carrier", [P, 1], stack=stack)
        self.stats = [p.sb(f"{name}_stats{s}", [P, TILES, 6], stack=stack) for s in SLOTS]
        self.mv = [p.sb(f"{name}_mv{s}", [P, TILES, 2], stack=stack) for s in SLOTS]
        self.rstd = [p.sb(f"{name}_rstd{s}", [P, TILES], stack=stack) for s in SLOTS]
        self.var_ready = p.signals(f"{name}_var_ready", 1)
        self.eps_added = p.signals(f"{name}_eps_added", 1)
        self.rstd_ready = p.signals(f"{name}_rstd_ready", 1)

    def statistics(self, links, s, z):
        nc = self.p.nc
        for t in range(TILES):
            ins = nc.vector.bn_stats(self.stats[s][:, t, :], z[:, t, :])
        links.link(ins)
        nc.vector.memset(self.carrier[:, :], 0.0)
        for t in range(TILES):
            ins = nc.vector.bn_aggr(self.mv[s][:, t, :], self.stats[s][:, t, :])
        ins.then_inc(self.var_ready[s].sem, 1)

    def root(self, pool, it, s):
        nc = self.p.nc
        pool.wait_ge(self.var_ready[s].sem, self.var_ready[s].at(it, 1))
        nc.gpsimd.tensor_tensor(self.rstd[s][:, :], self.mv[s][:, :, 1], self.p.eps[:, :],
                                ALU.add).then_inc(self.eps_added[s].sem, 1)
        pool.wait_ge(self.eps_added[s].sem, self.eps_added[s].at(it, 1))
        nc.gpsimd.tensor_tensor(self.rstd[s][:, :], self.rstd[s][:, :], self.p.minus_half[:, :],
                                ALU.pow).then_inc(self.rstd_ready[s].sem, 1)

    def apply(self, dve, it, s, z, y):
        nc = self.p.nc
        dve.wait_ge(self.rstd_ready[s].sem, self.rstd_ready[s].at(it, 1))
        for t in range(TILES):
            ins = nc.vector.tensor_scalar(y[:, t, :], z[:, t, :], self.mv[s][:, t, 0:1], self.rstd[s][:, t:t + 1],
                                          ALU.subtract, ALU.mult)
        return ins


def stream(p, block, src, dst, x_tok, y_tok, loaded, x_free, y_ready, stored):

    @block.sync
    def _(sp):
        for s in SLOTS:
            sp.sem_inc(stored[s].sem, stored[s].primed)

        def load(it):
            for s in SLOTS:
                sp.wait_ge(x_free[s].sem, x_free[s].at(it, 0))
                sp.dma_start(x_tok[s][:, :, :], src[it][s]).then_inc(loaded[s].sem, 16)

        def store(it):
            for s in SLOTS:
                sp.wait_ge(y_ready[s].sem, y_ready[s].at(it, 1))
                sp.dma_start(dst[it][s], y_tok[s][:, :, :]).then_inc(stored[s].sem, 16)

        load(0)
        with sp.Fori(0, PAIRS - 1) as it:
            load(it + 1)
            store(it)
        store(PAIRS - 1)
        for s in SLOTS:
            sp.wait_ge(stored[s].sem, stored[s].at(PAIRS, 0))


def layer0(p, src, dst):
    nc = p.nc
    with ExitStack() as own:
        WX = DIM + 2
        w = p.sb("l0_w", [P, CH, WX], stack=own)
        a_row = p.sb("l0_a", [P, 2, DIM], stack=own)
        wa = p.sb("l0_wa", [P, CH, DIM], stack=own)
        beta = p.sb("l0_beta", [P, 1], stack=own)
        w_parts = [p.sb(f"l0_w{n}", [P, CH, WX], F32R, stack=own) for n in ("hi", "lo")]
        two = lambda name, shape, dt=F32: [p.sb(f"l0_{name}{s}", shape, dt, stack=own) for s in SLOTS]
        x_tok = two("x", [P, TILES, DIM])
        y_tok = two("y", [P, TILES, DIM])
        x_hi = two("xhi", [P, CH, GROUP], F32R)
        x_lo = two("xlo", [P, CH, GROUP], F32R)
        h = two("h", [P, TILES, WX])
        s2_spread = two("s2", [P, TILES, P])
        e = two("e", [P, TILES, NODES])
        small = two("small", [P, 3, TILES])
        att = two("att", [P, TILES, P])
        att_t = two("att_t", [P, TILES, P])
        v = two("v", [P, TILES, DIM])
        neg = two("neg", [P, TILES, DIM])
        res = two("res", [P, TILES, DIM])
        norm = Norm(p, "l0", own)

        w_loaded, w_chain, w_hi, w_ready, att_zeroed = (p.sem(f"l0_{n}") for n in (
            "w_loaded", "w_chain", "w_hi", "w_ready", "att_zeroed"))
        loaded = p.signals("l0_loaded", 16)
        x_free = p.signals("l0_x_free", 1, 1)
        stored = p.signals("l0_stored", 16, 16)
        y_ready = p.signals("l0_y_ready", 1)
        turned = p.signals("l0_turned", CH)
        hi_ready = p.signals("l0_hi_ready", CH)
        lo_ready = p.signals("l0_lo_ready", CH)
        h_done = p.signals("l0_h_done", TILES, 1)
        h_ready = p.signals("l0_h_ready", TILES)
        spread = p.signals("l0_spread", 1)
        s2_done = p.signals("l0_s2_done", 1)
        shifted = p.signals("l0_shifted", 1)
        exp_done = p.signals("l0_exp_done", 1)
        att_ready = p.signals("l0_att_ready", 1)
        att_turned = p.signals("l0_att_turned", 1)
        att_t_ready = p.signals("l0_att_t_ready", 1)
        hp_done = p.signals("l0_hp_done", 2)
        v_ready = p.signals("l0_v_ready", 2, 1)
        relu_done = p.signals("l0_relu_done", 1)
        elu_ready = p.signals("l0_elu_ready", 1)
        res_ready = p.signals("l0_res_ready", 1)
        z_ready = p.signals("l0_z_ready", 1, 1)
        mid_chain = Chain(p.sem("l0_mid_chain"), 2 * 6)
        tail_chain = Chain(p.sem("l0_tail_chain"), 2)

        with nc.Block() as block:
            stream(p, block, src, dst, x_tok, y_tok, loaded, x_free, y_ready, stored)

            @block.gpsimd
            def _(pool):
                pool.dma_start(w[:, :, 0:DIM], p.a["L0_gnn_W"].rearrange("(k p) f -> p k f", p=P)).then_inc(w_loaded, 16)
                pool.dma_start(a_row[:, :, :], p.a["L0_gnn_a"].rearrange("(j f) o -> o j f", j=2).to_broadcast(
                    [P, 2, DIM])).then_inc(w_loaded, 16)
                pool.dma_start(beta[:, :], p.a["L0_gnn_beta"].rearrange("(o a) -> o a", o=1).to_broadcast(
                    [P, 1])).then_inc(w_loaded, 16)
                for s in SLOTS:
                    nc.gpsimd.memset(att[s][:, :, :], 0.0).then_inc(att_zeroed, 1)
                    pool.sem_inc(x_free[s].sem, 1)

                def mid(it):
                    for s in SLOTS:
                        pool.wait_ge(h_ready[s].sem, h_ready[s].at(it, TILES))
                        nc.gpsimd.tensor_tensor(s2_spread[s][:, :, :],
                                                p.same_graph[:, :].unsqueeze(1).to_broadcast([P, TILES, P]),
                                                h[s][:, :, DIM + 1:DIM + 2].to_broadcast([P, TILES, P]),
                                                ALU.mult).then_inc(spread[s].sem, 1)
                    for s in SLOTS:
                        pool.wait_ge(z_ready[s].sem, z_ready[s].at(it, 0))
                        nc.gpsimd.tensor_tensor(res[s][:, :, :], x_tok[s][:, :, :],
                                                p.minus_one[:, :].unsqueeze(1).to_broadcast([P, TILES, DIM]),
                                                ALU.add).then_inc(x_free[s].sem, 1)

                def tail(it):
                    for s in SLOTS:
                        pool.wait_ge(x_free[s].sem, x_free[s].at(it, 1))
                        pool.wait_ge(elu_ready[s].sem, elu_ready[s].at(it, 1))
                        nc.gpsimd.tensor_tensor(res[s][:, :, :], res[s][:, :, :], neg[s][:, :, :],
                                                ALU.add).then_inc(res_ready[s].sem, 1)
                    for s in SLOTS:
                        norm.root(pool, it, s)

                staged(pool, lambda it: None, mid, tail)

            @block.tensor
            def _(pe):
                pe.wait_ge(w_ready, 1)
                pe.wait_ge(w_hi, 1)
                pe.wait_ge(att_zeroed, 2)

                def front(it):
                    for s in SLOTS:
                        pe.wait_ge(loaded[s].sem, loaded[s].at(it, 16))
                        for k in range(CH):
                            for t in range(TILES):
                                ins = nc.tensor.transpose(p.ps[s][:, k, t * P:(t + 1) * P],
                                                          x_tok[s][:, t, k * P:(k + 1) * P], p.ident[:, :])
                            ins.then_inc(turned[s].sem, 1)

                def mid(it):
                    for s in SLOTS:
                        pe.wait_ge(lo_ready[s].sem, lo_ready[s].at(it, CH))
                        pe.wait_ge(v_ready[s].sem, v_ready[s].at(it, 0))
                        for t in range(TILES):
                            for k in range(CH):
                                q = slice(t * P, (t + 1) * P)
                                ins = matmul3(nc, p.ps[s][:, t, 0:WX], (x_hi[s][:, k, q], x_lo[s][:, k, q]),
                                              (w_parts[0][:, k, :], w_parts[1][:, k, :]), k == 0, k == CH - 1)
                            ins.then_inc(h_done[s].sem, 1)
                    for s in SLOTS:
                        pe.wait_ge(spread[s].sem, spread[s].at(it, 1))
                        for t in range(TILES):
                            ins = nc.tensor.matmul(p.ps[s][:, 0, t * NODES:(t + 1) * NODES], s2_spread[s][:, t, :],
                                                   p.ident2[:, :], start=True, stop=True)
                        ins.then_inc(s2_done[s].sem, 1)
                    for s in SLOTS:
                        pe.wait_ge(att_ready[s].sem, att_ready[s].at(it, 1))
                        for t in range(TILES):
                            ins = nc.tensor.transpose(p.ps[s][:, 1, t * P:(t + 1) * P], att[s][:, t, :], p.ident[:, :])
                        ins.then_inc(att_turned[s].sem, 1)
                    for s in SLOTS:
                        pe.wait_ge(att_t_ready[s].sem, att_t_ready[s].at(it, 1))
                        for t in range(TILES):
                            ins = nc.tensor.matmul(p.ps[s][:, 2 + t // 2, (t % 2) * DIM:(t % 2 + 1) * DIM],
                                                   att_t[s][:, t, :], h[s][:, t, 0:DIM], start=True, stop=True)
                            if t % 2:
                                ins.then_inc(hp_done[s].sem, 1)

                for s in SLOTS:
                    pe.sem_inc(h_done[s].sem, 1)
                staged(pe, front, mid, lambda it: None)

            @block.scalar
            def _(act):
                act.wait_ge(w_chain, 4)
                nc.scalar.activation(w_parts[0][:, :, :], w[:, :, :], ACT.Copy).then_inc(w_hi, 1)

                def front(it):
                    for s in SLOTS:
                        act.wait_ge(h_done[s].sem, h_done[s].at(it, 0))
                        for k in range(CH):
                            act.wait_ge(turned[s].sem, turned[s].at(it, k + 1))
                            nc.scalar.activation(x_hi[s][:, k, :], p.ps[s][:, k, :], ACT.Copy).then_inc(hi_ready[s].sem, 1)

                def mid(it):
                    for s in SLOTS:
                        for t in range(TILES):
                            act.wait_ge(h_done[s].sem, h_done[s].at(it, t + 1))
                            nc.scalar.activation(h[s][:, t, :], p.ps[s][:, t, 0:WX], ACT.Copy).then_inc(h_ready[s].sem, 1)
                    for s in SLOTS:
                        act.wait_ge(shifted[s].sem, shifted[s].at(it, 1))
                        nc.scalar.activation(e[s][:, :, :], e[s][:, :, :], ACT.Exp).then_inc(exp_done[s].sem, 1)
                    for s in SLOTS:
                        act.wait_ge(att_turned[s].sem, att_turned[s].at(it, 1))
                        nc.scalar.activation(att_t[s][:, :, :], p.ps[s][:, 1, :], ACT.Copy).then_inc(att_t_ready[s].sem, 1)

                def tail(it):
                    for s in SLOTS:
                        act.wait_ge(v_ready[s].sem, v_ready[s].at(it, 2))
                        nc.scalar.activation(neg[s][:, :, :], v[s][:, :, :], ACT.Relu, scale=-1.0).then_inc(relu_done[s].sem, 1)
                        act.wait_ge(relu_done[s].sem, relu_done[s].at(it, 1))
                        nc.scalar.activation(neg[s][:, :, :], neg[s][:, :, :], ACT.Exp, scale=-1.0).then_inc(elu_ready[s].sem, 1)

                staged(act, front, mid, tail)

            @block.vector
            def _(dve):
                links = Chain(w_chain, 4)
                links.start(dve, 0)
                dve.wait_ge(w_loaded, 48)
                for j in range(2):
                    links.link(nc.vector.tensor_tensor(wa[:, :, :], w[:, :, 0:DIM],
                                                       a_row[:, j, :].unsqueeze(1).to_broadcast([P, CH, DIM]), ALU.mult))
                    links.link(nc.vector.tensor_reduce(w[:, :, DIM + j:DIM + j + 1], wa[:, :, :], AX.X, ALU.add))
                dve.wait_ge(w_hi, 1)
                nc.vector.tensor_tensor(w_parts[1][:, :, :], w[:, :, :], w_parts[0][:, :, :].bitcast(F32),
                                        ALU.subtract).then_inc(w_ready, 1)
                dve.wait_ge(att_zeroed, 2)
                for s in SLOTS:
                    dve.sem_inc(v_ready[s].sem, 1)
                    dve.sem_inc(z_ready[s].sem, 1)

                def front(it):
                    for s in SLOTS:
                        for k in range(CH):
                            dve.wait_ge(hi_ready[s].sem, hi_ready[s].at(it, k + 1))
                            nc.vector.tensor_tensor(x_lo[s][:, k, :], p.ps[s][:, k, :], x_hi[s][:, k, :].bitcast(F32),
                                                    ALU.subtract).then_inc(lo_ready[s].sem, 1)

                def mid(it):
                    mid_chain.start(dve, it)
                    link = mid_chain.link
                    for s in SLOTS:
                        mx, total, inv = (small[s][:, n, :] for n in range(3))
                        dve.wait_ge(s2_done[s].sem, s2_done[s].at(it, 1))
                        ps2 = p.ps[s][:, 0, 0:TILES * NODES].rearrange("p (t j) -> p t j", t=TILES)
                        link(nc.vector.tensor_tensor(e[s][:, :, :], ps2,
                                                     h[s][:, :, DIM:DIM + 1].to_broadcast([P, TILES, NODES]), ALU.add))
                        link(nc.vector.scalar_tensor_tensor(e[s][:, :, :], e[s][:, :, :], SLOPE, e[s][:, :, :],
                                                            ALU.mult, ALU.max))
                        link(nc.vector.tensor_tensor(e[s][:, :, :], e[s][:, :, :],
                                                     p.adj2[:, :].unsqueeze(1).to_broadcast([P, TILES, NODES]), ALU.mult))
                        link(nc.vector.tensor_reduce(mx, e[s][:, :, :], AX.X, ALU.max))
                        nc.vector.tensor_tensor(e[s][:, :, :], e[s][:, :, :], mx.unsqueeze(2).to_broadcast(
                            [P, TILES, NODES]), ALU.subtract).then_inc(shifted[s].sem, 1)
                    for s in SLOTS:
                        mx, total, inv = (small[s][:, n, :] for n in range(3))
                        dve.wait_ge(exp_done[s].sem, exp_done[s].at(it, 1))
                        link(nc.vector.tensor_reduce(total, e[s][:, :, :], AX.X, ALU.add))
                        link(nc.vector.reciprocal(inv, total))
                        for b in range(PER_TILE):
                            q = slice(b * NODES, (b + 1) * NODES)
                            ins = nc.vector.tensor_tensor(att[s][q, :, q], e[s][q, :, :], inv[q].unsqueeze(2).to_broadcast(
                                [NODES, TILES, NODES]), ALU.mult)
                        ins.then_inc(att_ready[s].sem, 1)
                    for s in SLOTS:
                        for b in range(2):
                            dve.wait_ge(hp_done[s].sem, hp_done[s].at(it, b + 1))
                            ps = p.ps[s][:, 2 + b, :].rearrange("p (t f) -> p t f", t=2)
                            nc.vector.scalar_tensor_tensor(v[s][:, 2 * b:2 * b + 2, :], h[s][:, 2 * b:2 * b + 2, 0:DIM],
                                                           beta[:, :], ps, ALU.mult, ALU.add).then_inc(v_ready[s].sem, 1)

                def tail(it):
                    tail_chain.start(dve, it)
                    for s in SLOTS:
                        dve.wait_ge(res_ready[s].sem, res_ready[s].at(it, 1))
                        ins = nc.vector.scalar_tensor_tensor(v[s][:, :, :], v[s][:, :, :], 0.0, res[s][:, :, :],
                                                             ALU.max, ALU.add)
                        ins.then_inc(z_ready[s].sem, 1)
                        dve.wait_ge(z_ready[s].sem, z_ready[s].at(it, 1))
                        norm.statistics(tail_chain, s, v[s])
                    for s in SLOTS:
                        dve.wait_ge(stored[s].sem, stored[s].at(it, 0))
                        norm.apply(dve, it, s, v[s], y_tok[s]).then_inc(y_ready[s].sem, 1)

                staged(dve, front, mid, tail)


def layer1(p, src, dst):
    nc = p.nc
    with ExitStack() as own:
        w = p.sb("l1_w", [P, CH, DIM], stack=own)
        bias = p.sb("l1_bias", [P, DIM], stack=own)
        w_parts = [p.sb(f"l1_w{n}", [P, CH, DIM], F32R, stack=own) for n in ("hi", "lo")]
        two = lambda name, shape, dt=F32: [p.sb(f"l1_{name}{s}", shape, dt, stack=own) for s in SLOTS]
        x_tok = two("x", [P, TILES, DIM])
        y_tok = two("y", [P, TILES, DIM])
        a_hi = two("ahi", [P, CH, GROUP], F32R)
        a_lo = two("alo", [P, CH, GROUP], F32R)
        res = two("res", [P, TILES, DIM])
        z = two("z", [P, TILES, DIM])
        norm = Norm(p, "l1", own)

        w_loaded, w_hi, w_ready = (p.sem(f"l1_{n}") for n in ("w_loaded", "w_hi", "w_ready"))
        loaded = p.signals("l1_loaded", 16)
        x_free = p.signals("l1_x_free", 1, 1)
        stored = p.signals("l1_stored", 16, 16)
        y_ready = p.signals("l1_y_ready", 1, 1)
        adj_done = p.signals("l1_adj_done", CH)
        hi_ready = p.signals("l1_hi_ready", CH)
        lo_ready = p.signals("l1_lo_ready", CH)
        out_done = p.signals("l1_out_done", 2, 1)
        z_ready = p.signals("l1_z_ready", 2, 1)
        tail_chain = Chain(p.sem("l1_tail_chain"), 2)

        with nc.Block() as block:
            stream(p, block, src, dst, x_tok, y_tok, loaded, x_free, y_ready, stored)

            @block.gpsimd
            def _(pool):
                pool.dma_start(w[:, :, :], p.a["L1_gnn_weight"].rearrange("(k p) f -> p k f", p=P)).then_inc(w_loaded, 16)
                pool.dma_start(bias[:, :], p.a["L1_gnn_bias"].rearrange("(o f) -> o f", o=1).to_broadcast(
                    [P, DIM])).then_inc(w_loaded, 16)
                for s in SLOTS:
                    pool.sem_inc(x_free[s].sem, 1)
                pool.wait_ge(w_loaded, 32)

                def mid(it):
                    for s in SLOTS:
                        pool.wait_ge(adj_done[s].sem, adj_done[s].at(it, CH))
                        pool.wait_ge(z_ready[s].sem, z_ready[s].at(it, 0))
                        nc.gpsimd.tensor_tensor(res[s][:, :, :], x_tok[s][:, :, :],
                                                bias[:, :].unsqueeze(1).to_broadcast([P, TILES, DIM]),
                                                ALU.add).then_inc(x_free[s].sem, 1)

                def tail(it):
                    for s in SLOTS:
                        norm.root(pool, it, s)

                staged(pool, lambda it: None, mid, tail)

            @block.tensor
            def _(pe):
                for s in SLOTS:
                    pe.sem_inc(out_done[s].sem, 1)
                pe.wait_ge(w_ready, 1)
                pe.wait_ge(w_hi, 1)

                def front(it):
                    for s in SLOTS:
                        pe.wait_ge(loaded[s].sem, loaded[s].at(it, 16))
                        for k in range(CH):
                            for t in range(TILES):
                                ins = nc.tensor.matmul(p.ps[s][:, k, t * P:(t + 1) * P],
                                                       x_tok[s][:, t, k * P:(k + 1) * P], p.adj_t[:, :],
                                                       start=True, stop=True)
                            ins.then_inc(adj_done[s].sem, 1)

                def mid(it):
                    for s in SLOTS:
                        pe.wait_ge(lo_ready[s].sem, lo_ready[s].at(it, CH))
                        pe.wait_ge(z_ready[s].sem, z_ready[s].at(it, 0))
                        for t in range(TILES):
                            for k in range(CH):
                                q = slice(t * P, (t + 1) * P)
                                ins = matmul3(nc, p.ps[s][:, 2 + t // 2, (t % 2) * DIM:(t % 2 + 1) * DIM],
                                              (a_hi[s][:, k, q], a_lo[s][:, k, q]),
                                              (w_parts[0][:, k, :], w_parts[1][:, k, :]), k == 0, k == CH - 1)
                            if t % 2:
                                ins.then_inc(out_done[s].sem, 1)

                staged(pe, front, mid, lambda it: None)

            @block.scalar
            def _(act):
                act.wait_ge(w_loaded, 32)
                nc.scalar.activation(w_parts[0][:, :, :], w[:, :, :], ACT.Copy).then_inc(w_hi, 1)

                def front(it):
                    for s in SLOTS:
                        act.wait_ge(out_done[s].sem, out_done[s].at(it, 0))
                        for k in range(CH):
                            act.wait_ge(adj_done[s].sem, adj_done[s].at(it, k + 1))
                            nc.scalar.activation(a_hi[s][:, k, :], p.ps[s][:, k, :], ACT.Copy).then_inc(hi_ready[s].sem, 1)

                staged(act, front, lambda it: None, lambda it: None)

            @block.vector
            def _(dve):
                dve.wait_ge(w_loaded, 32)
                dve.wait_ge(w_hi, 1)
                nc.vector.tensor_tensor(w_parts[1][:, :, :], w[:, :, :], w_parts[0][:, :, :].bitcast(F32),
                                        ALU.subtract).then_inc(w_ready, 1)
                for s in SLOTS:
                    dve.sem_inc(z_ready[s].sem, 1)
                    dve.sem_inc(y_ready[s].sem, 1)

                def front(it):
                    for s in SLOTS:
                        for k in range(CH):
                            dve.wait_ge(hi_ready[s].sem, hi_ready[s].at(it, k + 1))
                            nc.vector.tensor_tensor(a_lo[s][:, k, :], p.ps[s][:, k, :], a_hi[s][:, k, :].bitcast(F32),
                                                    ALU.subtract).then_inc(lo_ready[s].sem, 1)

                def mid(it):
                    for s in SLOTS:
                        dve.wait_ge(x_free[s].sem, x_free[s].at(it, 1))
                        dve.wait_ge(y_ready[s].sem, y_ready[s].at(it, 0))
                        for b in range(2):
                            dve.wait_ge(out_done[s].sem, out_done[s].at(it, b + 1))
                            nc.vector.tensor_tensor(z[s][:, 2 * b:2 * b + 2, :],
                                                    p.ps[s][:, 2 + b, :].rearrange("p (t f) -> p t f", t=2),
                                                    res[s][:, 2 * b:2 * b + 2, :], ALU.add).then_inc(z_ready[s].sem, 1)

                def tail(it):
                    tail_chain.start(dve, it)
                    for s in SLOTS:
                        dve.wait_ge(z_ready[s].sem, z_ready[s].at(it, 2))
                        norm.statistics(tail_chain, s, z[s])
                    for s in SLOTS:
                        dve.wait_ge(stored[s].sem, stored[s].at(it, 0))
                        norm.apply(dve, it, s, z[s], y_tok[s]).then_inc(y_ready[s].sem, 1)

                staged(dve, front, mid, tail)


def layer2(p, src, dst):
    nc = p.nc
    with ExitStack() as own:
        ROWS = P // HD
        HP = HEADS // 2
        VW = 2 * HD + 2
        QK_BANK = (2, 3, 0, 1)
        w = p.sb("l2_w", [P, CH, 3 * DIM], stack=own)
        wp = p.sb("l2_wp", [P, CH, DIM], stack=own)
        w_parts = [p.sb(f"l2_w{n}", [P, CH, 3 * DIM], F32R, stack=own) for n in ("hi", "lo")]
        wp_parts = [p.sb(f"l2_wp{n}", [P, CH, DIM], F32R, stack=own) for n in ("hi", "lo")]
        rows = {n: p.sb(f"l2_{n}", [P, DIM], stack=own) for n in ("b_proj", "ln_gamma", "ln_beta")}
        two = lambda name, shape, dt=F32: [p.sb(f"l2_{name}{s}", shape, dt, stack=own) for s in SLOTS]
        x_tok = two("x", [P, TILES, DIM])
        y_tok = two("y", [P, TILES, DIM])
        x_parts = [(p.sb(f"l2_xhi{s}", [P, CH, GROUP], F32R, stack=own), p.sb(f"l2_xlo{s}", [P, CH, GROUP], F32R, stack=own))
                   for s in SLOTS]
        o_parts = [(p.sb(f"l2_ohi{s}", [P, CH, GROUP], F32R, stack=own), p.sb(f"l2_olo{s}", [P, CH, GROUP], F32R, stack=own))
                   for s in SLOTS]
        q_t = two("q", [P, CH, GROUP])
        k_t = two("k", [P, CH, GROUP])
        v_pair = two("vpair", [P, PER_TILE, TILES, HP, VW])
        v_stage = two("vstage", [P, TILES, HP, HD])
        prob = two("prob", [P, TILES, HEADS, NODES])
        prob_t = two("probt", [P, TILES, BANK])
        mx = two("mx", [P, ROWS, TILES * CH])
        inv = two("inv", [P, TILES, HP, 2])
        o_tok = two("otok", [P, TILES, DIM])
        t_ln = two("tln", [P, TILES, DIM])
        res = two("res", [P, TILES, DIM])
        inner, outer = Norm(p, "l2i", own), Norm(p, "l2o", own)

        w_loaded, w_hi, w_ready, blank, ones = (p.sem(f"l2_{n}") for n in ("w_loaded", "w_hi", "w_ready", "blank", "ones"))
        loaded = p.signals("l2_loaded", 16)
        x_free = p.signals("l2_x_free", 1, 1)
        stored = p.signals("l2_stored", 16, 16)
        y_ready = p.signals("l2_y_ready", 1, 1)
        turned = p.signals("l2_turned", CH)
        hi_ready = p.signals("l2_hi_ready", CH)
        lo_ready = p.signals("l2_lo_ready", CH)
        qk_done = p.signals("l2_qk_done", 2 * CH)
        qk_ready = p.signals("l2_qk_ready", 2 * CH)
        v_done = p.signals("l2_v_done", 1)
        v_staged = p.signals("l2_v_staged", 1)
        v_swapped = [p.signals(f"l2_v_swapped{b}_", 16) for b in range(PER_TILE)]
        scored = p.signals("l2_scored", ROWS)
        shifted = p.signals("l2_shifted", 1)
        exp_done = p.signals("l2_exp_done", TILES)
        prob_turned = p.signals("l2_prob_turned", TILES)
        prob_t_ready = p.signals("l2_prob_t_ready", TILES)
        pv_done = p.signals("l2_pv_done", TILES, 1)
        o_ready = p.signals("l2_o_ready", 1, 1)
        o_turned = p.signals("l2_o_turned", CH)
        o_hi_ready = p.signals("l2_o_hi_ready", CH)
        o_lo_ready = p.signals("l2_o_lo_ready", CH)
        proj_done = p.signals("l2_proj_done", 2, 1)
        proj_ready = p.signals("l2_proj_ready", 2, 1)
        sum_ready = p.signals("l2_sum_ready", 1)
        z_ready = p.signals("l2_z_ready", 1, 1)
        mid_chain = Chain(p.sem("l2_mid_chain"), 2 * 4)
        tail_chain = Chain(p.sem("l2_tail_chain"), 2 * 4)

        def wait(eng, signal, s, it, n):
            eng.wait_ge(signal[s].sem, signal[s].at(it, n))

        def two_tiles(s, bank):
            return p.ps[s][:, bank, :].rearrange("p (t f) -> p t f", t=2)

        def values(s, b, parity):
            q = slice(b * NODES, (b + 1) * NODES)
            v = p.ps[s][q, 2:4, :].rearrange("p b (t g e d) -> p (b t) g e d", t=2, e=2, d=HD)
            return v[:, :, :, parity, :]

        with nc.Block() as block:

            @block.sync
            def _(sp):
                for s in SLOTS:
                    sp.sem_inc(stored[s].sem, stored[s].primed)

                def load(it):
                    for s in SLOTS:
                        wait(sp, x_free, s, it, 0)
                        sp.dma_start(x_tok[s][:, :, :], src[it][s]).then_inc(loaded[s].sem, 16)

                def swap(it):
                    for s in SLOTS:
                        wait(sp, v_staged, s, it, 1)
                        for b in range(PER_TILE):
                            here = slice(b * NODES, (b + 1) * NODES)
                            there = slice((1 - b) * NODES, (2 - b) * NODES)
                            sp.dma_start(v_pair[s][there, b, :, :, (1 - b) * HD:(2 - b) * HD],
                                         v_stage[s][here, :, :, :]).then_inc(v_swapped[b][s].sem, 16)

                def store(it):
                    for s in SLOTS:
                        wait(sp, y_ready, s, it, 1)
                        sp.dma_start(dst[it][s], y_tok[s][:, :, :]).then_inc(stored[s].sem, 16)

                load(0)
                with sp.Fori(0, PAIRS - 1) as it:
                    swap(it)
                    load(it + 1)
                    store(it)
                swap(PAIRS - 1)
                store(PAIRS - 1)
                for s in SLOTS:
                    wait(sp, stored, s, PAIRS, 0)

            @block.gpsimd
            def _(pool):
                pool.dma_start(w[:, :, :], p.a["L2_gnn_w_qkv"].rearrange("(k p) f -> p k f", p=P)).then_inc(w_loaded, 16)
                pool.dma_start(wp[:, :, :], p.a["L2_gnn_w_proj"].rearrange("(k p) f -> p k f", p=P)).then_inc(w_loaded, 16)
                for n in rows:
                    pool.dma_start(rows[n][:, :], p.a[f"L2_gnn_{n}"].rearrange("(o f) -> o f", o=1).to_broadcast(
                        [P, DIM])).then_inc(w_loaded, 16)
                for s in SLOTS:
                    nc.gpsimd.memset(v_pair[s][:, :, :, :, :], 0.0).then_inc(blank, 1)
                    pool.sem_inc(x_free[s].sem, 1)
                pool.wait_ge(w_loaded, 80)

                def over_tiles(row):
                    return row[:, :].unsqueeze(1).to_broadcast([P, TILES, DIM])

                def mid(it):
                    for s in SLOTS:
                        wait(pool, turned, s, it, CH)
                        wait(pool, z_ready, s, it, 0)
                        nc.gpsimd.tensor_tensor(res[s][:, :, :], x_tok[s][:, :, :], over_tiles(rows["ln_beta"]),
                                                ALU.add).then_inc(x_free[s].sem, 1)

                def tail(it):
                    for s in SLOTS:
                        inner.root(pool, it, s)
                    for s in SLOTS:
                        wait(pool, x_free, s, it, 1)
                        nc.gpsimd.tensor_tensor(res[s][:, :, :], res[s][:, :, :], o_tok[s][:, :, :],
                                                ALU.add).then_inc(sum_ready[s].sem, 1)
                    for s in SLOTS:
                        outer.root(pool, it, s)

                staged(pool, lambda it: None, mid, tail)

            @block.tensor
            def _(pe):
                pe.wait_ge(w_ready, 2)
                pe.wait_ge(w_hi, 2)
                pe.wait_ge(ones, 4)
                for s in SLOTS:
                    pe.sem_inc(pv_done[s].sem, 1)
                    pe.sem_inc(proj_done[s].sem, 1)

                def turn(s, rows_, bank, done):
                    for k in range(CH):
                        for t in range(TILES):
                            ins = nc.tensor.transpose(p.ps[s][:, bank + k, t * P:(t + 1) * P],
                                                      rows_[:, t, k * P:(k + 1) * P], p.ident[:, :])
                        ins.then_inc(done[s].sem, 1)

                def rows_by_weights(s, t, bank, of, weights, f0):
                    q = slice(t * P, (t + 1) * P)
                    for k in range(CH):
                        ins = matmul3(nc, p.ps[s][:, bank + t // 2, (t % 2) * DIM:(t % 2 + 1) * DIM],
                                      (of[0][:, k, q], of[1][:, k, q]),
                                      (weights[0][:, k, f0:f0 + DIM], weights[1][:, k, f0:f0 + DIM]),
                                      k == 0, k == CH - 1)
                    return ins

                def front(it):
                    for s in SLOTS:
                        wait(pe, loaded, s, it, 16)
                        wait(pe, o_ready, s, it, 0)
                        turn(s, x_tok[s], 2, turned)

                def mid(it):
                    for s in SLOTS:
                        wait(pe, lo_ready, s, it, CH)
                        for m in range(2 * CH):
                            if m == CH:
                                wait(pe, proj_ready, s, it, 0)
                            for k in range(CH):
                                q = slice(m * P, (m + 1) * P)
                                ins = matmul3(nc, p.ps[s][:, QK_BANK[m], :], (w_parts[0][:, k, q], w_parts[1][:, k, q]),
                                              (x_parts[s][0][:, k, :], x_parts[s][1][:, k, :]), k == 0, k == CH - 1)
                            ins.then_inc(qk_done[s].sem, 1)
                    for s in SLOTS:
                        wait(pe, qk_ready, s, it, CH)
                        for t in range(TILES):
                            ins = rows_by_weights(s, t, 2, x_parts[s], w_parts, 2 * DIM)
                        ins.then_inc(v_done[s].sem, 1)
                    for s in SLOTS:
                        wait(pe, qk_ready, s, it, 2 * CH)
                        wait(pe, v_staged, s, it, 1)
                        for r in range(ROWS):
                            nc.tensor.matmul(p.ps[s][:, r, :], p.ident_bf[:, :],
                                             p.mask_bias[:, :].unsqueeze(1).to_broadcast([P, TILES * CH, NODES]),
                                             start=True, stop=False, skip_group_check=True)
                        for t in range(TILES):
                            for c in range(CH):
                                for b in range(PER_TILE):
                                    for r in range(ROWS):
                                        q = slice(t * P + b * NODES, t * P + (b + 1) * NODES)
                                        col = (t * CH + c) * NODES
                                        ins = nc.tensor.matmul(
                                            p.ps[s][b * NODES:(b + 1) * NODES, r, col:col + NODES],
                                            q_t[s][r * HD:(r + 1) * HD, c, q], k_t[s][r * HD:(r + 1) * HD, c, q],
                                            start=False, stop=True, skip_group_check=True)
                                        if (t, c, b) == (TILES - 1, CH - 1, PER_TILE - 1):
                                            ins.then_inc(scored[s].sem, 1)
                    for s in SLOTS:
                        for t in range(TILES):
                            wait(pe, exp_done, s, it, t + 1)
                            for g in range(HP):
                                ins = nc.tensor.transpose(p.ps[s][:, t, g * P:(g + 1) * P],
                                                          prob[s][:, t, 2 * g:2 * g + 2, :].rearrange("p h j -> p (h j)"),
                                                          p.ident[:, :])
                            ins.then_inc(prob_turned[s].sem, 1)
                        for b in range(PER_TILE):
                            wait(pe, v_swapped[b], s, it, 16)
                        for t in range(TILES):
                            wait(pe, prob_t_ready, s, it, t + 1)
                            for g in range(HP):
                                for b in range(PER_TILE):
                                    at = g * P + b * NODES
                                    ins = nc.tensor.matmul(p.ps[s][b * NODES:(b + 1) * NODES, t, g * VW:(g + 1) * VW],
                                                           prob_t[s][:, t, at:at + NODES], v_pair[s][:, b, t, g, :],
                                                           start=True, stop=True)
                            ins.then_inc(pv_done[s].sem, 1)
                    wait(pe, o_ready, 0, it, 1)
                    turn(0, o_tok[0], 0, o_turned)

                def tail(it):
                    wait(pe, o_ready, 1, it, 1)
                    turn(1, o_tok[1], 0, o_turned)
                    for s in SLOTS:
                        wait(pe, o_lo_ready, s, it, CH)
                        for t in range(TILES):
                            ins = rows_by_weights(s, t, 0, o_parts[s], wp_parts, 0)
                            if t % 2:
                                ins.then_inc(proj_done[s].sem, 1)

                for s in SLOTS:
                    pe.sem_inc(o_ready[s].sem, 1)
                staged(pe, front, mid, tail)

            @block.scalar
            def _(act):
                act.wait_ge(w_loaded, 80)
                nc.scalar.activation(w_parts[0][:, :, :], w[:, :, :], ACT.Copy).then_inc(w_hi, 1)
                nc.scalar.activation(wp_parts[0][:, :, :], wp[:, :, :], ACT.Copy).then_inc(w_hi, 1)
                act.wait_ge(blank, 2)

                def high(s, it, bank, done, parts, ready):
                    for k in range(CH):
                        wait(act, done, s, it, k + 1)
                        nc.scalar.activation(parts[s][0][:, k, :], p.ps[s][:, bank + k, :], ACT.Copy).then_inc(ready[s].sem, 1)

                def high_o(s, it):
                    wait(act, proj_done, s, it, 0)
                    high(s, it, 0, o_turned, o_parts, o_hi_ready)

                def front(it):
                    for s in SLOTS:
                        high(s, it, 2, turned, x_parts, hi_ready)

                def mid(it):
                    for s in SLOTS:
                        for m in range(2 * CH):
                            wait(act, qk_done, s, it, m + 1)
                            bank = p.ps[s][:, QK_BANK[m], :]
                            if m < CH:
                                ins = nc.scalar.activation(q_t[s][:, m, :], bank, ACT.Copy, scale=float(HD) ** -0.5)
                            else:
                                ins = nc.scalar.activation(k_t[s][:, m - CH, :], bank, ACT.Copy)
                            ins.then_inc(qk_ready[s].sem, 1)
                    for s in SLOTS:
                        wait(act, v_done, s, it, 1)
                        wait(act, pv_done, s, it, 0)
                        for b in range(PER_TILE):
                            q = slice(b * NODES, (b + 1) * NODES)
                            nc.scalar.activation(v_pair[s][q, b, :, :, b * HD:(b + 1) * HD], values(s, b, b), ACT.Copy)
                            ins = nc.scalar.activation(v_stage[s][q, :, :, :], values(s, b, 1 - b), ACT.Copy)
                        ins.then_inc(v_staged[s].sem, 1)
                    for s in SLOTS:
                        wait(act, shifted, s, it, 1)
                        for t in range(TILES):
                            nc.scalar.activation(prob[s][:, t, :, :], prob[s][:, t, :, :], ACT.Exp).then_inc(exp_done[s].sem, 1)
                        for t in range(TILES):
                            wait(act, prob_turned, s, it, t + 1)
                            nc.scalar.activation(prob_t[s][:, t, :], p.ps[s][:, t, :], ACT.Copy).then_inc(prob_t_ready[s].sem, 1)
                    high_o(0, it)

                staged(act, front, mid, lambda it: high_o(1, it))

            @block.vector
            def _(dve):
                dve.wait_ge(w_loaded, 80)
                dve.wait_ge(w_hi, 2)
                nc.vector.tensor_tensor(w_parts[1][:, :, :], w[:, :, :], w_parts[0][:, :, :].bitcast(F32),
                                        ALU.subtract).then_inc(w_ready, 1)
                nc.vector.tensor_tensor(wp_parts[1][:, :, :], wp[:, :, :], wp_parts[0][:, :, :].bitcast(F32),
                                        ALU.subtract).then_inc(w_ready, 1)
                dve.wait_ge(blank, 2)
                for s in SLOTS:
                    for e in range(2):
                        q = slice(e * NODES, (e + 1) * NODES)
                        nc.vector.memset(v_pair[s][q, :, :, :, 2 * HD + e], 1.0).then_inc(ones, 1)
                    for signal in (y_ready, proj_ready, z_ready):
                        dve.sem_inc(signal[s].sem, 1)

                def lower(s, it, bank, parts, hi, lo):
                    for k in range(CH):
                        wait(dve, hi, s, it, k + 1)
                        nc.vector.tensor_tensor(parts[s][1][:, k, :], p.ps[s][:, bank + k, :],
                                                parts[s][0][:, k, :].bitcast(F32), ALU.subtract).then_inc(lo[s].sem, 1)

                def front(it):
                    for s in SLOTS:
                        lower(s, it, 2, x_parts, hi_ready, lo_ready)

                def mid(it):
                    mid_chain.start(dve, it)
                    link = mid_chain.link
                    for s in SLOTS:
                        def scores(r):
                            return p.ps[s][:, r, :].rearrange("p (t c j) -> p t c j", t=TILES, c=CH)

                        by_bank = prob[s][:, :, :, :].rearrange("p t (c r) j -> p t c r j", c=CH)
                        for r0 in (0, 2):
                            for r in (r0, r0 + 1):
                                wait(dve, scored, s, it, r + 1)
                                ins = nc.vector.tensor_reduce(mx[s][:, r, :], p.ps[s][:, r, :].rearrange(
                                    "p (n j) -> p n j", j=NODES), AX.X, ALU.max)
                            link(ins)
                            for r in (r0, r0 + 1):
                                m = mx[s][:, r, :].rearrange("p (t c) -> p t c", t=TILES).unsqueeze(3).to_broadcast(
                                    [P, TILES, CH, NODES])
                                ins = nc.vector.tensor_tensor(by_bank[:, :, :, r, :], scores(r), m, ALU.subtract)
                        ins.then_inc(shifted[s].sem, 1)
                    for s in SLOTS:
                        heads = p.ps[s][:, :, 0:HP * VW].rearrange("p t (g c) -> p t g c", g=HP)
                        wait(dve, pv_done, s, it, TILES)
                        link(nc.vector.reciprocal(inv[s][:, :, :, :], heads[:, :, :, 2 * HD:VW]))
                        flat = inv[s][:, :, :, :].rearrange("p t g e -> p (t g e)")
                        link(nc.vector.tensor_scalar(flat, flat, p.nan_rows[:, :], None, ALU.add))
                        for t in range(TILES):
                            ins = nc.vector.tensor_tensor(
                                o_tok[s][:, t, :].rearrange("p (g e d) -> p g e d", g=HP, e=2),
                                heads[:, t, :, 0:2 * HD].rearrange("p g (e d) -> p g e d", e=2),
                                inv[s][:, t, :, :].unsqueeze(3).to_broadcast([P, HP, 2, HD]), ALU.mult)
                        ins.then_inc(o_ready[s].sem, 1)
                    lower(0, it, 0, o_parts, o_hi_ready, o_lo_ready)

                def tail(it):
                    tail_chain.start(dve, it)
                    link = tail_chain.link
                    lower(1, it, 0, o_parts, o_hi_ready, o_lo_ready)
                    for s in SLOTS:
                        for b in range(2):
                            wait(dve, proj_done, s, it, b + 1)
                            nc.vector.tensor_tensor(o_tok[s][:, 2 * b:2 * b + 2, :], two_tiles(s, b),
                                                    rows["b_proj"][:, :].unsqueeze(1).to_broadcast([P, 2, DIM]),
                                                    ALU.add).then_inc(proj_ready[s].sem, 1)
                    for s in SLOTS:
                        wait(dve, proj_ready, s, it, 2)
                        inner.statistics(tail_chain, s, o_tok[s])
                    for s in SLOTS:
                        wait(dve, y_ready, s, it, 0)
                        link(inner.apply(dve, it, s, o_tok[s], t_ln[s]))
                        link(nc.vector.tensor_tensor(t_ln[s][:, :, :], t_ln[s][:, :, :],
                                                     rows["ln_gamma"][:, :].unsqueeze(1).to_broadcast([P, TILES, DIM]),
                                                     ALU.mult))
                    for s in SLOTS:
                        wait(dve, sum_ready, s, it, 1)
                        nc.vector.tensor_tensor(t_ln[s][:, :, :], t_ln[s][:, :, :], res[s][:, :, :],
                                                ALU.add).then_inc(z_ready[s].sem, 1)
                        wait(dve, z_ready, s, it, 1)
                        outer.statistics(tail_chain, s, t_ln[s])
                    for s in SLOTS:
                        wait(dve, stored, s, it, 0)
                        outer.apply(dve, it, s, t_ln[s], y_tok[s]).then_inc(y_ready[s].sem, 1)

                staged(dve, front, mid, tail)


def gate_weights(p, parts, biases):
    nc = p.nc
    with ExitStack() as own:
        wide = {n: p.sb(f"l3_nat_{n}", [P, CH, 2 * DIM], stack=own) for n in ("w3", "w4", "w5")}
        nat = {n: p.sb(f"l3_nat_{n}", [P, CH, DIM], stack=own) for n in ("u3", "u5", "s3", "w4s", "w5s", "diff")}
        raw = p.sb("l3_raw_bias", [P, 5, CH], stack=own)
        loaded, natural, turned, high, bias_loaded, summed, low = (p.sem(f"l3w_{n}") for n in (
            "loaded", "natural", "turned", "high", "bias_loaded", "summed", "low"))
        order = ("u3", "w4s", "w5s", "diff", "u5")
        bank = {n: p.ps[i // TILES][:, i % TILES, :].rearrange("p (k o) -> p k o", k=CH) for i, n in enumerate(order)}
        with nc.Block() as block:

            @block.sync
            def _(sp):
                for n in ("w3", "w4", "w5"):
                    sp.dma_start(wide[n][:, :, :], p.a[f"L3_gnn_{n}_w"].rearrange("(m p) i -> p m i", p=P)).then_inc(loaded, 16)
                for n in ("u3", "u5"):
                    sp.dma_start(nat[n][:, :, :], p.a[f"L3_gnn_{n}_w"].rearrange("(m p) i -> p m i", p=P)).then_inc(loaded, 16)
                for i, n in enumerate(("w3", "w4", "w5", "u3", "u5")):
                    sp.dma_start(raw[:, i, :], p.a[f"L3_gnn_{n}_b"].rearrange("(m p) -> p m", p=P),
                                 allow_slow_non_contiguous=True).then_inc(bias_loaded, 16)
                sp.wait_ge(loaded, 80)

            @block.vector
            def _(dve):
                dve.wait_ge(loaded, 80)
                for n, to in (("w3", "s3"), ("w4", "w4s"), ("w5", "w5s")):
                    nc.vector.tensor_tensor(nat[to][:, :, :], wide[n][:, :, 0:DIM], wide[n][:, :, DIM:2 * DIM],
                                            ALU.add).then_inc(summed, 1)
                dve.wait_ge(summed, 3)
                nc.vector.tensor_tensor(nat["diff"][:, :, :], nat["s3"][:, :, :], nat["w4s"][:, :, :],
                                        ALU.subtract).then_inc(natural, 1)
                dve.wait_ge(bias_loaded, 80)
                for n, (i, j) in (("z", (0, 3)), ("r", (1, 3)), ("h", (2, 4))):
                    nc.vector.tensor_tensor(biases[n][:, :], raw[:, i, :], raw[:, j, :], ALU.add)
                for i, n in enumerate(order):
                    dve.wait_ge(high, i + 1)
                    nc.vector.tensor_tensor(parts[n][1][:, :, :], bank[n], parts[n][0][:, :, :].bitcast(F32),
                                            ALU.subtract).then_inc(low, 1)
                dve.wait_ge(low, len(order))

            @block.tensor
            def _(pe):
                pe.wait_ge(natural, 1)
                for n in order:
                    for k in range(CH):
                        for m in range(CH):
                            ins = nc.tensor.transpose(bank[n][:, k, m * P:(m + 1) * P], nat[n][:, m, k * P:(k + 1) * P],
                                                      p.ident[:, :])
                    ins.then_inc(turned, 1)

            @block.scalar
            def _(act):
                for i, n in enumerate(order):
                    act.wait_ge(turned, i + 1)
                    nc.scalar.activation(parts[n][0][:, :, :], bank[n], ACT.Copy).then_inc(high, 1)


def layer3(p, src, dst):
    nc = p.nc
    STEPS = 3
    A, B = SLOTS
    with ExitStack() as own:
        parts = {n: [p.sb(f"l3_{n}_{q}", [P, CH, DIM], F32R, stack=own) for q in ("hi", "lo")]
                 for n in ("u3", "w4s", "w5s", "diff", "u5")}
        biases = {n: p.sb(f"l3_bias_{n}", [P, CH], stack=own) for n in ("z", "r", "h")}
        gate_weights(p, parts, biases)
        two = lambda name, shape, dt=F32: [p.sb(f"l3_{name}{s}", shape, dt, stack=own) for s in SLOTS]
        x_tok = two("x", [P, TILES, DIM])
        y_tok = two("y", [P, TILES, DIM])
        h_tok = two("htok", [P, TILES, DIM])
        h = two("h", [P, CH, GROUP])
        h_hi = two("hhi", [P, CH, GROUP], F32R)
        h_lo = two("hlo", [P, CH, GROUP], F32R)
        a_hi = two("ahi", [P, CH, GROUP], F32R)
        a_lo = two("alo", [P, CH, GROUP], F32R)
        r = two("r", [P, CH, GROUP])
        rh_hi = two("rhhi", [P, CH, GROUP], F32R)
        rh_lo = two("rhlo", [P, CH, GROUP], F32R)
        d = two("d", [P, CH, GROUP])
        z = two("z", [P, TILES, DIM])
        norm = Norm(p, "l3", own)

        each = CH * STEPS
        loaded = p.signals("l3_loaded", 16)
        x_free = p.signals("l3_x_free", CH, 1)
        stored = p.signals("l3_stored", 16, 16)
        y_ready = p.signals("l3_y_ready", 1, 1)
        x_turned = p.signals("l3_x_turned", CH)
        adj_done = p.signals("l3_adj_done", each)
        r_done = p.signals("l3_r_done", each)
        z_done = p.signals("l3_z_done", each)
        hv_done = p.signals("l3_hv_done", each)
        tok_done = p.signals("l3_tok_done", each)
        h_hi_ready = p.signals("l3_h_hi_ready", each)
        h_lo_ready = p.signals("l3_h_lo_ready", each)
        a_hi_ready = p.signals("l3_a_hi_ready", each)
        a_lo_ready = p.signals("l3_a_lo_ready", each)
        r_ready = p.signals("l3_r_ready", each)
        rh_ready = p.signals("l3_rh_ready", each)
        rh_hi_ready = p.signals("l3_rh_hi_ready", each)
        rh_lo_ready = p.signals("l3_rh_lo_ready", each)
        z_ready = p.signals("l3_z_ready", each)
        hv_ready = p.signals("l3_hv_ready", each)
        h_new = p.signals("l3_h_new", each)
        tok_ready = p.signals("l3_tok_ready", CH * (STEPS - 1))
        mid_chain = Chain(p.sem("l3_mid_chain"), 2 * 2 * STEPS)
        tail_chain = Chain(p.sem("l3_tail_chain"), 2)

        RZ = [p.ps[s][:, 0:2, :] for s in SLOTS]
        HV = [p.ps[s][:, 2:4, :] for s in SLOTS]

        def wait(eng, signal, s, it, n):
            eng.wait_ge(signal[s].sem, signal[s].at(it, n))

        with nc.Block() as block:
            stream(p, block, src, dst, x_tok, y_tok, loaded, x_free, y_ready, stored)

            @block.tensor
            def _(pe):
                def turn_x(s, it):
                    wait(pe, loaded, s, it, 16)
                    wait(pe, x_free, s, it, 0)
                    for k in range(CH):
                        for t in range(TILES):
                            ins = nc.tensor.transpose(RZ[s][:, k, t * P:(t + 1) * P],
                                                      x_tok[s][:, t, k * P:(k + 1) * P], p.ident[:, :])
                        ins.then_inc(x_turned[s].sem, 1)

                def aggregate(s, step, it):
                    if step:
                        wait(pe, tok_ready, s, it, CH * step)
                    nodes = h_tok[s] if step else x_tok[s]
                    for k in range(CH):
                        for t in range(TILES):
                            ins = nc.tensor.matmul(HV[s][:, k, t * P:(t + 1) * P], nodes[:, t, k * P:(k + 1) * P],
                                                   p.adj_t[:, :], start=True, stop=True)
                        ins.then_inc(adj_done[s].sem, 1)

                def product(out, name, m, hi, lo, first, last):
                    for k in range(CH):
                        q = slice(m * P, (m + 1) * P)
                        ins = matmul3(nc, out[:, m, :], (parts[name][0][:, k, q], parts[name][1][:, k, q]),
                                      (hi[:, k, :], lo[:, k, :]), first and k == 0, last and k == CH - 1)
                    return ins

                def gates_from_a(s, step, it):
                    wait(pe, h_hi_ready, s, it, CH * (step + 1))
                    wait(pe, h_lo_ready, s, it, CH * (step + 1))
                    for m in range(CH):
                        product(RZ[s], "u3", m, h_hi[s], h_lo[s], True, False)
                    wait(pe, a_lo_ready, s, it, CH * (step + 1))
                    for m in range(CH):
                        product(RZ[s], "w4s", m, a_hi[s], a_lo[s], False, True).then_inc(r_done[s].sem, 1)
                    for m in range(CH):
                        product(HV[s], "w5s", m, a_hi[s], a_lo[s], True, False)

                def gate_z(s, step, it):
                    for m in range(CH):
                        wait(pe, r_ready, s, it, CH * step + m + 1)
                        product(RZ[s], "diff", m, a_hi[s], a_lo[s], False, True).then_inc(z_done[s].sem, 1)

                def candidate(s, step, it):
                    wait(pe, rh_lo_ready, s, it, CH * (step + 1))
                    for m in range(CH):
                        product(HV[s], "u5", m, rh_hi[s], rh_lo[s], False, True).then_inc(hv_done[s].sem, 1)

                def turn_h(s, step, it):
                    wait(pe, h_new, s, it, CH * (step + 1))
                    for b in range(2):
                        for t in range(2):
                            for k in range(CH):
                                q = slice((2 * b + t) * P, (2 * b + t + 1) * P)
                                at = t * DIM + k * P
                                ins = nc.tensor.transpose(RZ[s][:, b, at:at + P], h[s][:, k, q], p.ident[:, :])
                        ins.then_inc(tok_done[s].sem, 1)

                def front(it):
                    turn_x(A, it)
                    aggregate(A, 0, it)

                def mid(it):
                    for step in range(STEPS):
                        gates_from_a(A, step, it)
                        turn_h(B, step - 1, it) if step else turn_x(B, it)
                        gate_z(A, step, it)
                        candidate(A, step, it)
                        aggregate(B, step, it)
                        gates_from_a(B, step, it)
                        turn_h(A, step, it)
                        gate_z(B, step, it)
                        candidate(B, step, it)
                        if step < STEPS - 1:
                            aggregate(A, step + 1, it)

                staged(pe, front, mid, lambda it: turn_h(B, STEPS - 1, it))

            @block.scalar
            def _(act):
                def take_x(s, it):
                    for k in range(CH):
                        wait(act, x_turned, s, it, k + 1)
                        nc.scalar.activation(h[s][:, k, :], RZ[s][:, k, :], ACT.Copy)
                        nc.scalar.activation(h_hi[s][:, k, :], RZ[s][:, k, :], ACT.Copy).then_inc(h_hi_ready[s].sem, 1)

                def a_high(s, step, it):
                    for k in range(CH):
                        wait(act, adj_done, s, it, CH * step + k + 1)
                        nc.scalar.activation(a_hi[s][:, k, :], HV[s][:, k, :], ACT.Copy).then_inc(a_hi_ready[s].sem, 1)

                def gate_r(s, step, it):
                    for m in range(CH):
                        wait(act, r_done, s, it, CH * step + m + 1)
                        nc.scalar.activation(r[s][:, m, :], RZ[s][:, m, :], ACT.Sigmoid,
                                             bias=biases["r"][:, m:m + 1]).then_inc(r_ready[s].sem, 1)
                    for m in range(CH):
                        wait(act, rh_ready, s, it, CH * step + m + 1)
                        nc.scalar.activation(rh_hi[s][:, m, :], r[s][:, m, :], ACT.Copy).then_inc(rh_hi_ready[s].sem, 1)

                def gate_z(s, step, it):
                    for m in range(CH):
                        wait(act, z_done, s, it, CH * step + m + 1)
                        nc.scalar.activation(RZ[s][:, m, :], RZ[s][:, m, :], ACT.Sigmoid,
                                             bias=biases["z"][:, m:m + 1]).then_inc(z_ready[s].sem, 1)

                def candidate(s, step, it):
                    for m in range(CH):
                        wait(act, hv_done, s, it, CH * step + m + 1)
                        nc.scalar.activation(HV[s][:, m, :], HV[s][:, m, :], ACT.Tanh,
                                             bias=biases["h"][:, m:m + 1]).then_inc(hv_ready[s].sem, 1)

                def h_high(s, step, it):
                    for m in range(CH):
                        wait(act, h_new, s, it, CH * step + m + 1)
                        nc.scalar.activation(h_hi[s][:, m, :], h[s][:, m, :], ACT.Copy).then_inc(h_hi_ready[s].sem, 1)

                def take_h(s, step, it):
                    for b in range(2):
                        wait(act, tok_done, s, it, 2 * step + b + 1)
                        nc.scalar.activation(h_tok[s][:, 2 * b:2 * b + 2, :],
                                             RZ[s][:, b, :].rearrange("p (t f) -> p t f", t=2),
                                             ACT.Copy).then_inc(tok_ready[s].sem, 1)

                def front(it):
                    take_x(A, it)
                    a_high(A, 0, it)

                def mid(it):
                    for step in range(STEPS):
                        if step:
                            h_high(B, step - 1, it)
                        gate_r(A, step, it)
                        take_h(B, step - 1, it) if step else take_x(B, it)
                        gate_z(A, step, it)
                        candidate(A, step, it)
                        a_high(B, step, it)
                        if step < STEPS - 1:
                            h_high(A, step, it)
                        gate_r(B, step, it)
                        if step < STEPS - 1:
                            take_h(A, step, it)
                        gate_z(B, step, it)
                        candidate(B, step, it)
                        if step < STEPS - 1:
                            a_high(A, step + 1, it)

                staged(act, front, mid, lambda it: None)

            @block.gpsimd
            def _(pool):
                def h_low(s, step, it):
                    for m in range(CH):
                        wait(pool, h_hi_ready, s, it, CH * step + m + 1)
                        nc.gpsimd.tensor_tensor(h_lo[s][:, m, :], h[s][:, m, :], h_hi[s][:, m, :].bitcast(F32),
                                                ALU.subtract).then_inc(h_lo_ready[s].sem, 1)

                def mid(it):
                    for step in range(STEPS):
                        h_low(B, step, it)
                        if step < STEPS - 1:
                            h_low(A, step + 1, it)

                def tail(it):
                    for s in SLOTS:
                        norm.root(pool, it, s)

                for s in SLOTS:
                    pool.sem_inc(y_ready[s].sem, 1)
                staged(pool, lambda it: h_low(A, 0, it), mid, tail)

            @block.vector
            def _(dve):
                for s in SLOTS:
                    dve.sem_inc(x_free[s].sem, 1)

                def a_low(s, step, it):
                    for k in range(CH):
                        wait(dve, a_hi_ready, s, it, CH * step + k + 1)
                        nc.vector.tensor_tensor(a_lo[s][:, k, :], HV[s][:, k, :], a_hi[s][:, k, :].bitcast(F32),
                                                ALU.subtract).then_inc(a_lo_ready[s].sem, 1)

                def reset(s, step, it):
                    for m in range(CH):
                        wait(dve, r_ready, s, it, CH * step + m + 1)
                        nc.vector.tensor_tensor(r[s][:, m, :], r[s][:, m, :], h[s][:, m, :],
                                                ALU.mult).then_inc(rh_ready[s].sem, 1)
                    for m in range(CH):
                        wait(dve, rh_hi_ready, s, it, CH * step + m + 1)
                        nc.vector.tensor_tensor(rh_lo[s][:, m, :], r[s][:, m, :], rh_hi[s][:, m, :].bitcast(F32),
                                                ALU.subtract).then_inc(rh_lo_ready[s].sem, 1)

                def update(s, step, it):
                    for m in range(CH):
                        wait(dve, hv_ready, s, it, CH * step + m + 1)
                        ins = nc.vector.tensor_tensor(d[s][:, m, :], HV[s][:, m, :], h[s][:, m, :], ALU.subtract)
                    mid_chain.link(ins)
                    for m in range(CH):
                        wait(dve, z_ready, s, it, CH * step + m + 1)
                        ins = nc.vector.tensor_tensor(d[s][:, m, :], RZ[s][:, m, :], d[s][:, m, :], ALU.mult)
                    mid_chain.link(ins)
                    for m in range(CH):
                        nc.vector.tensor_tensor(h[s][:, m, :], h[s][:, m, :], d[s][:, m, :],
                                                ALU.add).then_inc(h_new[s].sem, 1)

                def residual(s, it):
                    wait(dve, y_ready, s, it, 0)
                    for b in range(2):
                        wait(dve, tok_done, s, it, 2 * (STEPS - 1) + b + 1)
                        nc.vector.tensor_tensor(z[s][:, 2 * b:2 * b + 2, :],
                                                RZ[s][:, b, :].rearrange("p (t f) -> p t f", t=2),
                                                x_tok[s][:, 2 * b:2 * b + 2, :], ALU.add).then_inc(x_free[s].sem, 1)

                def mid(it):
                    mid_chain.start(dve, it)
                    for step in range(STEPS):
                        if step:
                            update(B, step - 1, it)
                        reset(A, step, it)
                        a_low(B, step, it)
                        update(A, step, it)
                        reset(B, step, it)
                        if step < STEPS - 1:
                            a_low(A, step + 1, it)
                    residual(A, it)
                    update(B, STEPS - 1, it)

                def tail(it):
                    tail_chain.start(dve, it)
                    residual(B, it)
                    for s in SLOTS:
                        wait(dve, x_free, s, it, CH)
                        norm.statistics(tail_chain, s, z[s])
                    for s in SLOTS:
                        wait(dve, stored, s, it, 0)
                        norm.apply(dve, it, s, z[s], y_tok[s]).then_inc(y_ready[s].sem, 1)

                staged(dve, lambda it: a_low(A, 0, it), mid, tail)


LAYERS = (layer0, layer1, layer2, layer3,)


def build(nc, a, out):
    with ExitStack() as stack:
        p = Program(nc, a, out, stack)
        constants(p)
        p.clear_semaphores()
        src = a["x"].rearrange("b n d -> (b n) d")
        last = len(LAYERS) - 1
        for n, layer in enumerate(LAYERS):
            dst = (out.rearrange("b n d -> (b n) d") if n == last else
                   nc.dram_tensor(f"x_after_{n}", (GRAPHS * NODES, DIM), F32, kind="Internal").ap())
            layer(p, p.view(src), p.view(dst))
            src = dst
            p.clear_semaphores()


_OUT = ((GRAPHS, NODES, DIM), "float32")


def kernel(**inputs):
    import numpy as _np
    import concourse.bacc as _bacc
    from concourse import mybir as _mybir
    from concourse.bass_utils import run_bass_kernel_spmd as _run

    nc = _bacc.Bacc("TRN2", target_bir_lowering=False, num_devices=1)
    arrays, args = {}, {}
    for name in inputs:
        a = _np.ascontiguousarray(inputs[name])
        arrays[f"in_{name}_dram"] = a
        args[name] = nc.dram_tensor(f"in_{name}_dram", a.shape, _mybir.dt.from_np(a.dtype), kind="ExternalInput").ap()
    out = nc.dram_tensor("out_0_dram", _OUT[0], _mybir.dt.from_np(_np.dtype(_OUT[1])), kind="ExternalOutput").ap()
    build(nc, args, out)
    r = _run(nc, [arrays], core_ids=[0])
    return r.results[0]["out_0_dram"]
```

```python
from contextlib import ExitStack

import concourse.bass as bass
from concourse import mybir

F32 = mybir.dt.float32
F32R = mybir.dt.float32r
BF16 = mybir.dt.bfloat16
ALU = mybir.AluOpType
ACT = mybir.ActivationFunctionType
AX = mybir.AxisListType

GRAPHS, NODES, DIM = 128, 64, 256
P = 128
PER_TILE = P // NODES
TILES = 4
GROUP = TILES * P
PAIRS = GRAPHS * NODES // (2 * GROUP)
CH = DIM // P
HEADS, HD = 8, 32
BANK = 512
EPS = 1e-5
SLOPE = 0.2
MASKED = -3.0e38
SLOTS = (0, 1)


class Signal:

    def __init__(self, sem, per, primed=0):
        self.sem, self.per, self.primed = sem, per, primed

    def at(self, it, n):
        return it * self.per + (n + self.primed)


class Chain:

    def __init__(self, sem, per):
        self.sem, self.per, self.n = sem, per, 0

    def start(self, eng, it):
        assert self.n in (0, self.per), (self.sem, self.n)
        self.eng, self.it, self.n = eng, it, 0

    def link(self, ins):
        self.n += 1
        ins.then_inc(self.sem, 1)
        self.eng.wait_ge(self.sem, self.it * self.per + self.n)


NOW, NEXT, LATER = 0, 1, 2


def staged(eng, *parts):
    depth = max(ahead for ahead, _ in parts)

    def peeled(steps):
        for it in steps:
            for ahead, part in parts:
                if 0 <= it + ahead < PAIRS:
                    part(it + ahead)

    peeled(range(-depth, 0))
    with eng.Fori(0, PAIRS - depth) as it:
        for ahead, part in parts:
            part(it + ahead if ahead else it)
    peeled(range(PAIRS - depth, PAIRS))


class Program:
    def __init__(self, nc, a, out, stack):
        self.nc, self.a, self.out, self.stack = nc, a, out, stack
        self.taken = []
        self.ps = [stack.enter_context(nc.psum_tensor(f"banks{s}", [P, TILES, BANK], F32)) for s in SLOTS]
        sb = self.sb
        self.ident = sb("ident", [P, P])
        self.ident_bf = sb("ident_bf", [P, P], BF16)
        self.adj_t = sb("adj_t", [P, P])
        self.adj2 = sb("adj2", [P, NODES])
        self.mask_bias = sb("mask_bias", [P, NODES], BF16)
        self.nan_rows = sb("nan_rows", [P, 1])
        self.same_graph = sb("same_graph", [P, P])
        self.ident2 = sb("ident2", [P, NODES])
        self.eps = sb("eps", [P, TILES])
        self.minus_half = sb("minus_half", [P, TILES])
        self.minus_one = sb("minus_one", [P, 1])

    def sb(self, name, shape, dt=F32, stack=None):
        return (stack or self.stack).enter_context(self.nc.sbuf_tensor(name, shape, dt))

    def sem(self, name):
        self.taken.append(self.nc.alloc_semaphore(name=name))
        return self.taken[-1]

    def clear_semaphores(self):
        self.nc.all_engine_barrier()
        self.nc.clear_and_free_semaphores(self.taken)
        self.nc.all_engine_barrier()
        self.taken = []

    def signals(self, name, per, primed=0):
        return [Signal(self.sem(f"{name}{s}"), per, primed) for s in SLOTS]

    def view(self, x):
        return x.rearrange("(i s t p) d -> i s p t d", s=2, t=TILES, p=P)


def matmul3(nc, out, w, x, first, last):
    nc.tensor.matmul(out, w[0], x[0], start=first, stop=False, skip_group_check=True)
    nc.tensor.matmul(out, w[0], x[1], start=False, stop=False, skip_group_check=True)
    return nc.tensor.matmul(out, w[1], x[0], start=False, stop=last, skip_group_check=True)


def constants(p):
    nc = p.nc
    with ExitStack() as own:
        adj_blk = p.sb("adj_blk", [P, P], stack=own)
        hits = p.sb("hits", [P, NODES], stack=own)
        count = p.sb("count", [P, 1], stack=own)
        zeroed, made, loaded, turned, chain = (p.sem(n) for n in (
            "c_zeroed", "c_made", "c_loaded", "c_turned", "c_chain"))
        with nc.Block() as block:

            @block.gpsimd
            def _(pool):
                nc.gpsimd.memset(p.ident[:, :], 0.0).then_inc(zeroed, 1)
                nc.gpsimd.memset(adj_blk[:, :], 0.0).then_inc(zeroed, 1)
                nc.gpsimd.memset(p.same_graph[:, :], 0.0).then_inc(zeroed, 1)
                nc.gpsimd.memset(p.eps[:, :], EPS)
                nc.gpsimd.memset(p.minus_half[:, :], -0.5)
                nc.gpsimd.memset(p.minus_one[:, :], -1.0)
                pool.wait_ge(zeroed, 3)
                nc.gpsimd.affine_select(out=p.ident[:, :], in_=p.ident[:, :], compare_op=ALU.not_equal, fill=1.0,
                                        base=0, pattern=[[-1, P]], channel_multiplier=1).then_inc(made, 1)

            @block.sync
            def _(sp):
                sp.wait_ge(zeroed, 3)
                for b in range(PER_TILE):
                    q = slice(b * NODES, (b + 1) * NODES)
                    sp.dma_start(adj_blk[q, q], p.a["adj"]).then_inc(loaded, 16)
                    sp.dma_start(p.adj2[q, :], p.a["adj"]).then_inc(loaded, 16)
                sp.wait_ge(loaded, 64)

            @block.tensor
            def _(pe):
                pe.wait_ge(made, 1)
                pe.wait_ge(loaded, 64)
                nc.tensor.transpose(p.ps[0][:, 0, 0:P], adj_blk[:, :], p.ident[:, :]).then_inc(turned, 1)

            @block.vector
            def _(dve):
                links = Chain(chain, 7)
                links.start(dve, 0)
                dve.wait_ge(loaded, 64)
                dve.wait_ge(made, 1)
                for b in range(PER_TILE):
                    q = slice(b * NODES, (b + 1) * NODES)
                    nc.vector.memset(p.same_graph[q, q], 1.0)
                nc.vector.tensor_copy(p.ident_bf[:, :], p.ident[:, :])
                nc.vector.tensor_tensor(p.ident2[:, :], p.ident[:, 0:NODES], p.ident[:, NODES:P], ALU.add)
                nc.vector.tensor_scalar(p.mask_bias[:, :], p.adj2[:, :], 0.0, MASKED, ALU.is_equal, ALU.mult)
                links.link(nc.vector.tensor_scalar(hits[:, :], p.adj2[:, :], 0.0, None, ALU.not_equal))
                links.link(nc.vector.reduce_sum(count[:, :], hits[:, :], AX.X))
                links.link(nc.vector.tensor_scalar(count[:, :], count[:, :], 1.0, None, ALU.min))
                links.link(nc.vector.reciprocal(count[:, :], count[:, :]))
                links.link(nc.vector.tensor_scalar(p.nan_rows[:, :], count[:, :], 0.0, None, ALU.mult))
                dve.wait_ge(turned, 1)
                links.link(nc.vector.tensor_copy(p.adj_t[:, :], p.ps[0][:, 0, 0:P]))
                links.link(nc.vector.tensor_copy(hits[:, 0:1], p.nan_rows[:, :]))


class Norm:

    LINKS = 2

    def __init__(self, p, name, stack):
        self.p = p
        self.carrier = p.sb(f"{name}_carrier", [P, 1], stack=stack)
        self.stats = [p.sb(f"{name}_stats{s}", [P, TILES, 6], stack=stack) for s in SLOTS]
        self.mv = [p.sb(f"{name}_mv{s}", [P, TILES, 2], stack=stack) for s in SLOTS]
        self.rstd = [p.sb(f"{name}_rstd{s}", [P, TILES], stack=stack) for s in SLOTS]
        self.var_ready = p.signals(f"{name}_var_ready", 1)
        self.eps_added = p.signals(f"{name}_eps_added", 1)
        self.rstd_ready = p.signals(f"{name}_rstd_ready", 1)
        self.offset = [p.sb(f"{name}_offset{s}", [P, TILES], stack=stack) for s in SLOTS]
        self.offset_ready = p.signals(f"{name}_offset_ready", 1)

    def statistics(self, links, s, z):
        nc = self.p.nc
        for t in range(TILES):
            ins = nc.vector.bn_stats(self.stats[s][:, t, :], z[:, t, :])
        links.link(ins)
        nc.vector.memset(self.carrier[:, :], 0.0)
        for t in range(TILES):
            ins = nc.vector.bn_aggr(self.mv[s][:, t, :], self.stats[s][:, t, :])
        ins.then_inc(self.var_ready[s].sem, 1)

    def root(self, pool, it, s):
        nc = self.p.nc
        pool.wait_ge(self.var_ready[s].sem, self.var_ready[s].at(it, 1))
        nc.gpsimd.tensor_tensor(self.rstd[s][:, :], self.mv[s][:, :, 1], self.p.eps[:, :],
                                ALU.add).then_inc(self.eps_added[s].sem, 1)
        pool.wait_ge(self.eps_added[s].sem, self.eps_added[s].at(it, 1))
        nc.gpsimd.tensor_tensor(self.rstd[s][:, :], self.rstd[s][:, :], self.p.minus_half[:, :],
                                ALU.pow).then_inc(self.rstd_ready[s].sem, 1)

    def apply(self, dve, it, s, z, y):
        nc = self.p.nc
        dve.wait_ge(self.rstd_ready[s].sem, self.rstd_ready[s].at(it, 1))
        for t in range(TILES):
            ins = nc.vector.tensor_scalar(y[:, t, :], z[:, t, :], self.mv[s][:, t, 0:1], self.rstd[s][:, t:t + 1],
                                          ALU.subtract, ALU.mult)
        return ins

    def take_offset(self, dve, it, s):
        dve.wait_ge(self.rstd_ready[s].sem, self.rstd_ready[s].at(it, 1))
        self.p.nc.vector.scalar_tensor_tensor(self.offset[s][:, :], self.mv[s][:, :, 0], -1.0, self.rstd[s][:, :],
                                              ALU.mult, ALU.mult).then_inc(self.offset_ready[s].sem, 1)

    def apply_scalar(self, act, it, s, z, y):
        act.wait_ge(self.offset_ready[s].sem, self.offset_ready[s].at(it, 1))
        for t in range(TILES):
            ins = self.p.nc.scalar.activation(y[:, t, :], z[:, t, :], ACT.Identity, scale=self.rstd[s][:, t:t + 1],
                                              bias=self.offset[s][:, t:t + 1])
        return ins


def stream(p, block, src, dst, x_tok, y_tok, loaded, x_free, y_ready, stored, lead=LATER):

    @block.sync
    def _(sp):
        for s in SLOTS:
            sp.sem_inc(stored[s].sem, stored[s].primed)

        def load(s):
            def part(it):
                sp.wait_ge(x_free[s].sem, x_free[s].at(it, 0))
                sp.dma_start(x_tok[s][:, :, :], src[it][s]).then_inc(loaded[s].sem, 16)
            return lead, part

        def store(s):
            def part(it):
                sp.wait_ge(y_ready[s].sem, y_ready[s].at(it, 1))
                sp.dma_start(dst[it][s], y_tok[s][:, :, :]).then_inc(stored[s].sem, 16)
            return NOW, part

        if lead == LATER:
            staged(sp, load(0), store(0), load(1), store(1))
        else:
            staged(sp, load(0), load(1), store(0), store(1))
        for s in SLOTS:
            sp.wait_ge(stored[s].sem, stored[s].at(PAIRS, 0))


def layer0(p, src, dst):
    nc = p.nc
    with ExitStack() as own:
        WX = DIM + 2
        w = p.sb("l0_w", [P, CH, WX], stack=own)
        a_row = p.sb("l0_a", [P, 2, DIM], stack=own)
        wa = p.sb("l0_wa", [P, CH, DIM], stack=own)
        beta = p.sb("l0_beta", [P, 1], stack=own)
        w_parts = [p.sb(f"l0_w{n}", [P, CH, WX], F32R, stack=own) for n in ("hi", "lo")]
        two = lambda name, shape, dt=F32: [p.sb(f"l0_{name}{s}", shape, dt, stack=own) for s in SLOTS]
        x_tok = two("x", [P, TILES, DIM])
        y_tok = two("y", [P, TILES, DIM])
        x_hi = two("xhi", [P, CH, GROUP], F32R)
        x_lo = two("xlo", [P, CH, GROUP], F32R)
        h = two("h", [P, TILES, WX])
        s2_diag = two("s2", [P, TILES, NODES])
        e = two("e", [P, TILES, NODES])
        small = two("small", [P, 3, TILES])
        att = two("att", [P, TILES, P])
        att_t = two("att_t", [P, TILES, P])
        v = two("v", [P, TILES, DIM])
        neg = two("neg", [P, TILES, DIM])
        res = two("res", [P, TILES, DIM])
        norm = Norm(p, "l0", own)

        w_loaded, w_chain, w_hi, w_ready, att_zeroed = (p.sem(f"l0_{n}") for n in (
            "w_loaded", "w_chain", "w_hi", "w_ready", "att_zeroed"))
        loaded = p.signals("l0_loaded", 16)
        x_free = p.signals("l0_x_free", 1, 1)
        stored = p.signals("l0_stored", 16, 16)
        y_ready = p.signals("l0_y_ready", 1, 1)
        turned = p.signals("l0_turned", CH)
        hi_ready = p.signals("l0_hi_ready", CH)
        lo_ready = p.signals("l0_lo_ready", CH)
        h_done = p.signals("l0_h_done", TILES, 1)
        h_ready = p.signals("l0_h_ready", TILES)
        spread = p.signals("l0_spread", 1)
        s2_done = p.signals("l0_s2_done", 1)
        shifted = p.signals("l0_shifted", 1)
        exp_done = p.signals("l0_exp_done", 1)
        att_ready = p.signals("l0_att_ready", 1)
        att_turned = p.signals("l0_att_turned", 1)
        att_t_ready = p.signals("l0_att_t_ready", 1)
        hp_done = p.signals("l0_hp_done", 2)
        v_ready = p.signals("l0_v_ready", 2, 1)
        relu_done = p.signals("l0_relu_done", 2)
        elu_ready = p.signals("l0_elu_ready", 2)
        res_ready = p.signals("l0_res_ready", 2)
        z_ready = p.signals("l0_z_ready", 2, 1)
        score_chain, share_chain, stat_chain = (
            [Chain(p.sem(f"l0_{n}_chain{s}"), per) for s in SLOTS] for n, per in (("score", 4), ("share", 2), ("stat", 1)))
        A, B = SLOTS

        def wait(eng, signal, s, it, n):
            eng.wait_ge(signal[s].sem, signal[s].at(it, n))

        with nc.Block() as block:
            stream(p, block, src, dst, x_tok, y_tok, loaded, x_free, y_ready, stored)

            @block.gpsimd
            def _(pool):
                pool.dma_start(w[:, :, 0:DIM], p.a["L0_gnn_W"].rearrange("(k p) f -> p k f", p=P)).then_inc(w_loaded, 16)
                pool.dma_start(a_row[:, :, :], p.a["L0_gnn_a"].rearrange("(j f) o -> o j f", j=2).to_broadcast(
                    [P, 2, DIM])).then_inc(w_loaded, 16)
                pool.dma_start(beta[:, :], p.a["L0_gnn_beta"].rearrange("(o a) -> o a", o=1).to_broadcast(
                    [P, 1])).then_inc(w_loaded, 16)
                for s in SLOTS:
                    nc.gpsimd.memset(att[s][:, :, :], 0.0).then_inc(att_zeroed, 1)
                    pool.sem_inc(x_free[s].sem, 1)

                def spread_s2(s, it):
                    wait(pool, h_ready, s, it, TILES)
                    nc.gpsimd.tensor_tensor(s2_diag[s][:, :, :], p.ident2[:, :].unsqueeze(1).to_broadcast([P, TILES, NODES]),
                                            h[s][:, :, DIM + 1:DIM + 2].to_broadcast([P, TILES, NODES]),
                                            ALU.mult).then_inc(spread[s].sem, 1)

                def less_one(s, it):
                    wait(pool, turned, s, it, CH)
                    wait(pool, z_ready, s, it, 0)
                    nc.gpsimd.tensor_tensor(res[s][:, :, :], x_tok[s][:, :, :],
                                            p.minus_one[:, :].unsqueeze(1).to_broadcast([P, TILES, DIM]),
                                            ALU.add).then_inc(x_free[s].sem, 1)

                def add_exp(s, it):
                    wait(pool, x_free, s, it, 1)
                    for b in range(2):
                        two_tiles = res[s][:, 2 * b:2 * b + 2, :]
                        wait(pool, elu_ready, s, it, b + 1)
                        nc.gpsimd.tensor_tensor(two_tiles, two_tiles, neg[s][:, 2 * b:2 * b + 2, :],
                                                ALU.add).then_inc(res_ready[s].sem, 1)

                staged(pool,
                       (NEXT, lambda it: spread_s2(A, it)),
                       (NEXT, lambda it: less_one(A, it)),
                       (NOW, lambda it: norm.root(pool, it, A)),
                       (NOW, lambda it: add_exp(B, it)),
                       (NEXT, lambda it: spread_s2(B, it)),
                       (NEXT, lambda it: less_one(B, it)),
                       (NOW, lambda it: norm.root(pool, it, B)),
                       (NEXT, lambda it: add_exp(A, it)))

            @block.tensor
            def _(pe):

                def turn(s, it):
                    wait(pe, loaded, s, it, 16)
                    for k in range(CH):
                        for t in range(TILES):
                            ins = nc.tensor.transpose(p.ps[s][:, k, t * P:(t + 1) * P],
                                                      x_tok[s][:, t, k * P:(k + 1) * P], p.ident[:, :])
                        ins.then_inc(turned[s].sem, 1)

                def project(s, it):
                    pe.wait_ge(w_ready, 1)
                    wait(pe, lo_ready, s, it, CH)
                    wait(pe, v_ready, s, it, 0)
                    for t in range(TILES):
                        for k in range(CH):
                            q = slice(t * P, (t + 1) * P)
                            ins = matmul3(nc, p.ps[s][:, t, 0:WX], (x_hi[s][:, k, q], x_lo[s][:, k, q]),
                                          (w_parts[0][:, k, :], w_parts[1][:, k, :]), k == 0, k == CH - 1)
                        ins.then_inc(h_done[s].sem, 1)

                def spread_s2(s, it):
                    wait(pe, spread, s, it, 1)
                    nc.tensor.matmul(p.ps[s][:, 0, 0:TILES * NODES], p.same_graph[:, :],
                                     s2_diag[s][:, :, :].rearrange("p t j -> p (t j)"),
                                     start=True, stop=True).then_inc(s2_done[s].sem, 1)

                def attend(s, it):
                    wait(pe, att_ready, s, it, 1)
                    for t in range(TILES):
                        ins = nc.tensor.transpose(p.ps[s][:, 1, t * P:(t + 1) * P], att[s][:, t, :], p.ident[:, :])
                    ins.then_inc(att_turned[s].sem, 1)
                    wait(pe, att_t_ready, s, it, 1)
                    for t in range(TILES):
                        ins = nc.tensor.matmul(p.ps[s][:, 2 + t // 2, (t % 2) * DIM:(t % 2 + 1) * DIM],
                                               att_t[s][:, t, :], h[s][:, t, 0:DIM], start=True, stop=True)
                        if t % 2:
                            ins.then_inc(hp_done[s].sem, 1)

                for s in SLOTS:
                    pe.sem_inc(h_done[s].sem, 1)
                staged(pe,
                       (NEXT, lambda it: turn(A, it)),
                       (NOW, lambda it: spread_s2(B, it)),
                       (NEXT, lambda it: project(A, it)),
                       (NOW, lambda it: attend(B, it)),
                       (NEXT, lambda it: turn(B, it)),
                       (NEXT, lambda it: spread_s2(A, it)),
                       (NEXT, lambda it: project(B, it)),
                       (NEXT, lambda it: attend(A, it)))

            @block.scalar
            def _(act):
                act.wait_ge(w_chain, 4)
                nc.scalar.activation(w_parts[0][:, :, :], w[:, :, :], ACT.Copy).then_inc(w_hi, 1)

                def high(s, it):
                    wait(act, h_done, s, it, 0)
                    for k in range(CH):
                        wait(act, turned, s, it, k + 1)
                        nc.scalar.activation(x_hi[s][:, k, :], p.ps[s][:, k, :], ACT.Copy).then_inc(hi_ready[s].sem, 1)

                def take_h(s, it, tiles):
                    for t in tiles:
                        wait(act, h_done, s, it, t + 1)
                        nc.scalar.activation(h[s][:, t, :], p.ps[s][:, t, 0:WX], ACT.Copy).then_inc(h_ready[s].sem, 1)

                def exp(s, it):
                    wait(act, shifted, s, it, 1)
                    nc.scalar.activation(e[s][:, :, :], e[s][:, :, :], ACT.Exp).then_inc(exp_done[s].sem, 1)

                def take_att(s, it):
                    wait(act, att_turned, s, it, 1)
                    nc.scalar.activation(att_t[s][:, :, :], p.ps[s][:, 1, :], ACT.Copy).then_inc(att_t_ready[s].sem, 1)

                def exp_negative(s, it):
                    for b in range(2):
                        wait(act, v_ready, s, it, b + 1)
                        nc.scalar.activation(neg[s][:, 2 * b:2 * b + 2, :], v[s][:, 2 * b:2 * b + 2, :], ACT.Relu,
                                             scale=-1.0).then_inc(relu_done[s].sem, 1)
                        wait(act, relu_done, s, it, b + 1)
                        nc.scalar.activation(neg[s][:, 2 * b:2 * b + 2, :], neg[s][:, 2 * b:2 * b + 2, :], ACT.Exp,
                                             scale=-1.0).then_inc(elu_ready[s].sem, 1)

                def normalise(s, it):
                    wait(act, stored, s, it, 0)
                    norm.apply_scalar(act, it, s, v[s], y_tok[s]).then_inc(y_ready[s].sem, 1)

                def take_h_b_exp_a(it):
                    take_h(B, it, range(0, 2))
                    exp(A, it)
                    take_h(B, it, range(2, TILES))

                staged(act,
                       (NOW, lambda it: exp(B, it)),
                       (NEXT, lambda it: take_h(A, it, range(TILES))),
                       (NOW, lambda it: take_att(B, it)),
                       (NOW, lambda it: exp_negative(B, it)),
                       (NEXT, lambda it: high(B, it)),
                       (NOW, lambda it: normalise(A, it)),
                       (NEXT, take_h_b_exp_a),
                       (NEXT, lambda it: take_att(A, it)),
                       (LATER, lambda it: high(A, it)),
                       (NEXT, lambda it: exp_negative(A, it)),
                       (NOW, lambda it: normalise(B, it)))

            @block.vector
            def _(dve):
                links = Chain(w_chain, 4)
                links.start(dve, 0)
                dve.wait_ge(w_loaded, 48)
                for j in range(2):
                    links.link(nc.vector.tensor_tensor(wa[:, :, :], w[:, :, 0:DIM],
                                                       a_row[:, j, :].unsqueeze(1).to_broadcast([P, CH, DIM]), ALU.mult))
                    links.link(nc.vector.tensor_reduce(w[:, :, DIM + j:DIM + j + 1], wa[:, :, :], AX.X, ALU.add))
                dve.wait_ge(w_hi, 1)
                nc.vector.tensor_tensor(w_parts[1][:, :, :], w[:, :, :], w_parts[0][:, :, :].bitcast(F32),
                                        ALU.subtract).then_inc(w_ready, 1)
                dve.wait_ge(att_zeroed, 2)
                for s in SLOTS:
                    dve.sem_inc(v_ready[s].sem, 1)
                    dve.sem_inc(z_ready[s].sem, 1)
                    dve.sem_inc(y_ready[s].sem, 1)

                def low(s, it):
                    for k in range(CH):
                        wait(dve, hi_ready, s, it, k + 1)
                        nc.vector.tensor_tensor(x_lo[s][:, k, :], p.ps[s][:, k, :], x_hi[s][:, k, :].bitcast(F32),
                                                ALU.subtract).then_inc(lo_ready[s].sem, 1)

                def scores(s, it):
                    score_chain[s].start(dve, it)
                    link = score_chain[s].link
                    mx = small[s][:, 0, :]
                    wait(dve, s2_done, s, it, 1)
                    ps2 = p.ps[s][:, 0, 0:TILES * NODES].rearrange("p (t j) -> p t j", t=TILES)
                    link(nc.vector.tensor_tensor(e[s][:, :, :], ps2,
                                                 h[s][:, :, DIM:DIM + 1].to_broadcast([P, TILES, NODES]), ALU.add))
                    link(nc.vector.scalar_tensor_tensor(e[s][:, :, :], e[s][:, :, :], SLOPE, e[s][:, :, :],
                                                        ALU.mult, ALU.max))
                    link(nc.vector.tensor_tensor(e[s][:, :, :], e[s][:, :, :],
                                                 p.adj2[:, :].unsqueeze(1).to_broadcast([P, TILES, NODES]), ALU.mult))
                    link(nc.vector.tensor_reduce(mx, e[s][:, :, :], AX.X, ALU.max))
                    nc.vector.tensor_tensor(e[s][:, :, :], e[s][:, :, :], mx.unsqueeze(2).to_broadcast(
                        [P, TILES, NODES]), ALU.subtract).then_inc(shifted[s].sem, 1)

                def share(s, it):
                    share_chain[s].start(dve, it)
                    link = share_chain[s].link
                    total, inv = small[s][:, 1, :], small[s][:, 2, :]
                    wait(dve, exp_done, s, it, 1)
                    link(nc.vector.tensor_reduce(total, e[s][:, :, :], AX.X, ALU.add))
                    link(nc.vector.reciprocal(inv, total))
                    for b in range(PER_TILE):
                        q = slice(b * NODES, (b + 1) * NODES)
                        ins = nc.vector.tensor_tensor(att[s][q, :, q], e[s][q, :, :], inv[q].unsqueeze(2).to_broadcast(
                            [NODES, TILES, NODES]), ALU.mult)
                    ins.then_inc(att_ready[s].sem, 1)

                def add_h(s, it):
                    wait(dve, y_ready, s, it, 0)
                    for b in range(2):
                        wait(dve, hp_done, s, it, b + 1)
                        ps = p.ps[s][:, 2 + b, :].rearrange("p (t f) -> p t f", t=2)
                        nc.vector.scalar_tensor_tensor(v[s][:, 2 * b:2 * b + 2, :], h[s][:, 2 * b:2 * b + 2, 0:DIM],
                                                       beta[:, :], ps, ALU.mult, ALU.add).then_inc(v_ready[s].sem, 1)

                def residual(s, it):
                    stat_chain[s].start(dve, it)
                    for b in range(2):
                        q = slice(2 * b, 2 * b + 2)
                        wait(dve, res_ready, s, it, b + 1)
                        nc.vector.scalar_tensor_tensor(v[s][:, q, :], v[s][:, q, :], 0.0, res[s][:, q, :],
                                                       ALU.max, ALU.add).then_inc(z_ready[s].sem, 1)
                    wait(dve, z_ready, s, it, 2)
                    norm.statistics(stat_chain[s], s, v[s])

                staged(dve,
                       (NOW, lambda it: scores(B, it)),
                       (NOW, lambda it: share(B, it)),
                       (NOW, lambda it: residual(A, it)),
                       (NOW, lambda it: add_h(B, it)),
                       (NOW, lambda it: norm.take_offset(dve, it, A)),
                       (NEXT, lambda it: low(B, it)),
                       (NEXT, lambda it: scores(A, it)),
                       (NEXT, lambda it: share(A, it)),
                       (NOW, lambda it: residual(B, it)),
                       (NEXT, lambda it: add_h(A, it)),
                       (LATER, lambda it: low(A, it)),
                       (NOW, lambda it: norm.take_offset(dve, it, B)))


def layer1(p, src, dst):
    nc = p.nc
    with ExitStack() as own:
        w = p.sb("l1_w", [P, CH, DIM], stack=own)
        bias = p.sb("l1_bias", [P, DIM], stack=own)
        w_parts = [p.sb(f"l1_w{n}", [P, CH, DIM], F32R, stack=own) for n in ("hi", "lo")]
        two = lambda name, shape, dt=F32: [p.sb(f"l1_{name}{s}", shape, dt, stack=own) for s in SLOTS]
        x_tok = two("x", [P, TILES, DIM])
        y_tok = two("y", [P, TILES, DIM])
        a_hi = two("ahi", [P, CH, GROUP], F32R)
        a_lo = two("alo", [P, CH, GROUP], F32R)
        res = two("res", [P, TILES, DIM])
        z = two("z", [P, TILES, DIM])
        norm = Norm(p, "l1", own)

        w_loaded, w_hi, w_ready = (p.sem(f"l1_{n}") for n in ("w_loaded", "w_hi", "w_ready"))
        loaded = p.signals("l1_loaded", 16)
        x_free = p.signals("l1_x_free", 1, 1)
        stored = p.signals("l1_stored", 16, 16)
        y_ready = p.signals("l1_y_ready", 1, 1)
        adj_done = p.signals("l1_adj_done", CH)
        hi_ready = p.signals("l1_hi_ready", CH)
        lo_ready = p.signals("l1_lo_ready", CH)
        out_done = p.signals("l1_out_done", 2, 1)
        z_ready = p.signals("l1_z_ready", 2, 1)
        stat_chain = [Chain(p.sem(f"l1_stat_chain{s}"), 1) for s in SLOTS]
        A, B = SLOTS

        def wait(eng, signal, s, it, n):
            eng.wait_ge(signal[s].sem, signal[s].at(it, n))

        with nc.Block() as block:
            stream(p, block, src, dst, x_tok, y_tok, loaded, x_free, y_ready, stored)

            @block.gpsimd
            def _(pool):
                pool.dma_start(w[:, :, :], p.a["L1_gnn_weight"].rearrange("(k p) f -> p k f", p=P)).then_inc(w_loaded, 16)
                pool.dma_start(bias[:, :], p.a["L1_gnn_bias"].rearrange("(o f) -> o f", o=1).to_broadcast(
                    [P, DIM])).then_inc(w_loaded, 16)
                for s in SLOTS:
                    pool.sem_inc(x_free[s].sem, 1)
                pool.wait_ge(w_loaded, 32)

                def add_bias(s, it):
                    wait(pool, adj_done, s, it, CH)
                    wait(pool, z_ready, s, it, 0)
                    nc.gpsimd.tensor_tensor(res[s][:, :, :], x_tok[s][:, :, :],
                                            bias[:, :].unsqueeze(1).to_broadcast([P, TILES, DIM]),
                                            ALU.add).then_inc(x_free[s].sem, 1)

                staged(pool,
                       (NOW, lambda it: norm.root(pool, it, A)),
                       (NEXT, lambda it: add_bias(B, it)),
                       (NOW, lambda it: norm.root(pool, it, B)),
                       (LATER, lambda it: add_bias(A, it)))

            @block.tensor
            def _(pe):
                for s in SLOTS:
                    pe.sem_inc(out_done[s].sem, 1)

                def aggregate(s, it):
                    wait(pe, loaded, s, it, 16)
                    for k in range(CH):
                        for t in range(TILES):
                            ins = nc.tensor.matmul(p.ps[s][:, k, t * P:(t + 1) * P],
                                                   x_tok[s][:, t, k * P:(k + 1) * P], p.adj_t[:, :],
                                                   start=True, stop=True)
                        ins.then_inc(adj_done[s].sem, 1)

                def product(s, it):
                    pe.wait_ge(w_ready, 1)
                    wait(pe, lo_ready, s, it, CH)
                    wait(pe, z_ready, s, it, 0)
                    for t in range(TILES):
                        for k in range(CH):
                            q = slice(t * P, (t + 1) * P)
                            ins = matmul3(nc, p.ps[s][:, 2 + t // 2, (t % 2) * DIM:(t % 2 + 1) * DIM],
                                          (a_hi[s][:, k, q], a_lo[s][:, k, q]),
                                          (w_parts[0][:, k, :], w_parts[1][:, k, :]), k == 0, k == CH - 1)
                        if t % 2:
                            ins.then_inc(out_done[s].sem, 1)

                staged(pe,
                       (NOW, lambda it: product(B, it)),
                       (NEXT, lambda it: aggregate(B, it)),
                       (NEXT, lambda it: product(A, it)),
                       (LATER, lambda it: aggregate(A, it)))

            @block.scalar
            def _(act):
                act.wait_ge(w_loaded, 32)
                nc.scalar.activation(w_parts[0][:, :, :], w[:, :, :], ACT.Copy).then_inc(w_hi, 1)

                def high(s, it):
                    wait(act, out_done, s, it, 0)
                    for k in range(CH):
                        wait(act, adj_done, s, it, k + 1)
                        nc.scalar.activation(a_hi[s][:, k, :], p.ps[s][:, k, :], ACT.Copy).then_inc(hi_ready[s].sem, 1)

                def normalise(s, it):
                    wait(act, stored, s, it, 0)
                    norm.apply_scalar(act, it, s, z[s], y_tok[s]).then_inc(y_ready[s].sem, 1)

                staged(act,
                       (NEXT, lambda it: high(B, it)),
                       (NOW, lambda it: normalise(A, it)),
                       (LATER, lambda it: high(A, it)),
                       (NOW, lambda it: normalise(B, it)))

            @block.vector
            def _(dve):
                dve.wait_ge(w_loaded, 32)
                dve.wait_ge(w_hi, 1)
                nc.vector.tensor_tensor(w_parts[1][:, :, :], w[:, :, :], w_parts[0][:, :, :].bitcast(F32),
                                        ALU.subtract).then_inc(w_ready, 1)
                for s in SLOTS:
                    dve.sem_inc(z_ready[s].sem, 1)
                    dve.sem_inc(y_ready[s].sem, 1)

                def low(s, it):
                    for k in range(CH):
                        wait(dve, hi_ready, s, it, k + 1)
                        nc.vector.tensor_tensor(a_lo[s][:, k, :], p.ps[s][:, k, :], a_hi[s][:, k, :].bitcast(F32),
                                                ALU.subtract).then_inc(lo_ready[s].sem, 1)

                def residual(s, it):
                    wait(dve, x_free, s, it, 1)
                    wait(dve, y_ready, s, it, 0)
                    for b in range(2):
                        wait(dve, out_done, s, it, b + 1)
                        nc.vector.tensor_tensor(z[s][:, 2 * b:2 * b + 2, :],
                                                p.ps[s][:, 2 + b, :].rearrange("p (t f) -> p t f", t=2),
                                                res[s][:, 2 * b:2 * b + 2, :], ALU.add).then_inc(z_ready[s].sem, 1)

                def statistics(s, it):
                    stat_chain[s].start(dve, it)
                    wait(dve, z_ready, s, it, 2)
                    norm.statistics(stat_chain[s], s, z[s])

                staged(dve,
                       (NOW, lambda it: residual(B, it)),
                       (NEXT, lambda it: low(B, it)),
                       (NOW, lambda it: norm.take_offset(dve, it, A)),
                       (NOW, lambda it: statistics(B, it)),
                       (NEXT, lambda it: residual(A, it)),
                       (LATER, lambda it: low(A, it)),
                       (NOW, lambda it: norm.take_offset(dve, it, B)),
                       (NEXT, lambda it: statistics(A, it)))


def layer2(p, src, dst):
    nc = p.nc
    with ExitStack() as own:
        ROWS = P // HD
        HP = HEADS // 2
        VW = 2 * HD + 2
        QK_BANK = (2, 3, 0, 1)
        w = p.sb("l2_w", [P, CH, 3 * DIM], stack=own)
        wp = p.sb("l2_wp", [P, CH, DIM], stack=own)
        w_parts = [p.sb(f"l2_w{n}", [P, CH, 3 * DIM], F32R, stack=own) for n in ("hi", "lo")]
        wp_parts = [p.sb(f"l2_wp{n}", [P, CH, DIM], F32R, stack=own) for n in ("hi", "lo")]
        rows = {n: p.sb(f"l2_{n}", [P, DIM], stack=own) for n in ("b_proj", "ln_gamma", "ln_beta")}
        two = lambda name, shape, dt=F32: [p.sb(f"l2_{name}{s}", shape, dt, stack=own) for s in SLOTS]
        x_tok = two("x", [P, TILES, DIM])
        y_tok = two("y", [P, TILES, DIM])
        x_parts = [(p.sb(f"l2_xhi{s}", [P, CH, GROUP], F32R, stack=own), p.sb(f"l2_xlo{s}", [P, CH, GROUP], F32R, stack=own))
                   for s in SLOTS]
        o_parts = [(p.sb(f"l2_ohi{s}", [P, CH, GROUP], F32R, stack=own), p.sb(f"l2_olo{s}", [P, CH, GROUP], F32R, stack=own))
                   for s in SLOTS]
        q_t = two("q", [P, CH, GROUP])
        k_t = two("k", [P, CH, GROUP])
        v_pair = two("vpair", [P, PER_TILE, TILES, HP, VW])
        v_stage = two("vstage", [P, TILES, HP, HD])
        prob = two("prob", [P, TILES, HEADS, NODES])
        prob_t = two("probt", [P, TILES, BANK])
        mx = two("mx", [P, ROWS, TILES * CH])
        inv = two("inv", [P, TILES, HP, 2])
        o_tok = two("otok", [P, TILES, DIM])
        t_ln = two("tln", [P, TILES, DIM])
        res = two("res", [P, TILES, DIM])
        inner, outer = Norm(p, "l2i", own), Norm(p, "l2o", own)

        w_loaded, w_hi, w_ready, blank, ones = (p.sem(f"l2_{n}") for n in ("w_loaded", "w_hi", "w_ready", "blank", "ones"))
        loaded = p.signals("l2_loaded", 16)
        x_free = p.signals("l2_x_free", 1, 1)
        stored = p.signals("l2_stored", 16, 16)
        y_ready = p.signals("l2_y_ready", 1, 1)
        turned = p.signals("l2_turned", CH)
        hi_ready = p.signals("l2_hi_ready", CH)
        lo_ready = p.signals("l2_lo_ready", CH)
        qk_done = p.signals("l2_qk_done", 2 * CH)
        qk_ready = p.signals("l2_qk_ready", 2 * CH)
        v_done = p.signals("l2_v_done", 1)
        v_staged = p.signals("l2_v_staged", 1)
        v_swapped = [p.signals(f"l2_v_swapped{b}_", 16) for b in range(PER_TILE)]
        scored = p.signals("l2_scored", ROWS)
        shifted = p.signals("l2_shifted", 1)
        exp_done = p.signals("l2_exp_done", TILES)
        prob_turned = p.signals("l2_prob_turned", TILES)
        prob_t_ready = p.signals("l2_prob_t_ready", TILES)
        pv_done = p.signals("l2_pv_done", TILES, 1)
        o_ready = p.signals("l2_o_ready", 1, 1)
        o_turned = p.signals("l2_o_turned", CH)
        o_hi_ready = p.signals("l2_o_hi_ready", CH)
        o_lo_ready = p.signals("l2_o_lo_ready", CH)
        proj_done = p.signals("l2_proj_done", 2, 1)
        proj_ready = p.signals("l2_proj_ready", 2, 1)
        sum_ready = p.signals("l2_sum_ready", 1)
        z_ready = p.signals("l2_z_ready", 1, 1)
        mid_chain = Chain(p.sem("l2_mid_chain"), 2 * 4)
        tail_chain = Chain(p.sem("l2_tail_chain"), 2 * 4)

        def wait(eng, signal, s, it, n):
            eng.wait_ge(signal[s].sem, signal[s].at(it, n))

        def two_tiles(s, bank):
            return p.ps[s][:, bank, :].rearrange("p (t f) -> p t f", t=2)

        def values(s, b, parity):
            q = slice(b * NODES, (b + 1) * NODES)
            v = p.ps[s][q, 2:4, :].rearrange("p b (t g e d) -> p (b t) g e d", t=2, e=2, d=HD)
            return v[:, :, :, parity, :]

        with nc.Block() as block:

            @block.sync
            def _(sp):
                for s in SLOTS:
                    sp.sem_inc(stored[s].sem, stored[s].primed)

                def load(it):
                    for s in SLOTS:
                        wait(sp, x_free, s, it, 0)
                        sp.dma_start(x_tok[s][:, :, :], src[it][s]).then_inc(loaded[s].sem, 16)

                def swap(it):
                    for s in SLOTS:
                        wait(sp, v_staged, s, it, 1)
                        for b in range(PER_TILE):
                            here = slice(b * NODES, (b + 1) * NODES)
                            there = slice((1 - b) * NODES, (2 - b) * NODES)
                            sp.dma_start(v_pair[s][there, b, :, :, (1 - b) * HD:(2 - b) * HD],
                                         v_stage[s][here, :, :, :]).then_inc(v_swapped[b][s].sem, 16)

                def store(it):
                    for s in SLOTS:
                        wait(sp, y_ready, s, it, 1)
                        sp.dma_start(dst[it][s], y_tok[s][:, :, :]).then_inc(stored[s].sem, 16)

                load(0)
                with sp.Fori(0, PAIRS - 1) as it:
                    swap(it)
                    load(it + 1)
                    store(it)
                swap(PAIRS - 1)
                store(PAIRS - 1)
                for s in SLOTS:
                    wait(sp, stored, s, PAIRS, 0)

            @block.gpsimd
            def _(pool):
                pool.dma_start(w[:, :, :], p.a["L2_gnn_w_qkv"].rearrange("(k p) f -> p k f", p=P)).then_inc(w_loaded, 16)
                pool.dma_start(wp[:, :, :], p.a["L2_gnn_w_proj"].rearrange("(k p) f -> p k f", p=P)).then_inc(w_loaded, 16)
                for n in rows:
                    pool.dma_start(rows[n][:, :], p.a[f"L2_gnn_{n}"].rearrange("(o f) -> o f", o=1).to_broadcast(
                        [P, DIM])).then_inc(w_loaded, 16)
                for s in SLOTS:
                    nc.gpsimd.memset(v_pair[s][:, :, :, :, :], 0.0).then_inc(blank, 1)
                    pool.sem_inc(x_free[s].sem, 1)
                pool.wait_ge(w_loaded, 80)

                def over_tiles(row):
                    return row[:, :].unsqueeze(1).to_broadcast([P, TILES, DIM])

                def mid(it):
                    for s in SLOTS:
                        wait(pool, turned, s, it, CH)
                        wait(pool, z_ready, s, it, 0)
                        nc.gpsimd.tensor_tensor(res[s][:, :, :], x_tok[s][:, :, :], over_tiles(rows["ln_beta"]),
                                                ALU.add).then_inc(x_free[s].sem, 1)

                def tail(it):
                    for s in SLOTS:
                        inner.root(pool, it, s)
                    for s in SLOTS:
                        wait(pool, x_free, s, it, 1)
                        nc.gpsimd.tensor_tensor(res[s][:, :, :], res[s][:, :, :], o_tok[s][:, :, :],
                                                ALU.add).then_inc(sum_ready[s].sem, 1)
                    for s in SLOTS:
                        outer.root(pool, it, s)

                staged(pool, (NOW, mid), (NOW, tail))

            @block.tensor
            def _(pe):
                pe.wait_ge(w_ready, 2)
                pe.wait_ge(w_hi, 2)
                pe.wait_ge(ones, 4)
                for s in SLOTS:
                    pe.sem_inc(pv_done[s].sem, 1)
                    pe.sem_inc(proj_done[s].sem, 1)

                def turn(s, rows_, bank, done):
                    for k in range(CH):
                        for t in range(TILES):
                            ins = nc.tensor.transpose(p.ps[s][:, bank + k, t * P:(t + 1) * P],
                                                      rows_[:, t, k * P:(k + 1) * P], p.ident[:, :])
                        ins.then_inc(done[s].sem, 1)

                def rows_by_weights(s, t, bank, of, weights, f0):
                    q = slice(t * P, (t + 1) * P)
                    for k in range(CH):
                        ins = matmul3(nc, p.ps[s][:, bank + t // 2, (t % 2) * DIM:(t % 2 + 1) * DIM],
                                      (of[0][:, k, q], of[1][:, k, q]),
                                      (weights[0][:, k, f0:f0 + DIM], weights[1][:, k, f0:f0 + DIM]),
                                      k == 0, k == CH - 1)
                    return ins

                def front(it):
                    for s in SLOTS:
                        wait(pe, loaded, s, it, 16)
                        wait(pe, o_ready, s, it, 0)
                        turn(s, x_tok[s], 2, turned)

                def mid(it):
                    for s in SLOTS:
                        wait(pe, lo_ready, s, it, CH)
                        for m in range(2 * CH):
                            if m == CH:
                                wait(pe, proj_ready, s, it, 0)
                            for k in range(CH):
                                q = slice(m * P, (m + 1) * P)
                                ins = matmul3(nc, p.ps[s][:, QK_BANK[m], :], (w_parts[0][:, k, q], w_parts[1][:, k, q]),
                                              (x_parts[s][0][:, k, :], x_parts[s][1][:, k, :]), k == 0, k == CH - 1)
                            ins.then_inc(qk_done[s].sem, 1)
                    for s in SLOTS:
                        wait(pe, qk_ready, s, it, CH)
                        for t in range(TILES):
                            ins = rows_by_weights(s, t, 2, x_parts[s], w_parts, 2 * DIM)
                        ins.then_inc(v_done[s].sem, 1)
                    for s in SLOTS:
                        wait(pe, qk_ready, s, it, 2 * CH)
                        wait(pe, v_staged, s, it, 1)
                        for r in range(ROWS):
                            nc.tensor.matmul(p.ps[s][:, r, :], p.ident_bf[:, :],
                                             p.mask_bias[:, :].unsqueeze(1).to_broadcast([P, TILES * CH, NODES]),
                                             start=True, stop=False, skip_group_check=True)
                        for t in range(TILES):
                            for c in range(CH):
                                for b in range(PER_TILE):
                                    for r in range(ROWS):
                                        q = slice(t * P + b * NODES, t * P + (b + 1) * NODES)
                                        col = (t * CH + c) * NODES
                                        ins = nc.tensor.matmul(
                                            p.ps[s][b * NODES:(b + 1) * NODES, r, col:col + NODES],
                                            q_t[s][r * HD:(r + 1) * HD, c, q], k_t[s][r * HD:(r + 1) * HD, c, q],
                                            start=False, stop=True, skip_group_check=True)
                                        if (t, c, b) == (TILES - 1, CH - 1, PER_TILE - 1):
                                            ins.then_inc(scored[s].sem, 1)
                    for s in SLOTS:
                        for t in range(TILES):
                            wait(pe, exp_done, s, it, t + 1)
                            for g in range(HP):
                                ins = nc.tensor.transpose(p.ps[s][:, t, g * P:(g + 1) * P],
                                                          prob[s][:, t, 2 * g:2 * g + 2, :].rearrange("p h j -> p (h j)"),
                                                          p.ident[:, :])
                            ins.then_inc(prob_turned[s].sem, 1)
                        for b in range(PER_TILE):
                            wait(pe, v_swapped[b], s, it, 16)
                        for t in range(TILES):
                            wait(pe, prob_t_ready, s, it, t + 1)
                            for g in range(HP):
                                for b in range(PER_TILE):
                                    at = g * P + b * NODES
                                    ins = nc.tensor.matmul(p.ps[s][b * NODES:(b + 1) * NODES, t, g * VW:(g + 1) * VW],
                                                           prob_t[s][:, t, at:at + NODES], v_pair[s][:, b, t, g, :],
                                                           start=True, stop=True)
                            ins.then_inc(pv_done[s].sem, 1)
                    wait(pe, o_ready, 0, it, 1)
                    turn(0, o_tok[0], 0, o_turned)

                def tail(it):
                    wait(pe, o_ready, 1, it, 1)
                    turn(1, o_tok[1], 0, o_turned)
                    for s in SLOTS:
                        wait(pe, o_lo_ready, s, it, CH)
                        for t in range(TILES):
                            ins = rows_by_weights(s, t, 0, o_parts[s], wp_parts, 0)
                            if t % 2:
                                ins.then_inc(proj_done[s].sem, 1)

                for s in SLOTS:
                    pe.sem_inc(o_ready[s].sem, 1)
                staged(pe, (NOW, mid), (NEXT, front), (NOW, tail))

            @block.scalar
            def _(act):
                act.wait_ge(w_loaded, 80)
                nc.scalar.activation(w_parts[0][:, :, :], w[:, :, :], ACT.Copy).then_inc(w_hi, 1)
                nc.scalar.activation(wp_parts[0][:, :, :], wp[:, :, :], ACT.Copy).then_inc(w_hi, 1)
                act.wait_ge(blank, 2)

                def high(s, it, bank, done, parts, ready):
                    for k in range(CH):
                        wait(act, done, s, it, k + 1)
                        nc.scalar.activation(parts[s][0][:, k, :], p.ps[s][:, bank + k, :], ACT.Copy).then_inc(ready[s].sem, 1)

                def high_o(s, it):
                    wait(act, proj_done, s, it, 0)
                    high(s, it, 0, o_turned, o_parts, o_hi_ready)

                def front(it):
                    for s in SLOTS:
                        high(s, it, 2, turned, x_parts, hi_ready)

                def mid(it):
                    for s in SLOTS:
                        for m in range(2 * CH):
                            wait(act, qk_done, s, it, m + 1)
                            bank = p.ps[s][:, QK_BANK[m], :]
                            if m < CH:
                                ins = nc.scalar.activation(q_t[s][:, m, :], bank, ACT.Copy, scale=float(HD) ** -0.5)
                            else:
                                ins = nc.scalar.activation(k_t[s][:, m - CH, :], bank, ACT.Copy)
                            ins.then_inc(qk_ready[s].sem, 1)
                    for s in SLOTS:
                        wait(act, v_done, s, it, 1)
                        wait(act, pv_done, s, it, 0)
                        for b in range(PER_TILE):
                            q = slice(b * NODES, (b + 1) * NODES)
                            nc.scalar.activation(v_pair[s][q, b, :, :, b * HD:(b + 1) * HD], values(s, b, b), ACT.Copy)
                            ins = nc.scalar.activation(v_stage[s][q, :, :, :], values(s, b, 1 - b), ACT.Copy)
                        ins.then_inc(v_staged[s].sem, 1)
                    for s in SLOTS:
                        wait(act, shifted, s, it, 1)
                        for t in range(TILES):
                            nc.scalar.activation(prob[s][:, t, :, :], prob[s][:, t, :, :], ACT.Exp).then_inc(exp_done[s].sem, 1)
                        for t in range(TILES):
                            wait(act, prob_turned, s, it, t + 1)
                            nc.scalar.activation(prob_t[s][:, t, :], p.ps[s][:, t, :], ACT.Copy).then_inc(prob_t_ready[s].sem, 1)
                    high_o(0, it)

                staged(act, (NOW, mid), (NEXT, front), (NOW, lambda it: high_o(1, it)))

            @block.vector
            def _(dve):
                dve.wait_ge(w_loaded, 80)
                dve.wait_ge(w_hi, 2)
                nc.vector.tensor_tensor(w_parts[1][:, :, :], w[:, :, :], w_parts[0][:, :, :].bitcast(F32),
                                        ALU.subtract).then_inc(w_ready, 1)
                nc.vector.tensor_tensor(wp_parts[1][:, :, :], wp[:, :, :], wp_parts[0][:, :, :].bitcast(F32),
                                        ALU.subtract).then_inc(w_ready, 1)
                dve.wait_ge(blank, 2)
                for s in SLOTS:
                    for e in range(2):
                        q = slice(e * NODES, (e + 1) * NODES)
                        nc.vector.memset(v_pair[s][q, :, :, :, 2 * HD + e], 1.0).then_inc(ones, 1)
                    for signal in (y_ready, proj_ready, z_ready):
                        dve.sem_inc(signal[s].sem, 1)

                def lower(s, it, bank, parts, hi, lo):
                    for k in range(CH):
                        wait(dve, hi, s, it, k + 1)
                        nc.vector.tensor_tensor(parts[s][1][:, k, :], p.ps[s][:, bank + k, :],
                                                parts[s][0][:, k, :].bitcast(F32), ALU.subtract).then_inc(lo[s].sem, 1)

                def front(it):
                    for s in SLOTS:
                        lower(s, it, 2, x_parts, hi_ready, lo_ready)

                def mid(it):
                    mid_chain.start(dve, it)
                    link = mid_chain.link
                    for s in SLOTS:
                        def scores(r):
                            return p.ps[s][:, r, :].rearrange("p (t c j) -> p t c j", t=TILES, c=CH)

                        by_bank = prob[s][:, :, :, :].rearrange("p t (c r) j -> p t c r j", c=CH)
                        for r0 in (0, 2):
                            for r in (r0, r0 + 1):
                                wait(dve, scored, s, it, r + 1)
                                ins = nc.vector.tensor_reduce(mx[s][:, r, :], p.ps[s][:, r, :].rearrange(
                                    "p (n j) -> p n j", j=NODES), AX.X, ALU.max)
                            link(ins)
                            for r in (r0, r0 + 1):
                                m = mx[s][:, r, :].rearrange("p (t c) -> p t c", t=TILES).unsqueeze(3).to_broadcast(
                                    [P, TILES, CH, NODES])
                                ins = nc.vector.tensor_tensor(by_bank[:, :, :, r, :], scores(r), m, ALU.subtract)
                        ins.then_inc(shifted[s].sem, 1)
                    for s in SLOTS:
                        heads = p.ps[s][:, :, 0:HP * VW].rearrange("p t (g c) -> p t g c", g=HP)
                        wait(dve, pv_done, s, it, TILES)
                        link(nc.vector.reciprocal(inv[s][:, :, :, :], heads[:, :, :, 2 * HD:VW]))
                        flat = inv[s][:, :, :, :].rearrange("p t g e -> p (t g e)")
                        link(nc.vector.tensor_scalar(flat, flat, p.nan_rows[:, :], None, ALU.add))
                        for t in range(TILES):
                            ins = nc.vector.tensor_tensor(
                                o_tok[s][:, t, :].rearrange("p (g e d) -> p g e d", g=HP, e=2),
                                heads[:, t, :, 0:2 * HD].rearrange("p g (e d) -> p g e d", e=2),
                                inv[s][:, t, :, :].unsqueeze(3).to_broadcast([P, HP, 2, HD]), ALU.mult)
                        ins.then_inc(o_ready[s].sem, 1)
                    lower(0, it, 0, o_parts, o_hi_ready, o_lo_ready)

                def tail(it):
                    tail_chain.start(dve, it)
                    link = tail_chain.link
                    lower(1, it, 0, o_parts, o_hi_ready, o_lo_ready)
                    for s in SLOTS:
                        for b in range(2):
                            wait(dve, proj_done, s, it, b + 1)
                            nc.vector.tensor_tensor(o_tok[s][:, 2 * b:2 * b + 2, :], two_tiles(s, b),
                                                    rows["b_proj"][:, :].unsqueeze(1).to_broadcast([P, 2, DIM]),
                                                    ALU.add).then_inc(proj_ready[s].sem, 1)
                    for s in SLOTS:
                        wait(dve, proj_ready, s, it, 2)
                        inner.statistics(tail_chain, s, o_tok[s])
                    for s in SLOTS:
                        wait(dve, y_ready, s, it, 0)
                        link(inner.apply(dve, it, s, o_tok[s], t_ln[s]))
                        link(nc.vector.tensor_tensor(t_ln[s][:, :, :], t_ln[s][:, :, :],
                                                     rows["ln_gamma"][:, :].unsqueeze(1).to_broadcast([P, TILES, DIM]),
                                                     ALU.mult))
                    for s in SLOTS:
                        wait(dve, sum_ready, s, it, 1)
                        nc.vector.tensor_tensor(t_ln[s][:, :, :], t_ln[s][:, :, :], res[s][:, :, :],
                                                ALU.add).then_inc(z_ready[s].sem, 1)
                        wait(dve, z_ready, s, it, 1)
                        outer.statistics(tail_chain, s, t_ln[s])
                    for s in SLOTS:
                        wait(dve, stored, s, it, 0)
                        outer.apply(dve, it, s, t_ln[s], y_tok[s]).then_inc(y_ready[s].sem, 1)

                staged(dve, (NOW, mid), (NEXT, front), (NOW, tail))


def gate_weights(p, parts, biases):
    nc = p.nc
    with ExitStack() as own:
        wide = {n: p.sb(f"l3_nat_{n}", [P, CH, 2 * DIM], stack=own) for n in ("w3", "w4", "w5")}
        nat = {n: p.sb(f"l3_nat_{n}", [P, CH, DIM], stack=own) for n in ("u3", "u5", "s3", "w4s", "w5s", "diff")}
        raw = p.sb("l3_raw_bias", [P, 5, CH], stack=own)
        loaded, natural, turned, high, bias_loaded, summed, low = (p.sem(f"l3w_{n}") for n in (
            "loaded", "natural", "turned", "high", "bias_loaded", "summed", "low"))
        order = ("u3", "w4s", "w5s", "diff", "u5")
        bank = {n: p.ps[i // TILES][:, i % TILES, :].rearrange("p (k o) -> p k o", k=CH) for i, n in enumerate(order)}
        with nc.Block() as block:

            @block.sync
            def _(sp):
                for n in ("w3", "w4", "w5"):
                    sp.dma_start(wide[n][:, :, :], p.a[f"L3_gnn_{n}_w"].rearrange("(m p) i -> p m i", p=P)).then_inc(loaded, 16)
                for n in ("u3", "u5"):
                    sp.dma_start(nat[n][:, :, :], p.a[f"L3_gnn_{n}_w"].rearrange("(m p) i -> p m i", p=P)).then_inc(loaded, 16)
                for i, n in enumerate(("w3", "w4", "w5", "u3", "u5")):
                    sp.dma_start(raw[:, i, :], p.a[f"L3_gnn_{n}_b"].rearrange("(m p) -> p m", p=P),
                                 allow_slow_non_contiguous=True).then_inc(bias_loaded, 16)
                sp.wait_ge(loaded, 80)

            @block.vector
            def _(dve):
                dve.wait_ge(loaded, 80)
                for n, to in (("w3", "s3"), ("w4", "w4s"), ("w5", "w5s")):
                    nc.vector.tensor_tensor(nat[to][:, :, :], wide[n][:, :, 0:DIM], wide[n][:, :, DIM:2 * DIM],
                                            ALU.add).then_inc(summed, 1)
                dve.wait_ge(summed, 3)
                nc.vector.tensor_tensor(nat["diff"][:, :, :], nat["s3"][:, :, :], nat["w4s"][:, :, :],
                                        ALU.subtract).then_inc(natural, 1)
                dve.wait_ge(bias_loaded, 80)
                for n, (i, j) in (("z", (0, 3)), ("r", (1, 3)), ("h", (2, 4))):
                    nc.vector.tensor_tensor(biases[n][:, :], raw[:, i, :], raw[:, j, :], ALU.add)
                for i, n in enumerate(order):
                    dve.wait_ge(high, i + 1)
                    nc.vector.tensor_tensor(parts[n][1][:, :, :], bank[n], parts[n][0][:, :, :].bitcast(F32),
                                            ALU.subtract).then_inc(low, 1)
                dve.wait_ge(low, len(order))

            @block.tensor
            def _(pe):
                pe.wait_ge(natural, 1)
                for n in order:
                    for k in range(CH):
                        for m in range(CH):
                            ins = nc.tensor.transpose(bank[n][:, k, m * P:(m + 1) * P], nat[n][:, m, k * P:(k + 1) * P],
                                                      p.ident[:, :])
                    ins.then_inc(turned, 1)

            @block.scalar
            def _(act):
                for i, n in enumerate(order):
                    act.wait_ge(turned, i + 1)
                    nc.scalar.activation(parts[n][0][:, :, :], bank[n], ACT.Copy).then_inc(high, 1)


def layer3(p, src, dst):
    nc = p.nc
    STEPS = 3
    A, B = SLOTS
    with ExitStack() as own:
        parts = {n: [p.sb(f"l3_{n}_{q}", [P, CH, DIM], F32R, stack=own) for q in ("hi", "lo")]
                 for n in ("u3", "w4s", "w5s", "diff", "u5")}
        biases = {n: p.sb(f"l3_bias_{n}", [P, CH], stack=own) for n in ("z", "r", "h")}
        gate_weights(p, parts, biases)
        two = lambda name, shape, dt=F32: [p.sb(f"l3_{name}{s}", shape, dt, stack=own) for s in SLOTS]
        x_tok = two("x", [P, TILES, DIM])
        y_tok = two("y", [P, TILES, DIM])
        h_tok = two("htok", [P, TILES, DIM])
        h = two("h", [P, CH, GROUP])
        h_hi = two("hhi", [P, CH, GROUP], F32R)
        h_lo = two("hlo", [P, CH, GROUP], F32R)
        a_hi = two("ahi", [P, CH, GROUP], F32R)
        a_lo = two("alo", [P, CH, GROUP], F32R)
        r = two("r", [P, CH, GROUP])
        rh_hi = two("rhhi", [P, CH, GROUP], F32R)
        rh_lo = two("rhlo", [P, CH, GROUP], F32R)
        d = two("d", [P, CH, GROUP])
        z = two("z", [P, TILES, DIM])
        norm = Norm(p, "l3", own)

        each = CH * STEPS
        loaded = p.signals("l3_loaded", 16)
        x_free = p.signals("l3_x_free", CH, 1)
        stored = p.signals("l3_stored", 16, 16)
        y_ready = p.signals("l3_y_ready", 1, 1)
        x_turned = p.signals("l3_x_turned", CH)
        adj_done = p.signals("l3_adj_done", each)
        r_done = p.signals("l3_r_done", each)
        z_done = p.signals("l3_z_done", each)
        hv_done = p.signals("l3_hv_done", each)
        tok_done = p.signals("l3_tok_done", each)
        h_hi_ready = p.signals("l3_h_hi_ready", each)
        h_lo_ready = p.signals("l3_h_lo_ready", each)
        a_hi_ready = p.signals("l3_a_hi_ready", each)
        a_lo_ready = p.signals("l3_a_lo_ready", each)
        r_ready = p.signals("l3_r_ready", each)
        rh_ready = p.signals("l3_rh_ready", each)
        rh_hi_ready = p.signals("l3_rh_hi_ready", each)
        rh_lo_ready = p.signals("l3_rh_lo_ready", each)
        z_ready = p.signals("l3_z_ready", each)
        hv_ready = p.signals("l3_hv_ready", each)
        h_new = p.signals("l3_h_new", each)
        tok_ready = p.signals("l3_tok_ready", CH * (STEPS - 1))
        mid_chain = Chain(p.sem("l3_mid_chain"), 2 * 2 * STEPS)
        tail_chain = Chain(p.sem("l3_tail_chain"), 2)

        RZ = [p.ps[s][:, 0:2, :] for s in SLOTS]
        HV = [p.ps[s][:, 2:4, :] for s in SLOTS]

        def wait(eng, signal, s, it, n):
            eng.wait_ge(signal[s].sem, signal[s].at(it, n))

        with nc.Block() as block:
            stream(p, block, src, dst, x_tok, y_tok, loaded, x_free, y_ready, stored, lead=NEXT)

            @block.tensor
            def _(pe):
                def turn_x(s, it):
                    wait(pe, loaded, s, it, 16)
                    wait(pe, x_free, s, it, 0)
                    for k in range(CH):
                        for t in range(TILES):
                            ins = nc.tensor.transpose(RZ[s][:, k, t * P:(t + 1) * P],
                                                      x_tok[s][:, t, k * P:(k + 1) * P], p.ident[:, :])
                        ins.then_inc(x_turned[s].sem, 1)

                def aggregate(s, step, it):
                    if step:
                        wait(pe, tok_ready, s, it, CH * step)
                    nodes = h_tok[s] if step else x_tok[s]
                    for k in range(CH):
                        for t in range(TILES):
                            ins = nc.tensor.matmul(HV[s][:, k, t * P:(t + 1) * P], nodes[:, t, k * P:(k + 1) * P],
                                                   p.adj_t[:, :], start=True, stop=True)
                        ins.then_inc(adj_done[s].sem, 1)

                def product(out, name, m, hi, lo, first, last):
                    for k in range(CH):
                        q = slice(m * P, (m + 1) * P)
                        ins = matmul3(nc, out[:, m, :], (parts[name][0][:, k, q], parts[name][1][:, k, q]),
                                      (hi[:, k, :], lo[:, k, :]), first and k == 0, last and k == CH - 1)
                    return ins

                def gates_from_a(s, step, it):
                    wait(pe, h_hi_ready, s, it, CH * (step + 1))
                    wait(pe, h_lo_ready, s, it, CH * (step + 1))
                    for m in range(CH):
                        product(RZ[s], "u3", m, h_hi[s], h_lo[s], True, False)
                    wait(pe, a_lo_ready, s, it, CH * (step + 1))
                    for m in range(CH):
                        product(RZ[s], "w4s", m, a_hi[s], a_lo[s], False, True).then_inc(r_done[s].sem, 1)
                    for m in range(CH):
                        product(HV[s], "w5s", m, a_hi[s], a_lo[s], True, False)

                def gate_z(s, step, it):
                    for m in range(CH):
                        wait(pe, r_ready, s, it, CH * step + m + 1)
                        product(RZ[s], "diff", m, a_hi[s], a_lo[s], False, True).then_inc(z_done[s].sem, 1)

                def candidate(s, step, it):
                    wait(pe, rh_lo_ready, s, it, CH * (step + 1))
                    for m in range(CH):
                        product(HV[s], "u5", m, rh_hi[s], rh_lo[s], False, True).then_inc(hv_done[s].sem, 1)

                def turn_h(s, step, it):
                    wait(pe, h_new, s, it, CH * (step + 1))
                    for b in range(2):
                        for t in range(2):
                            for k in range(CH):
                                q = slice((2 * b + t) * P, (2 * b + t + 1) * P)
                                at = t * DIM + k * P
                                ins = nc.tensor.transpose(RZ[s][:, b, at:at + P], h[s][:, k, q], p.ident[:, :])
                        ins.then_inc(tok_done[s].sem, 1)

                def front(it):
                    turn_x(A, it)
                    aggregate(A, 0, it)

                def mid(it):
                    for step in range(STEPS):
                        gates_from_a(A, step, it)
                        turn_h(B, step - 1, it) if step else turn_x(B, it)
                        gate_z(A, step, it)
                        candidate(A, step, it)
                        aggregate(B, step, it)
                        gates_from_a(B, step, it)
                        turn_h(A, step, it)
                        gate_z(B, step, it)
                        candidate(B, step, it)
                        if step < STEPS - 1:
                            aggregate(A, step + 1, it)

                staged(pe, (NOW, mid), (NEXT, front), (NOW, lambda it: turn_h(B, STEPS - 1, it)))

            @block.scalar
            def _(act):
                def take_x(s, it):
                    for k in range(CH):
                        wait(act, x_turned, s, it, k + 1)
                        nc.scalar.activation(h[s][:, k, :], RZ[s][:, k, :], ACT.Copy)
                        nc.scalar.activation(h_hi[s][:, k, :], RZ[s][:, k, :], ACT.Copy).then_inc(h_hi_ready[s].sem, 1)

                def a_high(s, step, it):
                    for k in range(CH):
                        wait(act, adj_done, s, it, CH * step + k + 1)
                        nc.scalar.activation(a_hi[s][:, k, :], HV[s][:, k, :], ACT.Copy).then_inc(a_hi_ready[s].sem, 1)

                def gate_r(s, step, it):
                    for m in range(CH):
                        wait(act, r_done, s, it, CH * step + m + 1)
                        nc.scalar.activation(r[s][:, m, :], RZ[s][:, m, :], ACT.Sigmoid,
                                             bias=biases["r"][:, m:m + 1]).then_inc(r_ready[s].sem, 1)
                    for m in range(CH):
                        wait(act, rh_ready, s, it, CH * step + m + 1)
                        nc.scalar.activation(rh_hi[s][:, m, :], r[s][:, m, :], ACT.Copy).then_inc(rh_hi_ready[s].sem, 1)

                def gate_z(s, step, it):
                    for m in range(CH):
                        wait(act, z_done, s, it, CH * step + m + 1)
                        nc.scalar.activation(RZ[s][:, m, :], RZ[s][:, m, :], ACT.Sigmoid,
                                             bias=biases["z"][:, m:m + 1]).then_inc(z_ready[s].sem, 1)

                def candidate(s, step, it):
                    for m in range(CH):
                        wait(act, hv_done, s, it, CH * step + m + 1)
                        nc.scalar.activation(HV[s][:, m, :], HV[s][:, m, :], ACT.Tanh,
                                             bias=biases["h"][:, m:m + 1]).then_inc(hv_ready[s].sem, 1)

                def h_high(s, step, it):
                    for m in range(CH):
                        wait(act, h_new, s, it, CH * step + m + 1)
                        nc.scalar.activation(h_hi[s][:, m, :], h[s][:, m, :], ACT.Copy).then_inc(h_hi_ready[s].sem, 1)

                def take_h(s, step, it):
                    for b in range(2):
                        wait(act, tok_done, s, it, 2 * step + b + 1)
                        nc.scalar.activation(h_tok[s][:, 2 * b:2 * b + 2, :],
                                             RZ[s][:, b, :].rearrange("p (t f) -> p t f", t=2),
                                             ACT.Copy).then_inc(tok_ready[s].sem, 1)

                def front(it):
                    take_x(A, it)
                    a_high(A, 0, it)

                def mid(it):
                    for step in range(STEPS):
                        if step:
                            h_high(B, step - 1, it)
                        gate_r(A, step, it)
                        take_h(B, step - 1, it) if step else take_x(B, it)
                        gate_z(A, step, it)
                        candidate(A, step, it)
                        a_high(B, step, it)
                        if step < STEPS - 1:
                            h_high(A, step, it)
                        gate_r(B, step, it)
                        if step < STEPS - 1:
                            take_h(A, step, it)
                        gate_z(B, step, it)
                        candidate(B, step, it)
                        if step < STEPS - 1:
                            a_high(A, step + 1, it)

                staged(act, (NOW, mid), (NEXT, front))

            @block.gpsimd
            def _(pool):
                def h_low(s, step, it):
                    for m in range(CH):
                        wait(pool, h_hi_ready, s, it, CH * step + m + 1)
                        nc.gpsimd.tensor_tensor(h_lo[s][:, m, :], h[s][:, m, :], h_hi[s][:, m, :].bitcast(F32),
                                                ALU.subtract).then_inc(h_lo_ready[s].sem, 1)

                def mid(it):
                    for step in range(STEPS):
                        h_low(B, step, it)
                        if step < STEPS - 1:
                            h_low(A, step + 1, it)

                def tail(it):
                    for s in SLOTS:
                        norm.root(pool, it, s)

                for s in SLOTS:
                    pool.sem_inc(y_ready[s].sem, 1)
                staged(pool, (NOW, mid), (NEXT, lambda it: h_low(A, 0, it)), (NOW, tail))

            @block.vector
            def _(dve):
                for s in SLOTS:
                    dve.sem_inc(x_free[s].sem, 1)

                def a_low(s, step, it):
                    for k in range(CH):
                        wait(dve, a_hi_ready, s, it, CH * step + k + 1)
                        nc.vector.tensor_tensor(a_lo[s][:, k, :], HV[s][:, k, :], a_hi[s][:, k, :].bitcast(F32),
                                                ALU.subtract).then_inc(a_lo_ready[s].sem, 1)

                def reset(s, step, it):
                    for m in range(CH):
                        wait(dve, r_ready, s, it, CH * step + m + 1)
                        nc.vector.tensor_tensor(r[s][:, m, :], r[s][:, m, :], h[s][:, m, :],
                                                ALU.mult).then_inc(rh_ready[s].sem, 1)
                    for m in range(CH):
                        wait(dve, rh_hi_ready, s, it, CH * step + m + 1)
                        nc.vector.tensor_tensor(rh_lo[s][:, m, :], r[s][:, m, :], rh_hi[s][:, m, :].bitcast(F32),
                                                ALU.subtract).then_inc(rh_lo_ready[s].sem, 1)

                def update(s, step, it):
                    for m in range(CH):
                        wait(dve, hv_ready, s, it, CH * step + m + 1)
                        ins = nc.vector.tensor_tensor(d[s][:, m, :], HV[s][:, m, :], h[s][:, m, :], ALU.subtract)
                    mid_chain.link(ins)
                    for m in range(CH):
                        wait(dve, z_ready, s, it, CH * step + m + 1)
                        ins = nc.vector.tensor_tensor(d[s][:, m, :], RZ[s][:, m, :], d[s][:, m, :], ALU.mult)
                    mid_chain.link(ins)
                    for m in range(CH):
                        nc.vector.tensor_tensor(h[s][:, m, :], h[s][:, m, :], d[s][:, m, :],
                                                ALU.add).then_inc(h_new[s].sem, 1)

                def residual(s, it):
                    wait(dve, y_ready, s, it, 0)
                    for b in range(2):
                        wait(dve, tok_done, s, it, 2 * (STEPS - 1) + b + 1)
                        nc.vector.tensor_tensor(z[s][:, 2 * b:2 * b + 2, :],
                                                RZ[s][:, b, :].rearrange("p (t f) -> p t f", t=2),
                                                x_tok[s][:, 2 * b:2 * b + 2, :], ALU.add).then_inc(x_free[s].sem, 1)

                def mid(it):
                    mid_chain.start(dve, it)
                    for step in range(STEPS):
                        if step:
                            update(B, step - 1, it)
                        reset(A, step, it)
                        a_low(B, step, it)
                        update(A, step, it)
                        reset(B, step, it)
                        if step < STEPS - 1:
                            a_low(A, step + 1, it)
                    residual(A, it)
                    update(B, STEPS - 1, it)

                def tail(it):
                    tail_chain.start(dve, it)
                    residual(B, it)
                    for s in SLOTS:
                        wait(dve, x_free, s, it, CH)
                        norm.statistics(tail_chain, s, z[s])
                    for s in SLOTS:
                        wait(dve, stored, s, it, 0)
                        norm.apply(dve, it, s, z[s], y_tok[s]).then_inc(y_ready[s].sem, 1)

                staged(dve, (NOW, mid), (NEXT, lambda it: a_low(A, 0, it)), (NOW, tail))


LAYERS = (layer0, layer1, layer2, layer3,)


def build(nc, a, out):
    with ExitStack() as stack:
        p = Program(nc, a, out, stack)
        constants(p)
        p.clear_semaphores()
        src = a["x"].rearrange("b n d -> (b n) d")
        last = len(LAYERS) - 1
        for n, layer in enumerate(LAYERS):
            dst = (out.rearrange("b n d -> (b n) d") if n == last else
                   nc.dram_tensor(f"x_after_{n}", (GRAPHS * NODES, DIM), F32, kind="Internal").ap())
            layer(p, p.view(src), p.view(dst))
            src = dst
            p.clear_semaphores()


_OUT = ((GRAPHS, NODES, DIM), "float32")


def kernel(**inputs):
    import numpy as _np
    import concourse.bacc as _bacc
    from concourse import mybir as _mybir
    from concourse.bass_utils import run_bass_kernel_spmd as _run

    nc = _bacc.Bacc("TRN2", target_bir_lowering=False, num_devices=1)
    arrays, args = {}, {}
    for name in inputs:
        a = _np.ascontiguousarray(inputs[name])
        arrays[f"in_{name}_dram"] = a
        args[name] = nc.dram_tensor(f"in_{name}_dram", a.shape, _mybir.dt.from_np(a.dtype), kind="ExternalInput").ap()
    out = nc.dram_tensor("out_0_dram", _OUT[0], _mybir.dt.from_np(_np.dtype(_OUT[1])), kind="ExternalOutput").ap()
    build(nc, args, out)
    r = _run(nc, [arrays], core_ids=[0])
    return r.results[0]["out_0_dram"]
```

```python
from contextlib import ExitStack

import concourse.bass as bass
from concourse import mybir

F32 = mybir.dt.float32
F32R = mybir.dt.float32r
BF16 = mybir.dt.bfloat16
ALU = mybir.AluOpType
ACT = mybir.ActivationFunctionType
AX = mybir.AxisListType

GRAPHS, NODES, DIM = 128, 64, 256
P = 128
PER_TILE = P // NODES
TILES = 4
GROUP = TILES * P
PAIRS = GRAPHS * NODES // (2 * GROUP)
CH = DIM // P
HEADS, HD = 8, 32
BANK = 512
EPS = 1e-5
SLOPE = 0.2
MASKED = -3.0e38
SLOTS = (0, 1)


class Signal:

    def __init__(self, sem, per, primed=0):
        self.sem, self.per, self.primed = sem, per, primed

    def at(self, it, n):
        return it * self.per + (n + self.primed)


class Chain:

    def __init__(self, sem, per):
        self.sem, self.per, self.n = sem, per, 0

    def start(self, eng, it):
        assert self.n in (0, self.per), (self.sem, self.n)
        self.eng, self.it, self.n = eng, it, 0

    def link(self, ins):
        self.n += 1
        ins.then_inc(self.sem, 1)
        self.eng.wait_ge(self.sem, self.it * self.per + self.n)


NOW, NEXT, LATER = 0, 1, 2


def staged(eng, *parts, before_last=None):
    depth = max(NEXT, *(ahead for ahead, _ in parts))

    def peeled(steps):
        for it in steps:
            for ahead, part in parts:
                if 0 <= it + ahead < PAIRS:
                    part(it + ahead)

    peeled(range(-depth, 0))
    with eng.Fori(0, PAIRS - depth) as it:
        for ahead, part in parts:
            part(it + ahead if ahead else it)
    peeled(range(PAIRS - depth, PAIRS - 1))
    if before_last:
        before_last()
    peeled(range(PAIRS - 1, PAIRS))


class Program:
    def __init__(self, nc, a, out, stack):
        self.nc, self.a, self.out, self.stack = nc, a, out, stack
        self.taken = []
        self.ps = [stack.enter_context(nc.psum_tensor(f"banks{s}", [P, TILES, BANK], F32)) for s in SLOTS]
        sb = self.sb
        self.ident = sb("ident", [P, P])
        self.ident_bf = sb("ident_bf", [P, P], BF16)
        self.adj_t = sb("adj_t", [P, P])
        self.adj2 = sb("adj2", [P, NODES])
        self.mask_bias = sb("mask_bias", [P, NODES], BF16)
        self.nan_rows = sb("nan_rows", [P, 1])
        self.same_graph = sb("same_graph", [P, P])
        self.ident2 = sb("ident2", [P, NODES])
        self.eps = sb("eps", [P, TILES])
        self.minus_half = sb("minus_half", [P, TILES])
        self.minus_one = sb("minus_one", [P, 1])
        self.const_ready = self.sem("const_ready")

    def sb(self, name, shape, dt=F32, stack=None):
        return (stack or self.stack).enter_context(self.nc.sbuf_tensor(name, shape, dt))

    def sem(self, name):
        self.taken.append(self.nc.alloc_semaphore(name=name))
        return self.taken[-1]

    def clear_semaphores(self):
        self.nc.all_engine_barrier()
        self.nc.clear_and_free_semaphores(self.taken)
        self.nc.all_engine_barrier()
        self.taken = []

    def signals(self, name, per, primed=0):
        return [Signal(self.sem(f"{name}{s}"), per, primed) for s in SLOTS]

    def view(self, x):
        return x.rearrange("(i s t p) d -> i s p t d", s=2, t=TILES, p=P)


def matmul3(nc, out, w, x, first, last):
    nc.tensor.matmul(out, w[0], x[0], start=first, stop=False, skip_group_check=True)
    nc.tensor.matmul(out, w[0], x[1], start=False, stop=False, skip_group_check=True)
    return nc.tensor.matmul(out, w[1], x[0], start=False, stop=last, skip_group_check=True)


def constants(p, block, own):
    nc = p.nc
    adj_blk = p.sb("adj_blk", [P, P], stack=own)
    hits = p.sb("hits", [P, NODES], stack=own)
    count = p.sb("count", [P, 1], stack=own)
    zeroed, made, loaded, turned, chain = (p.sem(n) for n in (
        "c_zeroed", "c_made", "c_loaded", "c_turned", "c_chain"))

    @block.gpsimd
    def _(pool):
        nc.gpsimd.memset(p.ident[:, :], 0.0).then_inc(zeroed, 1)
        nc.gpsimd.memset(adj_blk[:, :], 0.0).then_inc(zeroed, 1)
        nc.gpsimd.memset(p.same_graph[:, :], 0.0).then_inc(zeroed, 1)
        nc.gpsimd.memset(p.eps[:, :], EPS)
        nc.gpsimd.memset(p.minus_half[:, :], -0.5)
        nc.gpsimd.memset(p.minus_one[:, :], -1.0).then_inc(zeroed, 1)
        pool.wait_ge(zeroed, 3)
        nc.gpsimd.affine_select(out=p.ident[:, :], in_=p.ident[:, :], compare_op=ALU.not_equal, fill=1.0,
                                base=0, pattern=[[-1, P]], channel_multiplier=1).then_inc(made, 1)

    @block.sync
    def _(sp):
        p.stream.prime(sp)
        sp.wait_ge(zeroed, 3)
        for b in range(PER_TILE):
            q = slice(b * NODES, (b + 1) * NODES)
            sp.dma_start(adj_blk[q, q], p.a["adj"]).then_inc(loaded, 16)
            sp.dma_start(p.adj2[q, :], p.a["adj"]).then_inc(loaded, 16)
                

    @block.tensor
    def _(pe):
        pe.wait_ge(made, 1)
        pe.wait_ge(loaded, 64)
        nc.tensor.transpose(p.ps[0][:, 0, 0:P], adj_blk[:, :], p.ident[:, :]).then_inc(turned, 1)

    @block.vector
    def _(dve):
        links = Chain(chain, 7)
        links.start(dve, 0)
        dve.wait_ge(loaded, 64)
        dve.wait_ge(made, 1)
        for b in range(PER_TILE):
            q = slice(b * NODES, (b + 1) * NODES)
            nc.vector.memset(p.same_graph[q, q], 1.0)
        nc.vector.tensor_copy(p.ident_bf[:, :], p.ident[:, :])
        nc.vector.tensor_tensor(p.ident2[:, :], p.ident[:, 0:NODES], p.ident[:, NODES:P], ALU.add)
        nc.vector.tensor_scalar(p.mask_bias[:, :], p.adj2[:, :], 0.0, MASKED, ALU.is_equal, ALU.mult)
        links.link(nc.vector.tensor_scalar(hits[:, :], p.adj2[:, :], 0.0, None, ALU.not_equal))
        links.link(nc.vector.reduce_sum(count[:, :], hits[:, :], AX.X))
        links.link(nc.vector.tensor_scalar(count[:, :], count[:, :], 1.0, None, ALU.min))
        links.link(nc.vector.reciprocal(count[:, :], count[:, :]))
        links.link(nc.vector.tensor_scalar(p.nan_rows[:, :], count[:, :], 0.0, None, ALU.mult))
        dve.wait_ge(turned, 1)
        links.link(nc.vector.tensor_copy(p.adj_t[:, :], p.ps[0][:, 0, 0:P]))
        links.link(nc.vector.tensor_copy(hits[:, 0:1], p.nan_rows[:, :]))
        nc.vector.memset(count[:, :], 0.0).then_inc(p.const_ready, 1)


class Norm:

    LINKS = 2

    def __init__(self, p, name, stack):
        self.p = p
        self.carrier = p.sb(f"{name}_carrier", [P, 1], stack=stack)
        self.stats = [p.sb(f"{name}_stats{s}", [P, TILES, 6], stack=stack) for s in SLOTS]
        self.mv = [p.sb(f"{name}_mv{s}", [P, TILES, 2], stack=stack) for s in SLOTS]
        self.rstd = [p.sb(f"{name}_rstd{s}", [P, TILES], stack=stack) for s in SLOTS]
        self.var_ready = p.signals(f"{name}_var_ready", 1)
        self.eps_added = p.signals(f"{name}_eps_added", 1)
        self.rstd_ready = p.signals(f"{name}_rstd_ready", 1)
        self.offset = [p.sb(f"{name}_offset{s}", [P, TILES], stack=stack) for s in SLOTS]
        self.offset_ready = p.signals(f"{name}_offset_ready", 1)

    def statistics(self, links, s, z):
        nc = self.p.nc
        for t in range(TILES):
            ins = nc.vector.bn_stats(self.stats[s][:, t, :], z[:, t, :])
        links.link(ins)
        nc.vector.memset(self.carrier[:, :], 0.0)
        for t in range(TILES):
            ins = nc.vector.bn_aggr(self.mv[s][:, t, :], self.stats[s][:, t, :])
        ins.then_inc(self.var_ready[s].sem, 1)

    def root(self, pool, it, s):
        nc = self.p.nc
        pool.wait_ge(self.var_ready[s].sem, self.var_ready[s].at(it, 1))
        nc.gpsimd.tensor_tensor(self.rstd[s][:, :], self.mv[s][:, :, 1], self.p.eps[:, :],
                                ALU.add).then_inc(self.eps_added[s].sem, 1)
        pool.wait_ge(self.eps_added[s].sem, self.eps_added[s].at(it, 1))
        nc.gpsimd.tensor_tensor(self.rstd[s][:, :], self.rstd[s][:, :], self.p.minus_half[:, :],
                                ALU.pow).then_inc(self.rstd_ready[s].sem, 1)

    def apply(self, dve, it, s, z, y):
        nc = self.p.nc
        dve.wait_ge(self.rstd_ready[s].sem, self.rstd_ready[s].at(it, 1))
        for t in range(TILES):
            ins = nc.vector.tensor_scalar(y[:, t, :], z[:, t, :], self.mv[s][:, t, 0:1], self.rstd[s][:, t:t + 1],
                                          ALU.subtract, ALU.mult)
        return ins

    def take_offset(self, dve, it, s):
        dve.wait_ge(self.rstd_ready[s].sem, self.rstd_ready[s].at(it, 1))
        self.p.nc.vector.scalar_tensor_tensor(self.offset[s][:, :], self.mv[s][:, :, 0], -1.0, self.rstd[s][:, :],
                                              ALU.mult, ALU.mult).then_inc(self.offset_ready[s].sem, 1)

    def apply_scalar(self, act, it, s, z, y):
        act.wait_ge(self.offset_ready[s].sem, self.offset_ready[s].at(it, 1))
        for t in range(TILES):
            ins = self.p.nc.scalar.activation(y[:, t, :], z[:, t, :], ACT.Identity, scale=self.rstd[s][:, t:t + 1],
                                              bias=self.offset[s][:, t:t + 1])
        return ins


class Stream:

    def __init__(self, p):
        self.x_tok = [p.sb(f"x_tok{s}", [P, TILES, DIM]) for s in SLOTS]
        self.y_tok = [p.sb(f"y_tok{s}", [P, TILES, DIM]) for s in SLOTS]
        alloc = p.nc.alloc_semaphore
        self.sems = {n: [alloc(name=f"{n}{s}") for s in SLOTS] for n in ("loaded", "x_free", "y_ready", "stored")}
        self.raised = {"loaded": 0, "x_free": 1, "y_ready": 1, "stored": 16}

    def prime(self, sp):
        for n, value in self.raised.items():
            for s in SLOTS:
                if value:
                    sp.sem_inc(self.sems[n][s], value)

    def open(self, src, dst, x_readers=1):
        self.src, self.dst = src, dst
        per = {"loaded": 16, "x_free": x_readers, "y_ready": 1, "stored": 16}
        signals = []
        for n in ("loaded", "x_free", "y_ready", "stored"):
            signals.append([Signal(self.sems[n][s], per[n], self.raised[n]) for s in SLOTS])
            self.raised[n] += per[n] * PAIRS
        self.loaded, self.x_free, self.y_ready, self.stored = signals
        return signals

    def load(self, sp, s, it):
        sp.wait_ge(self.x_free[s].sem, self.x_free[s].at(it, 0))
        sp.dma_start(self.x_tok[s][:, :, :], self.src[it][s]).then_inc(self.loaded[s].sem, 16)

    def store(self, sp, s, it):
        sp.wait_ge(self.y_ready[s].sem, self.y_ready[s].at(it, 1))
        sp.dma_start(self.dst[it][s], self.y_tok[s][:, :, :]).then_inc(self.stored[s].sem, 16)

    def load_next_first(self, sp):
        for s in SLOTS:
            sp.wait_ge(self.stored[s].sem, self.stored[s].at(1, 0))
            sp.wait_ge(self.x_free[s].sem, self.x_free[s].at(PAIRS, 0))
            sp.dma_start(self.x_tok[s][:, :, :], self.dst[0][s]).then_inc(self.loaded[s].sem, 16)

    def all_stored(self, sp, it=0):
        for s in SLOTS:
            sp.wait_ge(self.stored[s].sem, self.stored[s].at(it, 0))

    def run(self, sp, first=False, last=False, lead=LATER):
        def load(s):
            def part(it):
                if first or not (isinstance(it, int) and it == 0):
                    self.load(sp, s, it)
            return lead, part

        def store(s):
            return NOW, lambda it: self.store(sp, s, it)

        self.all_stored(sp)
        before_last = None if last else lambda: self.load_next_first(sp)
        if lead == LATER:
            staged(sp, load(0), store(0), load(1), store(1), before_last=before_last)
        else:
            staged(sp, load(0), load(1), store(0), store(1), before_last=before_last)


WX = DIM + 2


def load_weights(p, block, own):
    raw = {"l0_w": p.sb("l0_w", [P, CH, WX], stack=own), "l0_a": p.sb("l0_a", [P, 2, DIM], stack=own),
           "l0_beta": p.sb("l0_beta", [P, 1], stack=own),
           "l1_w": p.sb("l1_w", [P, CH, DIM], stack=own), "l1_bias": p.sb("l1_bias", [P, DIM], stack=own)}
    p.weights.room(p, own)
    for layer in range(4):
        raw[f"l{layer}_loaded"] = p.sem(f"l{layer}_w_loaded")

    def load(eng, layer, tile, source, **how):
        eng.dma_start(tile, source, **how).then_inc(raw[f"l{layer}_loaded"], 16)

    def rows_on_partitions(name):
        return p.a[name].rearrange("(k p) f -> p k f", p=P)

    def on_all_partitions(name, width):
        return p.a[name].rearrange("(o f) -> o f", o=1).to_broadcast([P, width])

    @block.scalar
    def _(act):
        load(act, 0, raw["l0_w"][:, :, 0:DIM], rows_on_partitions("L0_gnn_W"))
        load(act, 0, raw["l0_a"][:, :, :],
             p.a["L0_gnn_a"].rearrange("(j f) o -> o j f", j=2).to_broadcast([P, 2, DIM]))
        load(act, 0, raw["l0_beta"][:, :], on_all_partitions("L0_gnn_beta", 1))

    @block.gpsimd
    def _(pool):
        for n in ("w3", "w4", "w5", "u3", "u5"):
            load(pool, 3, p.gate_raw[n][:, :, :], rows_on_partitions(f"L3_gnn_{n}_w"))
        for i, n in enumerate(("w3", "w4", "w5", "u3", "u5")):
            load(pool, 3, p.bias_raw[:, i, :], p.a[f"L3_gnn_{n}_b"].rearrange("(m p) -> p m", p=P),
                 allow_slow_non_contiguous=True)
        load(pool, 1, raw["l1_w"][:, :, :], rows_on_partitions("L1_gnn_weight"))
        load(pool, 1, raw["l1_bias"][:, :], on_all_partitions("L1_gnn_bias", DIM))
        load(pool, 2, p.qkv_raw[:, :, :], rows_on_partitions("L2_gnn_w_qkv"))
        load(pool, 2, p.proj_raw[:, :, :], rows_on_partitions("L2_gnn_w_proj"))
        for n, row in p.rows.items():
            load(pool, 2, row[:, :], on_all_partitions(f"L2_gnn_{n}", DIM))

    return raw


GATES = ("u3", "w4s", "w5s", "diff", "u5")


class Weights:

    def __init__(self, p):
        split = lambda name, width: [p.sb(f"{name}_{q}", [P, CH, width], F32R) for q in ("hi", "lo")]
        self.qkv, self.proj = split("qkv", 3 * DIM), split("proj", DIM)
        self.gates = {n: split(n, DIM) for n in GATES}
        self.biases = {n: p.sb(f"bias_{n}", [P, CH]) for n in ("z", "r", "h")}
        p.rows = {n: p.sb(n, [P, DIM]) for n in ("b_proj", "ln_gamma", "ln_beta")}

    def room(self, p, own):
        p.qkv_raw = p.sb("qkv_raw", [P, CH, 3 * DIM], stack=own)
        p.proj_raw = p.sb("proj_raw", [P, CH, DIM], stack=own)
        p.gate_raw = {n: p.sb(f"{n}_raw", [P, CH, 2 * DIM if n[0] == "w" else DIM], stack=own)
                      for n in ("w3", "w4", "w5", "u3", "u5")}
        p.bias_raw = p.sb("bias_raw", [P, 5, CH], stack=own)


def gate_sums(p, block, raw):
    nc = p.nc
    wide = p.gate_raw
    halves = {n: wide[n][:, :, 0:DIM] for n in ("w3", "w4", "w5")}
    diff = wide["w3"][:, :, DIM:2 * DIM]
    p.natural = {"u3": wide["u3"], "w4s": halves["w4"], "w5s": halves["w5"], "diff": diff, "u5": wide["u5"]}
    summed, p.gates_natural = p.sem("w_summed"), p.sem("w_natural")

    @block.gpsimd
    def _(pool):
        pool.wait_ge(raw["l3_loaded"], 160)
        for n in ("w3", "w4", "w5"):
            nc.gpsimd.tensor_tensor(halves[n], halves[n], wide[n][:, :, DIM:2 * DIM], ALU.add).then_inc(summed, 1)
        pool.wait_ge(summed, 3)
        nc.gpsimd.tensor_tensor(diff, halves["w3"], halves["w4"], ALU.subtract).then_inc(p.gates_natural, 1)
        for n, (i, j) in (("z", (0, 3)), ("r", (1, 3)), ("h", (2, 4))):
            nc.gpsimd.tensor_tensor(p.weights.biases[n][:, :], p.bias_raw[:, i, :], p.bias_raw[:, j, :], ALU.add)


def split_gates(p, block):
    nc = p.nc
    bank = {n: p.ps[i // TILES][:, i % TILES, :].rearrange("p (k o) -> p k o", k=CH) for i, n in enumerate(GATES)}
    turned, high, low = (p.sem(f"w_{n}") for n in ("turned", "high", "low"))
    p.split_low = low

    @block.tensor
    def _(pe):
        pe.wait_ge(p.gates_natural, 1)
        for n in GATES:
            for k in range(CH):
                for m in range(CH):
                    ins = nc.tensor.transpose(bank[n][:, k, m * P:(m + 1) * P],
                                              p.natural[n][:, m, k * P:(k + 1) * P], p.ident[:, :])
            ins.then_inc(turned, 1)

    @block.scalar
    def _(act):
        for i, n in enumerate(GATES):
            act.wait_ge(turned, i + 1)
            nc.scalar.activation(p.weights.gates[n][0][:, :, :], bank[n], ACT.Copy).then_inc(high, 1)

    @block.vector
    def _(dve):
        for i, n in enumerate(GATES):
            dve.wait_ge(high, i + 1)
            nc.vector.tensor_tensor(p.weights.gates[n][1][:, :, :], bank[n],
                                    p.weights.gates[n][0][:, :, :].bitcast(F32), ALU.subtract).then_inc(low, 1)


def split_attention(p, block, raw):
    nc = p.nc
    high, low = p.sem("attention_high"), p.sem("attention_low")
    pairs = ((p.weights.qkv, p.qkv_raw), (p.weights.proj, p.proj_raw))

    @block.scalar
    def _(act):
        act.wait_ge(raw["l2_loaded"], 80)
        for parts, whole in pairs:
            nc.scalar.activation(parts[0][:, :, :], whole[:, :, :], ACT.Copy).then_inc(high, 1)

    @block.vector
    def _(dve):
        for i, (parts, whole) in enumerate(pairs):
            dve.wait_ge(high, i + 1)
            nc.vector.tensor_tensor(parts[1][:, :, :], whole[:, :, :], parts[0][:, :, :].bitcast(F32),
                                    ALU.subtract).then_inc(low, 1)


def layer0(p, block, own, raw, src, dst):
    nc = p.nc
    w, a_row, beta, w_loaded = raw["l0_w"], raw["l0_a"], raw["l0_beta"], raw["l0_loaded"]
    wa = p.sb("l0_wa", [P, CH, DIM], stack=own)
    w_parts = [p.sb(f"l0_w{n}", [P, CH, WX], F32R, stack=own) for n in ("hi", "lo")]
    two = lambda name, shape, dt=F32: [p.sb(f"l0_{name}{s}", shape, dt, stack=own) for s in SLOTS]
    x_tok, y_tok = p.stream.x_tok, p.stream.y_tok
    x_hi, x_lo = p.operand
    h = two("h", [P, TILES, WX])
    s2_diag = two("s2", [P, TILES, NODES])
    e = two("e", [P, TILES, NODES])
    small = two("small", [P, 3, TILES])
    att = two("att", [P, TILES, P])
    att_t = two("att_t", [P, TILES, P])
    v = two("v", [P, TILES, DIM])
    neg = two("neg", [P, TILES, DIM])
    res = two("res", [P, TILES, DIM])
    norm = Norm(p, "l0", own)

    w_chain, w_hi, w_ready, att_zeroed = (p.sem(f"l0_{n}") for n in (
        "w_chain", "w_hi", "w_ready", "att_zeroed"))
    loaded, x_free, y_ready, stored = p.stream.open(src, dst)
    turned = p.signals("l0_turned", CH)
    hi_ready = p.signals("l0_hi_ready", CH)
    lo_ready = p.signals("l0_lo_ready", CH)
    h_done = p.signals("l0_h_done", TILES, 1)
    h_ready = p.signals("l0_h_ready", TILES)
    spread = p.signals("l0_spread", 1)
    s2_done = p.signals("l0_s2_done", 1)
    shifted = p.signals("l0_shifted", 1)
    exp_done = p.signals("l0_exp_done", 1)
    att_ready = p.signals("l0_att_ready", 1)
    att_turned = p.signals("l0_att_turned", 1)
    att_t_ready = p.signals("l0_att_t_ready", 1)
    hp_done = p.signals("l0_hp_done", 2)
    v_ready = p.signals("l0_v_ready", 2, 1)
    relu_done = p.signals("l0_relu_done", 2)
    elu_ready = p.signals("l0_elu_ready", 2)
    res_ready = p.signals("l0_res_ready", 2)
    z_ready = p.signals("l0_z_ready", 2, 1)
    score_chain, share_chain, stat_chain = (
        [Chain(p.sem(f"l0_{n}_chain{s}"), per) for s in SLOTS] for n, per in (("score", 4), ("share", 2), ("stat", 1)))
    A, B = SLOTS

    def wait(eng, signal, s, it, n):
        eng.wait_ge(signal[s].sem, signal[s].at(it, n))

    @block.sync
    def _(sp):
        p.stream.run(sp, first=True)

    @block.gpsimd
    def _(pool):
        for s in SLOTS:
            nc.gpsimd.memset(att[s][:, :, :], 0.0).then_inc(att_zeroed, 1)
        pool.wait_ge(p.const_ready, 1)

        def spread_s2(s, it):
            wait(pool, h_ready, s, it, TILES)
            nc.gpsimd.tensor_tensor(s2_diag[s][:, :, :], p.ident2[:, :].unsqueeze(1).to_broadcast([P, TILES, NODES]),
                                    h[s][:, :, DIM + 1:DIM + 2].to_broadcast([P, TILES, NODES]),
                                    ALU.mult).then_inc(spread[s].sem, 1)

        def less_one(s, it):
            wait(pool, turned, s, it, CH)
            wait(pool, z_ready, s, it, 0)
            nc.gpsimd.tensor_tensor(res[s][:, :, :], x_tok[s][:, :, :],
                                    p.minus_one[:, :].unsqueeze(1).to_broadcast([P, TILES, DIM]),
                                    ALU.add).then_inc(x_free[s].sem, 1)

        def add_exp(s, it):
            wait(pool, x_free, s, it, 1)
            for b in range(2):
                two_tiles = res[s][:, 2 * b:2 * b + 2, :]
                wait(pool, elu_ready, s, it, b + 1)
                nc.gpsimd.tensor_tensor(two_tiles, two_tiles, neg[s][:, 2 * b:2 * b + 2, :],
                                        ALU.add).then_inc(res_ready[s].sem, 1)

        staged(pool,
               (NEXT, lambda it: spread_s2(A, it)),
               (NEXT, lambda it: less_one(A, it)),
               (NOW, lambda it: norm.root(pool, it, A)),
               (NOW, lambda it: add_exp(B, it)),
               (NEXT, lambda it: spread_s2(B, it)),
               (NEXT, lambda it: less_one(B, it)),
               (NOW, lambda it: norm.root(pool, it, B)),
               (NEXT, lambda it: add_exp(A, it)))

    @block.tensor
    def _(pe):
        pe.wait_ge(p.const_ready, 1)

        def turn(s, it):
            wait(pe, loaded, s, it, 16)
            for k in range(CH):
                for t in range(TILES):
                    ins = nc.tensor.transpose(p.ps[s][:, k, t * P:(t + 1) * P],
                                              x_tok[s][:, t, k * P:(k + 1) * P], p.ident[:, :])
                ins.then_inc(turned[s].sem, 1)

        def project(s, it):
            pe.wait_ge(w_ready, 1)
            wait(pe, lo_ready, s, it, CH)
            wait(pe, v_ready, s, it, 0)
            for t in range(TILES):
                for k in range(CH):
                    q = slice(t * P, (t + 1) * P)
                    ins = matmul3(nc, p.ps[s][:, t, 0:WX], (x_hi[s][:, k, q], x_lo[s][:, k, q]),
                                  (w_parts[0][:, k, :], w_parts[1][:, k, :]), k == 0, k == CH - 1)
                ins.then_inc(h_done[s].sem, 1)

        def spread_s2(s, it):
            wait(pe, spread, s, it, 1)
            nc.tensor.matmul(p.ps[s][:, 0, 0:TILES * NODES], p.same_graph[:, :],
                             s2_diag[s][:, :, :].rearrange("p t j -> p (t j)"),
                             start=True, stop=True).then_inc(s2_done[s].sem, 1)

        def attend(s, it):
            wait(pe, att_ready, s, it, 1)
            for t in range(TILES):
                ins = nc.tensor.transpose(p.ps[s][:, 1, t * P:(t + 1) * P], att[s][:, t, :], p.ident[:, :])
            ins.then_inc(att_turned[s].sem, 1)
            wait(pe, att_t_ready, s, it, 1)
            for t in range(TILES):
                ins = nc.tensor.matmul(p.ps[s][:, 2 + t // 2, (t % 2) * DIM:(t % 2 + 1) * DIM],
                                       att_t[s][:, t, :], h[s][:, t, 0:DIM], start=True, stop=True)
                if t % 2:
                    ins.then_inc(hp_done[s].sem, 1)

        for s in SLOTS:
            pe.sem_inc(h_done[s].sem, 1)
        staged(pe,
               (NEXT, lambda it: turn(A, it)),
               (NOW, lambda it: spread_s2(B, it)),
               (NEXT, lambda it: project(A, it)),
               (NOW, lambda it: attend(B, it)),
               (NEXT, lambda it: turn(B, it)),
               (NEXT, lambda it: spread_s2(A, it)),
               (NEXT, lambda it: project(B, it)),
               (NEXT, lambda it: attend(A, it)))

    @block.scalar
    def _(act):
        act.wait_ge(w_chain, 4)
        nc.scalar.activation(w_parts[0][:, :, :], w[:, :, :], ACT.Copy).then_inc(w_hi, 1)

        def high(s, it):
            wait(act, h_done, s, it, 0)
            for k in range(CH):
                wait(act, turned, s, it, k + 1)
                nc.scalar.activation(x_hi[s][:, k, :], p.ps[s][:, k, :], ACT.Copy).then_inc(hi_ready[s].sem, 1)

        def take_h(s, it, tiles):
            for t in tiles:
                wait(act, h_done, s, it, t + 1)
                nc.scalar.activation(h[s][:, t, :], p.ps[s][:, t, 0:WX], ACT.Copy).then_inc(h_ready[s].sem, 1)

        def exp(s, it):
            wait(act, shifted, s, it, 1)
            nc.scalar.activation(e[s][:, :, :], e[s][:, :, :], ACT.Exp).then_inc(exp_done[s].sem, 1)

        def take_att(s, it):
            wait(act, att_turned, s, it, 1)
            nc.scalar.activation(att_t[s][:, :, :], p.ps[s][:, 1, :], ACT.Copy).then_inc(att_t_ready[s].sem, 1)

        def exp_negative(s, it):
            for b in range(2):
                wait(act, v_ready, s, it, b + 1)
                nc.scalar.activation(neg[s][:, 2 * b:2 * b + 2, :], v[s][:, 2 * b:2 * b + 2, :], ACT.Relu,
                                     scale=-1.0).then_inc(relu_done[s].sem, 1)
                wait(act, relu_done, s, it, b + 1)
                nc.scalar.activation(neg[s][:, 2 * b:2 * b + 2, :], neg[s][:, 2 * b:2 * b + 2, :], ACT.Exp,
                                     scale=-1.0).then_inc(elu_ready[s].sem, 1)

        def normalise(s, it):
            wait(act, stored, s, it, 0)
            norm.apply_scalar(act, it, s, v[s], y_tok[s]).then_inc(y_ready[s].sem, 1)

        def take_h_b_exp_a(it):
            take_h(B, it, range(0, 2))
            exp(A, it)
            take_h(B, it, range(2, TILES))

        staged(act,
               (NEXT, lambda it: take_h(A, it, range(TILES))),
               (NOW, lambda it: take_att(B, it)),
               (NOW, lambda it: exp_negative(B, it)),
               (NEXT, lambda it: high(B, it)),
               (NOW, lambda it: normalise(A, it)),
               (NEXT, take_h_b_exp_a),
               (NEXT, lambda it: take_att(A, it)),
               (LATER, lambda it: high(A, it)),
               (NEXT, lambda it: exp_negative(A, it)),
               (NEXT, lambda it: exp(B, it)),
               (NOW, lambda it: normalise(B, it)))

    @block.vector
    def _(dve):
        links = Chain(w_chain, 4)
        links.start(dve, 0)
        dve.wait_ge(w_loaded, 48)
        for j in range(2):
            links.link(nc.vector.tensor_tensor(wa[:, :, :], w[:, :, 0:DIM],
                                               a_row[:, j, :].unsqueeze(1).to_broadcast([P, CH, DIM]), ALU.mult))
            links.link(nc.vector.tensor_reduce(w[:, :, DIM + j:DIM + j + 1], wa[:, :, :], AX.X, ALU.add))
        dve.wait_ge(w_hi, 1)
        nc.vector.tensor_tensor(w_parts[1][:, :, :], w[:, :, :], w_parts[0][:, :, :].bitcast(F32),
                                ALU.subtract).then_inc(w_ready, 1)
        for s in SLOTS:
            dve.sem_inc(v_ready[s].sem, 1)
            dve.sem_inc(z_ready[s].sem, 1)

        def low(s, it):
            for k in range(CH):
                wait(dve, hi_ready, s, it, k + 1)
                nc.vector.tensor_tensor(x_lo[s][:, k, :], p.ps[s][:, k, :], x_hi[s][:, k, :].bitcast(F32),
                                        ALU.subtract).then_inc(lo_ready[s].sem, 1)

        def scores(s, it):
            score_chain[s].start(dve, it)
            link = score_chain[s].link
            mx = small[s][:, 0, :]
            wait(dve, s2_done, s, it, 1)
            ps2 = p.ps[s][:, 0, 0:TILES * NODES].rearrange("p (t j) -> p t j", t=TILES)
            link(nc.vector.tensor_tensor(e[s][:, :, :], ps2,
                                         h[s][:, :, DIM:DIM + 1].to_broadcast([P, TILES, NODES]), ALU.add))
            link(nc.vector.scalar_tensor_tensor(e[s][:, :, :], e[s][:, :, :], SLOPE, e[s][:, :, :],
                                                ALU.mult, ALU.max))
            link(nc.vector.tensor_tensor(e[s][:, :, :], e[s][:, :, :],
                                         p.adj2[:, :].unsqueeze(1).to_broadcast([P, TILES, NODES]), ALU.mult))
            link(nc.vector.tensor_reduce(mx, e[s][:, :, :], AX.X, ALU.max))
            nc.vector.tensor_tensor(e[s][:, :, :], e[s][:, :, :], mx.unsqueeze(2).to_broadcast(
                [P, TILES, NODES]), ALU.subtract).then_inc(shifted[s].sem, 1)

        def share(s, it):
            share_chain[s].start(dve, it)
            link = share_chain[s].link
            total, inv = small[s][:, 1, :], small[s][:, 2, :]
            wait(dve, exp_done, s, it, 1)
            link(nc.vector.tensor_reduce(total, e[s][:, :, :], AX.X, ALU.add))
            link(nc.vector.reciprocal(inv, total))
            dve.wait_ge(att_zeroed, 2)
            for b in range(PER_TILE):
                q = slice(b * NODES, (b + 1) * NODES)
                ins = nc.vector.tensor_tensor(att[s][q, :, q], e[s][q, :, :], inv[q].unsqueeze(2).to_broadcast(
                    [NODES, TILES, NODES]), ALU.mult)
            ins.then_inc(att_ready[s].sem, 1)

        def add_h(s, it):
            wait(dve, y_ready, s, it, 0)
            for b in range(2):
                wait(dve, hp_done, s, it, b + 1)
                ps = p.ps[s][:, 2 + b, :].rearrange("p (t f) -> p t f", t=2)
                nc.vector.scalar_tensor_tensor(v[s][:, 2 * b:2 * b + 2, :], h[s][:, 2 * b:2 * b + 2, 0:DIM],
                                               beta[:, :], ps, ALU.mult, ALU.add).then_inc(v_ready[s].sem, 1)

        def residual(s, it):
            stat_chain[s].start(dve, it)
            for b in range(2):
                q = slice(2 * b, 2 * b + 2)
                wait(dve, res_ready, s, it, b + 1)
                nc.vector.scalar_tensor_tensor(v[s][:, q, :], v[s][:, q, :], 0.0, res[s][:, q, :],
                                               ALU.max, ALU.add).then_inc(z_ready[s].sem, 1)
            wait(dve, z_ready, s, it, 2)
            norm.statistics(stat_chain[s], s, v[s])

        staged(dve,
               (NOW, lambda it: scores(B, it)),
               (NOW, lambda it: share(B, it)),
               (NOW, lambda it: residual(A, it)),
               (NOW, lambda it: add_h(B, it)),
               (NOW, lambda it: norm.take_offset(dve, it, A)),
               (NEXT, lambda it: low(B, it)),
               (NEXT, lambda it: scores(A, it)),
               (NEXT, lambda it: share(A, it)),
               (NOW, lambda it: residual(B, it)),
               (NEXT, lambda it: add_h(A, it)),
               (LATER, lambda it: low(A, it)),
               (NOW, lambda it: norm.take_offset(dve, it, B)))


def layer1(p, block, own, raw, src, dst):
    nc = p.nc
    w, bias, w_loaded = raw["l1_w"], raw["l1_bias"], raw["l1_loaded"]
    w_parts = [p.sb(f"l1_w{n}", [P, CH, DIM], F32R, stack=own) for n in ("hi", "lo")]
    two = lambda name, shape, dt=F32: [p.sb(f"l1_{name}{s}", shape, dt, stack=own) for s in SLOTS]
    x_tok, y_tok = p.stream.x_tok, p.stream.y_tok
    a_hi, a_lo = p.operand
    res = two("res", [P, TILES, DIM])
    z = two("z", [P, TILES, DIM])
    norm = Norm(p, "l1", own)

    w_hi, w_ready = (p.sem(f"l1_{n}") for n in ("w_hi", "w_ready"))
    loaded, x_free, y_ready, stored = p.stream.open(src, dst)
    adj_done = p.signals("l1_adj_done", CH)
    hi_ready = p.signals("l1_hi_ready", CH)
    lo_ready = p.signals("l1_lo_ready", CH)
    out_done = p.signals("l1_out_done", 2, 1)
    z_ready = p.signals("l1_z_ready", 2, 1)
    stat_chain = [Chain(p.sem(f"l1_stat_chain{s}"), 1) for s in SLOTS]
    A, B = SLOTS

    def wait(eng, signal, s, it, n):
        eng.wait_ge(signal[s].sem, signal[s].at(it, n))

    @block.sync
    def _(sp):
        p.stream.run(sp)

    @block.gpsimd
    def _(pool):
        pool.wait_ge(w_loaded, 32)

        def add_bias(s, it):
            wait(pool, adj_done, s, it, CH)
            wait(pool, z_ready, s, it, 0)
            nc.gpsimd.tensor_tensor(res[s][:, :, :], x_tok[s][:, :, :],
                                    bias[:, :].unsqueeze(1).to_broadcast([P, TILES, DIM]),
                                    ALU.add).then_inc(x_free[s].sem, 1)

        staged(pool,
               (NOW, lambda it: norm.root(pool, it, A)),
               (NEXT, lambda it: add_bias(B, it)),
               (NOW, lambda it: norm.root(pool, it, B)),
               (LATER, lambda it: add_bias(A, it)))

    @block.tensor
    def _(pe):
        pe.wait_ge(p.split_low, len(GATES))
        for s in SLOTS:
            pe.sem_inc(out_done[s].sem, 1)

        def aggregate(s, it):
            wait(pe, loaded, s, it, 16)
            for k in range(CH):
                for t in range(TILES):
                    ins = nc.tensor.matmul(p.ps[s][:, k, t * P:(t + 1) * P],
                                           x_tok[s][:, t, k * P:(k + 1) * P], p.adj_t[:, :],
                                           start=True, stop=True)
                ins.then_inc(adj_done[s].sem, 1)

        def product(s, it):
            pe.wait_ge(w_ready, 1)
            wait(pe, lo_ready, s, it, CH)
            wait(pe, z_ready, s, it, 0)
            for t in range(TILES):
                for k in range(CH):
                    q = slice(t * P, (t + 1) * P)
                    ins = matmul3(nc, p.ps[s][:, 2 + t // 2, (t % 2) * DIM:(t % 2 + 1) * DIM],
                                  (a_hi[s][:, k, q], a_lo[s][:, k, q]),
                                  (w_parts[0][:, k, :], w_parts[1][:, k, :]), k == 0, k == CH - 1)
                if t % 2:
                    ins.then_inc(out_done[s].sem, 1)

        staged(pe,
               (NOW, lambda it: product(B, it)),
               (NEXT, lambda it: aggregate(B, it)),
               (NEXT, lambda it: product(A, it)),
               (LATER, lambda it: aggregate(A, it)))

    @block.scalar
    def _(act):
        act.wait_ge(w_loaded, 32)
        nc.scalar.activation(w_parts[0][:, :, :], w[:, :, :], ACT.Copy).then_inc(w_hi, 1)

        def high(s, it):
            wait(act, out_done, s, it, 0)
            for k in range(CH):
                wait(act, adj_done, s, it, k + 1)
                nc.scalar.activation(a_hi[s][:, k, :], p.ps[s][:, k, :], ACT.Copy).then_inc(hi_ready[s].sem, 1)

        def normalise(s, it):
            wait(act, stored, s, it, 0)
            norm.apply_scalar(act, it, s, z[s], y_tok[s]).then_inc(y_ready[s].sem, 1)

        staged(act,
               (NEXT, lambda it: high(B, it)),
               (NOW, lambda it: normalise(A, it)),
               (LATER, lambda it: high(A, it)),
               (NOW, lambda it: normalise(B, it)))

    @block.vector
    def _(dve):
        dve.wait_ge(w_loaded, 32)
        dve.wait_ge(w_hi, 1)
        nc.vector.tensor_tensor(w_parts[1][:, :, :], w[:, :, :], w_parts[0][:, :, :].bitcast(F32),
                                ALU.subtract).then_inc(w_ready, 1)
        for s in SLOTS:
            dve.sem_inc(z_ready[s].sem, 1)

        def low(s, it):
            for k in range(CH):
                wait(dve, hi_ready, s, it, k + 1)
                nc.vector.tensor_tensor(a_lo[s][:, k, :], p.ps[s][:, k, :], a_hi[s][:, k, :].bitcast(F32),
                                        ALU.subtract).then_inc(lo_ready[s].sem, 1)

        def residual(s, it):
            wait(dve, x_free, s, it, 1)
            wait(dve, y_ready, s, it, 0)
            for b in range(2):
                wait(dve, out_done, s, it, b + 1)
                nc.vector.tensor_tensor(z[s][:, 2 * b:2 * b + 2, :],
                                        p.ps[s][:, 2 + b, :].rearrange("p (t f) -> p t f", t=2),
                                        res[s][:, 2 * b:2 * b + 2, :], ALU.add).then_inc(z_ready[s].sem, 1)

        def statistics(s, it):
            stat_chain[s].start(dve, it)
            wait(dve, z_ready, s, it, 2)
            norm.statistics(stat_chain[s], s, z[s])

        staged(dve,
               (NOW, lambda it: residual(B, it)),
               (NEXT, lambda it: low(B, it)),
               (NOW, lambda it: norm.take_offset(dve, it, A)),
               (NOW, lambda it: statistics(B, it)),
               (NEXT, lambda it: residual(A, it)),
               (LATER, lambda it: low(A, it)),
               (NOW, lambda it: norm.take_offset(dve, it, B)),
               (NEXT, lambda it: statistics(A, it)))


def layer2(p, src, dst):
    nc = p.nc
    with ExitStack() as own:
        ROWS = P // HD
        HP = HEADS // 2
        VW = 2 * HD + 2
        QK_BANK = (2, 3, 0, 1)
        w_parts, wp_parts, rows = p.weights.qkv, p.weights.proj, p.rows
        two = lambda name, shape, dt=F32: [p.sb(f"l2_{name}{s}", shape, dt, stack=own) for s in SLOTS]
        x_tok, y_tok = p.stream.x_tok, p.stream.y_tok
        x_parts = [(p.sb(f"l2_xhi{s}", [P, CH, GROUP], F32R, stack=own), p.sb(f"l2_xlo{s}", [P, CH, GROUP], F32R, stack=own))
                   for s in SLOTS]
        o_parts = [(p.sb(f"l2_ohi{s}", [P, CH, GROUP], F32R, stack=own), p.sb(f"l2_olo{s}", [P, CH, GROUP], F32R, stack=own))
                   for s in SLOTS]
        q_t = two("q", [P, CH, GROUP])
        k_t = two("k", [P, CH, GROUP])
        v_pair = two("vpair", [P, PER_TILE, TILES, HP, VW])
        v_stage = two("vstage", [P, TILES, HP, HD])
        prob = two("prob", [P, TILES, HEADS, NODES])
        prob_t = two("probt", [P, TILES, BANK])
        mx = two("mx", [P, ROWS, TILES * CH])
        inv = two("inv", [P, TILES, HP, 2])
        o_tok = two("otok", [P, TILES, DIM])
        t_ln = two("tln", [P, TILES, DIM])
        res = two("res", [P, TILES, DIM])
        inner, outer = Norm(p, "l2i", own), Norm(p, "l2o", own)

        blank, ones = (p.sem(f"l2_{n}") for n in ("blank", "ones"))
        loaded, x_free, y_ready, stored = p.stream.open(src, dst)
        turned = p.signals("l2_turned", CH)
        hi_ready = p.signals("l2_hi_ready", CH)
        lo_ready = p.signals("l2_lo_ready", CH)
        qk_done = p.signals("l2_qk_done", 2 * CH)
        qk_ready = p.signals("l2_qk_ready", 2 * CH)
        v_done = p.signals("l2_v_done", 1)
        v_staged = p.signals("l2_v_staged", 1)
        v_swapped = [p.signals(f"l2_v_swapped{b}_", 16) for b in range(PER_TILE)]
        scored = p.signals("l2_scored", ROWS)
        shifted = p.signals("l2_shifted", 1)
        exp_done = p.signals("l2_exp_done", TILES)
        prob_turned = p.signals("l2_prob_turned", TILES)
        prob_t_ready = p.signals("l2_prob_t_ready", TILES)
        pv_done = p.signals("l2_pv_done", TILES, 1)
        o_ready = p.signals("l2_o_ready", 1, 1)
        o_turned = p.signals("l2_o_turned", CH)
        o_hi_ready = p.signals("l2_o_hi_ready", CH)
        o_lo_ready = p.signals("l2_o_lo_ready", CH)
        proj_done = p.signals("l2_proj_done", 2, 1)
        proj_ready = p.signals("l2_proj_ready", 2, 1)
        sum_ready = p.signals("l2_sum_ready", 1)
        z_ready = p.signals("l2_z_ready", 1, 1)
        mid_chain = Chain(p.sem("l2_mid_chain"), 2 * 4)
        tail_chain = Chain(p.sem("l2_tail_chain"), 2 * 4)

        def wait(eng, signal, s, it, n):
            eng.wait_ge(signal[s].sem, signal[s].at(it, n))

        def two_tiles(s, bank):
            return p.ps[s][:, bank, :].rearrange("p (t f) -> p t f", t=2)

        def values(s, b, parity):
            q = slice(b * NODES, (b + 1) * NODES)
            v = p.ps[s][q, 2:4, :].rearrange("p b (t g e d) -> p (b t) g e d", t=2, e=2, d=HD)
            return v[:, :, :, parity, :]

        with nc.Block() as block:

            @block.sync
            def _(sp):
                stream = p.stream

                def load(it):
                    if not (isinstance(it, int) and it == 0):
                        for s in SLOTS:
                            stream.load(sp, s, it)

                def store(it):
                    for s in SLOTS:
                        stream.store(sp, s, it)

                def swap(it):
                    for s in SLOTS:
                        wait(sp, v_staged, s, it, 1)
                        for b in range(PER_TILE):
                            here = slice(b * NODES, (b + 1) * NODES)
                            there = slice((1 - b) * NODES, (2 - b) * NODES)
                            sp.dma_start(v_pair[s][there, b, :, :, (1 - b) * HD:(2 - b) * HD],
                                         v_stage[s][here, :, :, :]).then_inc(v_swapped[b][s].sem, 16)

                stream.all_stored(sp)
                staged(sp,
                       (NOW, swap),
                       (NEXT, load),
                       (NOW, store),
                       before_last=lambda: stream.load_next_first(sp))

            @block.gpsimd
            def _(pool):
                for s in SLOTS:
                    nc.gpsimd.memset(v_pair[s][:, :, :, :, :], 0.0).then_inc(blank, 1)

                def over_tiles(row):
                    return row[:, :].unsqueeze(1).to_broadcast([P, TILES, DIM])

                def mid(it):
                    for s in SLOTS:
                        wait(pool, turned, s, it, CH)
                        wait(pool, z_ready, s, it, 0)
                        nc.gpsimd.tensor_tensor(res[s][:, :, :], x_tok[s][:, :, :], over_tiles(rows["ln_beta"]),
                                                ALU.add).then_inc(x_free[s].sem, 1)

                def tail(it):
                    for s in SLOTS:
                        inner.root(pool, it, s)
                    for s in SLOTS:
                        wait(pool, x_free, s, it, 1)
                        nc.gpsimd.tensor_tensor(res[s][:, :, :], res[s][:, :, :], o_tok[s][:, :, :],
                                                ALU.add).then_inc(sum_ready[s].sem, 1)
                    for s in SLOTS:
                        outer.root(pool, it, s)

                staged(pool, (NOW, mid), (NOW, tail))

            @block.tensor
            def _(pe):
                for s in SLOTS:
                    pe.sem_inc(pv_done[s].sem, 1)
                    pe.sem_inc(proj_done[s].sem, 1)

                def turn(s, rows_, bank, done):
                    for k in range(CH):
                        for t in range(TILES):
                            ins = nc.tensor.transpose(p.ps[s][:, bank + k, t * P:(t + 1) * P],
                                                      rows_[:, t, k * P:(k + 1) * P], p.ident[:, :])
                        ins.then_inc(done[s].sem, 1)

                def rows_by_weights(s, t, bank, of, weights, f0):
                    q = slice(t * P, (t + 1) * P)
                    for k in range(CH):
                        ins = matmul3(nc, p.ps[s][:, bank + t // 2, (t % 2) * DIM:(t % 2 + 1) * DIM],
                                      (of[0][:, k, q], of[1][:, k, q]),
                                      (weights[0][:, k, f0:f0 + DIM], weights[1][:, k, f0:f0 + DIM]),
                                      k == 0, k == CH - 1)
                    return ins

                def front(it):
                    for s in SLOTS:
                        wait(pe, loaded, s, it, 16)
                        wait(pe, o_ready, s, it, 0)
                        turn(s, x_tok[s], 2, turned)

                def project(s, it, m):
                    if m == 0:
                        wait(pe, lo_ready, s, it, CH)
                    if m == CH:
                        wait(pe, proj_ready, s, it, 0)
                    for k in range(CH):
                        q = slice(m * P, (m + 1) * P)
                        ins = matmul3(nc, p.ps[s][:, QK_BANK[m], :], (w_parts[0][:, k, q], w_parts[1][:, k, q]),
                                      (x_parts[s][0][:, k, :], x_parts[s][1][:, k, :]), k == 0, k == CH - 1)
                    ins.then_inc(qk_done[s].sem, 1)

                def project_v(s, it):
                    wait(pe, qk_ready, s, it, CH)
                    for t in range(TILES):
                        ins = rows_by_weights(s, t, 2, x_parts[s], w_parts, 2 * DIM)
                    ins.then_inc(v_done[s].sem, 1)

                def mask(s, it):
                    wait(pe, qk_ready, s, it, 2 * CH)
                    wait(pe, v_staged, s, it, 1)
                    for r in range(ROWS):
                        nc.tensor.matmul(p.ps[s][:, r, :], p.ident_bf[:, :],
                                         p.mask_bias[:, :].unsqueeze(1).to_broadcast([P, TILES * CH, NODES]),
                                         start=True, stop=False, skip_group_check=True)

                def score(s, t):
                    for c in range(CH):
                        for b in range(PER_TILE):
                            for r in range(ROWS):
                                q = slice(t * P + b * NODES, t * P + (b + 1) * NODES)
                                col = (t * CH + c) * NODES
                                ins = nc.tensor.matmul(
                                    p.ps[s][b * NODES:(b + 1) * NODES, r, col:col + NODES],
                                    q_t[s][r * HD:(r + 1) * HD, c, q], k_t[s][r * HD:(r + 1) * HD, c, q],
                                    start=False, stop=True, skip_group_check=True)
                                if (t, c, b) == (TILES - 1, CH - 1, PER_TILE - 1):
                                    ins.then_inc(scored[s].sem, 1)

                def turn_prob(s, it, t):
                    wait(pe, exp_done, s, it, t + 1)
                    for g in range(HP):
                        ins = nc.tensor.transpose(p.ps[s][:, t, g * P:(g + 1) * P],
                                                  prob[s][:, t, 2 * g:2 * g + 2, :].rearrange("p h j -> p (h j)"),
                                                  p.ident[:, :])
                    ins.then_inc(prob_turned[s].sem, 1)

                def attend(s, it):
                    pe.wait_ge(ones, 4)
                    for b in range(PER_TILE):
                        wait(pe, v_swapped[b], s, it, 16)
                    for t in range(TILES):
                        wait(pe, prob_t_ready, s, it, t + 1)
                        for g in range(HP):
                            for b in range(PER_TILE):
                                at = g * P + b * NODES
                                ins = nc.tensor.matmul(p.ps[s][b * NODES:(b + 1) * NODES, t, g * VW:(g + 1) * VW],
                                                       prob_t[s][:, t, at:at + NODES], v_pair[s][:, b, t, g, :],
                                                       start=True, stop=True)
                        ins.then_inc(pv_done[s].sem, 1)

                def mid(it):
                    A, B = SLOTS
                    for m in range(2 * CH):
                        project(A, it, m)
                    project_v(A, it)
                    project(B, it, 0)
                    project(B, it, 1)
                    mask(A, it)
                    score(A, 0)
                    project(B, it, 2)
                    score(A, 1)
                    project_v(B, it)
                    score(A, 2)
                    project(B, it, 3)
                    score(A, 3)
                    mask(B, it)
                    for t in range(TILES):
                        score(B, t)
                    for s in SLOTS:
                        for t in range(TILES):
                            turn_prob(s, it, t)
                        attend(s, it)
                    wait(pe, o_ready, 0, it, 1)
                    turn(0, o_tok[0], 0, o_turned)

                def tail(it):
                    wait(pe, o_ready, 1, it, 1)
                    turn(1, o_tok[1], 0, o_turned)
                    for s in SLOTS:
                        wait(pe, o_lo_ready, s, it, CH)
                        for t in range(TILES):
                            ins = rows_by_weights(s, t, 0, o_parts[s], wp_parts, 0)
                            if t % 2:
                                ins.then_inc(proj_done[s].sem, 1)

                for s in SLOTS:
                    pe.sem_inc(o_ready[s].sem, 1)
                staged(pe, (NOW, mid), (NEXT, front), (NOW, tail))

            @block.scalar
            def _(act):
                act.wait_ge(blank, 2)

                def high(s, it, bank, done, parts, ready):
                    for k in range(CH):
                        wait(act, done, s, it, k + 1)
                        nc.scalar.activation(parts[s][0][:, k, :], p.ps[s][:, bank + k, :], ACT.Copy).then_inc(ready[s].sem, 1)

                def high_o(s, it):
                    wait(act, proj_done, s, it, 0)
                    high(s, it, 0, o_turned, o_parts, o_hi_ready)

                def front(it):
                    for s in SLOTS:
                        high(s, it, 2, turned, x_parts, hi_ready)

                def take_qk(s, it, chunks):
                    for m in chunks:
                        wait(act, qk_done, s, it, m + 1)
                        bank = p.ps[s][:, QK_BANK[m], :]
                        if m < CH:
                            ins = nc.scalar.activation(q_t[s][:, m, :], bank, ACT.Copy, scale=float(HD) ** -0.5)
                        else:
                            ins = nc.scalar.activation(k_t[s][:, m - CH, :], bank, ACT.Copy)
                        ins.then_inc(qk_ready[s].sem, 1)

                def take_v(s, it):
                    wait(act, v_done, s, it, 1)
                    wait(act, pv_done, s, it, 0)
                    for b in range(PER_TILE):
                        q = slice(b * NODES, (b + 1) * NODES)
                        nc.scalar.activation(v_pair[s][q, b, :, :, b * HD:(b + 1) * HD], values(s, b, b), ACT.Copy)
                        ins = nc.scalar.activation(v_stage[s][q, :, :, :], values(s, b, 1 - b), ACT.Copy)
                    ins.then_inc(v_staged[s].sem, 1)

                def mid(it):
                    take_qk(0, it, range(2 * CH))
                    take_v(0, it)
                    take_qk(1, it, range(2 * CH - 1))
                    take_v(1, it)
                    take_qk(1, it, [2 * CH - 1])
                    for s in SLOTS:
                        wait(act, shifted, s, it, 1)
                        for t in range(TILES):
                            nc.scalar.activation(prob[s][:, t, :, :], prob[s][:, t, :, :], ACT.Exp).then_inc(exp_done[s].sem, 1)
                        for t in range(TILES):
                            wait(act, prob_turned, s, it, t + 1)
                            nc.scalar.activation(prob_t[s][:, t, :], p.ps[s][:, t, :], ACT.Copy).then_inc(prob_t_ready[s].sem, 1)
                    high_o(0, it)

                staged(act, (NOW, mid), (NEXT, front), (NOW, lambda it: high_o(1, it)))

            @block.vector
            def _(dve):
                dve.wait_ge(blank, 2)
                for s in SLOTS:
                    for e in range(2):
                        q = slice(e * NODES, (e + 1) * NODES)
                        nc.vector.memset(v_pair[s][q, :, :, :, 2 * HD + e], 1.0).then_inc(ones, 1)
                    for signal in (proj_ready, z_ready):
                        dve.sem_inc(signal[s].sem, 1)

                def lower(s, it, bank, parts, hi, lo):
                    for k in range(CH):
                        wait(dve, hi, s, it, k + 1)
                        nc.vector.tensor_tensor(parts[s][1][:, k, :], p.ps[s][:, bank + k, :],
                                                parts[s][0][:, k, :].bitcast(F32), ALU.subtract).then_inc(lo[s].sem, 1)

                def front(it):
                    for s in SLOTS:
                        lower(s, it, 2, x_parts, hi_ready, lo_ready)

                def mid(it):
                    mid_chain.start(dve, it)
                    link = mid_chain.link
                    for s in SLOTS:
                        def scores(r):
                            return p.ps[s][:, r, :].rearrange("p (t c j) -> p t c j", t=TILES, c=CH)

                        by_bank = prob[s][:, :, :, :].rearrange("p t (c r) j -> p t c r j", c=CH)
                        for r0 in (0, 2):
                            for r in (r0, r0 + 1):
                                wait(dve, scored, s, it, r + 1)
                                ins = nc.vector.tensor_reduce(mx[s][:, r, :], p.ps[s][:, r, :].rearrange(
                                    "p (n j) -> p n j", j=NODES), AX.X, ALU.max)
                            link(ins)
                            for r in (r0, r0 + 1):
                                m = mx[s][:, r, :].rearrange("p (t c) -> p t c", t=TILES).unsqueeze(3).to_broadcast(
                                    [P, TILES, CH, NODES])
                                ins = nc.vector.tensor_tensor(by_bank[:, :, :, r, :], scores(r), m, ALU.subtract)
                        ins.then_inc(shifted[s].sem, 1)
                    for s in SLOTS:
                        heads = p.ps[s][:, :, 0:HP * VW].rearrange("p t (g c) -> p t g c", g=HP)
                        wait(dve, pv_done, s, it, TILES)
                        link(nc.vector.reciprocal(inv[s][:, :, :, :], heads[:, :, :, 2 * HD:VW]))
                        flat = inv[s][:, :, :, :].rearrange("p t g e -> p (t g e)")
                        link(nc.vector.tensor_scalar(flat, flat, p.nan_rows[:, :], None, ALU.add))
                        for t in range(TILES):
                            ins = nc.vector.tensor_tensor(
                                o_tok[s][:, t, :].rearrange("p (g e d) -> p g e d", g=HP, e=2),
                                heads[:, t, :, 0:2 * HD].rearrange("p g (e d) -> p g e d", e=2),
                                inv[s][:, t, :, :].unsqueeze(3).to_broadcast([P, HP, 2, HD]), ALU.mult)
                        ins.then_inc(o_ready[s].sem, 1)
                    lower(0, it, 0, o_parts, o_hi_ready, o_lo_ready)

                def tail(it):
                    tail_chain.start(dve, it)
                    link = tail_chain.link
                    lower(1, it, 0, o_parts, o_hi_ready, o_lo_ready)
                    for s in SLOTS:
                        for b in range(2):
                            wait(dve, proj_done, s, it, b + 1)
                            nc.vector.tensor_tensor(o_tok[s][:, 2 * b:2 * b + 2, :], two_tiles(s, b),
                                                    rows["b_proj"][:, :].unsqueeze(1).to_broadcast([P, 2, DIM]),
                                                    ALU.add).then_inc(proj_ready[s].sem, 1)
                    for s in SLOTS:
                        wait(dve, proj_ready, s, it, 2)
                        inner.statistics(tail_chain, s, o_tok[s])
                    for s in SLOTS:
                        wait(dve, y_ready, s, it, 0)
                        link(inner.apply(dve, it, s, o_tok[s], t_ln[s]))
                        link(nc.vector.tensor_tensor(t_ln[s][:, :, :], t_ln[s][:, :, :],
                                                     rows["ln_gamma"][:, :].unsqueeze(1).to_broadcast([P, TILES, DIM]),
                                                     ALU.mult))
                    for s in SLOTS:
                        wait(dve, sum_ready, s, it, 1)
                        nc.vector.tensor_tensor(t_ln[s][:, :, :], t_ln[s][:, :, :], res[s][:, :, :],
                                                ALU.add).then_inc(z_ready[s].sem, 1)
                        wait(dve, z_ready, s, it, 1)
                        outer.statistics(tail_chain, s, t_ln[s])
                    for s in SLOTS:
                        wait(dve, stored, s, it, 0)
                        outer.apply(dve, it, s, t_ln[s], y_tok[s]).then_inc(y_ready[s].sem, 1)

                staged(dve, (NOW, mid), (NEXT, front), (NOW, tail))


def layer3(p, src, dst):
    nc = p.nc
    STEPS = 3
    A, B = SLOTS
    with ExitStack() as own:
        parts, biases = p.weights.gates, p.weights.biases
        two = lambda name, shape, dt=F32: [p.sb(f"l3_{name}{s}", shape, dt, stack=own) for s in SLOTS]
        x_tok, y_tok = p.stream.x_tok, p.stream.y_tok
        h_tok = two("htok", [P, TILES, DIM])
        h = two("h", [P, CH, GROUP])
        h_hi = two("hhi", [P, CH, GROUP], F32R)
        h_lo = two("hlo", [P, CH, GROUP], F32R)
        a_hi = two("ahi", [P, CH, GROUP], F32R)
        a_lo = two("alo", [P, CH, GROUP], F32R)
        r = two("r", [P, CH, GROUP])
        rh_hi = two("rhhi", [P, CH, GROUP], F32R)
        rh_lo = two("rhlo", [P, CH, GROUP], F32R)
        d = two("d", [P, CH, GROUP])
        z = two("z", [P, TILES, DIM])
        norm = Norm(p, "l3", own)

        each = CH * STEPS
        loaded, x_free, y_ready, stored = p.stream.open(src, dst, x_readers=2)
        x_turned = p.signals("l3_x_turned", CH)
        adj_done = p.signals("l3_adj_done", each)
        r_done = p.signals("l3_r_done", each)
        z_done = p.signals("l3_z_done", each)
        hv_done = p.signals("l3_hv_done", each)
        tok_done = p.signals("l3_tok_done", each)
        h_hi_ready = p.signals("l3_h_hi_ready", each)
        h_lo_ready = p.signals("l3_h_lo_ready", each)
        a_hi_ready = p.signals("l3_a_hi_ready", each)
        a_lo_ready = p.signals("l3_a_lo_ready", each)
        r_ready = p.signals("l3_r_ready", each)
        rh_ready = p.signals("l3_rh_ready", each)
        rh_hi_ready = p.signals("l3_rh_hi_ready", each)
        rh_lo_ready = p.signals("l3_rh_lo_ready", each)
        z_ready = p.signals("l3_z_ready", each)
        hv_ready = p.signals("l3_hv_ready", each)
        h_new = p.signals("l3_h_new", each)
        tok_ready = p.signals("l3_tok_ready", CH * (STEPS - 1))
        mid_chain = Chain(p.sem("l3_mid_chain"), 2 * 2 * STEPS)
        tail_chain = Chain(p.sem("l3_tail_chain"), 2)

        RZ = [p.ps[s][:, 0:2, :] for s in SLOTS]
        HV = [p.ps[s][:, 2:4, :] for s in SLOTS]

        def wait(eng, signal, s, it, n):
            eng.wait_ge(signal[s].sem, signal[s].at(it, n))

        with nc.Block() as block:
            @block.sync
            def _(sp):
                p.stream.run(sp, last=True, lead=NEXT)
                p.stream.all_stored(sp, PAIRS)

            @block.tensor
            def _(pe):
                def turn_x(s, it):
                    wait(pe, loaded, s, it, 16)
                    wait(pe, x_free, s, it, 0)
                    for k in range(CH):
                        for t in range(TILES):
                            ins = nc.tensor.transpose(RZ[s][:, k, t * P:(t + 1) * P],
                                                      x_tok[s][:, t, k * P:(k + 1) * P], p.ident[:, :])
                        ins.then_inc(x_turned[s].sem, 1)

                def aggregate(s, step, it):
                    if step:
                        wait(pe, tok_ready, s, it, CH * step)
                    nodes = h_tok[s] if step else x_tok[s]
                    for k in range(CH):
                        for t in range(TILES):
                            ins = nc.tensor.matmul(HV[s][:, k, t * P:(t + 1) * P], nodes[:, t, k * P:(k + 1) * P],
                                                   p.adj_t[:, :], start=True, stop=True)
                        ins.then_inc(adj_done[s].sem, 1)

                def product(out, name, m, hi, lo, first, last):
                    for k in range(CH):
                        q = slice(m * P, (m + 1) * P)
                        ins = matmul3(nc, out[:, m, :], (parts[name][0][:, k, q], parts[name][1][:, k, q]),
                                      (hi[:, k, :], lo[:, k, :]), first and k == 0, last and k == CH - 1)
                    return ins

                def gates_from_a(s, step, it):
                    wait(pe, h_hi_ready, s, it, CH * (step + 1))
                    wait(pe, h_lo_ready, s, it, CH * (step + 1))
                    for m in range(CH):
                        product(RZ[s], "u3", m, h_hi[s], h_lo[s], True, False)
                    wait(pe, a_lo_ready, s, it, CH * (step + 1))
                    for m in range(CH):
                        product(RZ[s], "w4s", m, a_hi[s], a_lo[s], False, True).then_inc(r_done[s].sem, 1)
                    for m in range(CH):
                        product(HV[s], "w5s", m, a_hi[s], a_lo[s], True, False)

                def gate_z(s, step, it):
                    for m in range(CH):
                        wait(pe, r_ready, s, it, CH * step + m + 1)
                        product(RZ[s], "diff", m, a_hi[s], a_lo[s], False, True).then_inc(z_done[s].sem, 1)

                def candidate(s, step, it):
                    wait(pe, rh_lo_ready, s, it, CH * (step + 1))
                    for m in range(CH):
                        product(HV[s], "u5", m, rh_hi[s], rh_lo[s], False, True).then_inc(hv_done[s].sem, 1)

                def turn_h(s, step, it):
                    wait(pe, h_new, s, it, CH * (step + 1))
                    for b in range(2):
                        for t in range(2):
                            for k in range(CH):
                                q = slice((2 * b + t) * P, (2 * b + t + 1) * P)
                                at = t * DIM + k * P
                                ins = nc.tensor.transpose(RZ[s][:, b, at:at + P], h[s][:, k, q], p.ident[:, :])
                        ins.then_inc(tok_done[s].sem, 1)

                def front(it):
                    turn_x(A, it)
                    aggregate(A, 0, it)

                def mid(it):
                    for step in range(STEPS):
                        gates_from_a(A, step, it)
                        turn_h(B, step - 1, it) if step else turn_x(B, it)
                        gate_z(A, step, it)
                        candidate(A, step, it)
                        aggregate(B, step, it)
                        gates_from_a(B, step, it)
                        turn_h(A, step, it)
                        gate_z(B, step, it)
                        candidate(B, step, it)
                        if step < STEPS - 1:
                            aggregate(A, step + 1, it)

                staged(pe, (NOW, mid), (NEXT, front), (NOW, lambda it: turn_h(B, STEPS - 1, it)))

            @block.scalar
            def _(act):
                def take_x(s, it):
                    for k in range(CH):
                        wait(act, x_turned, s, it, k + 1)
                        nc.scalar.activation(h[s][:, k, :], RZ[s][:, k, :], ACT.Copy)
                        nc.scalar.activation(h_hi[s][:, k, :], RZ[s][:, k, :], ACT.Copy).then_inc(h_hi_ready[s].sem, 1)

                def a_high(s, step, it):
                    for k in range(CH):
                        wait(act, adj_done, s, it, CH * step + k + 1)
                        nc.scalar.activation(a_hi[s][:, k, :], HV[s][:, k, :], ACT.Copy).then_inc(a_hi_ready[s].sem, 1)

                def gate_r(s, step, it):
                    for m in range(CH):
                        wait(act, r_done, s, it, CH * step + m + 1)
                        nc.scalar.activation(r[s][:, m, :], RZ[s][:, m, :], ACT.Sigmoid,
                                             bias=biases["r"][:, m:m + 1]).then_inc(r_ready[s].sem, 1)
                    for m in range(CH):
                        wait(act, rh_ready, s, it, CH * step + m + 1)
                        nc.scalar.activation(rh_hi[s][:, m, :], r[s][:, m, :], ACT.Copy).then_inc(rh_hi_ready[s].sem, 1)

                def gate_z(s, step, it):
                    for m in range(CH):
                        wait(act, z_done, s, it, CH * step + m + 1)
                        nc.scalar.activation(RZ[s][:, m, :], RZ[s][:, m, :], ACT.Sigmoid,
                                             bias=biases["z"][:, m:m + 1]).then_inc(z_ready[s].sem, 1)

                def candidate(s, step, it):
                    for m in range(CH):
                        wait(act, hv_done, s, it, CH * step + m + 1)
                        nc.scalar.activation(HV[s][:, m, :], HV[s][:, m, :], ACT.Tanh,
                                             bias=biases["h"][:, m:m + 1]).then_inc(hv_ready[s].sem, 1)

                def h_high(s, step, it):
                    for m in range(CH):
                        wait(act, h_new, s, it, CH * step + m + 1)
                        nc.scalar.activation(h_hi[s][:, m, :], h[s][:, m, :], ACT.Copy).then_inc(h_hi_ready[s].sem, 1)

                def take_h(s, step, it):
                    for b in range(2):
                        wait(act, tok_done, s, it, 2 * step + b + 1)
                        nc.scalar.activation(h_tok[s][:, 2 * b:2 * b + 2, :],
                                             RZ[s][:, b, :].rearrange("p (t f) -> p t f", t=2),
                                             ACT.Copy).then_inc(tok_ready[s].sem, 1)

                def front(it):
                    take_x(A, it)
                    a_high(A, 0, it)

                def mid(it):
                    for step in range(STEPS):
                        if step:
                            h_high(B, step - 1, it)
                        gate_r(A, step, it)
                        take_h(B, step - 1, it) if step else take_x(B, it)
                        gate_z(A, step, it)
                        candidate(A, step, it)
                        a_high(B, step, it)
                        if step < STEPS - 1:
                            h_high(A, step, it)
                        gate_r(B, step, it)
                        if step < STEPS - 1:
                            take_h(A, step, it)
                        gate_z(B, step, it)
                        candidate(B, step, it)
                        if step < STEPS - 1:
                            a_high(A, step + 1, it)

                staged(act, (NOW, mid), (NEXT, front))

            @block.gpsimd
            def _(pool):
                def h_low(s, step, it):
                    for m in range(CH):
                        wait(pool, h_hi_ready, s, it, CH * step + m + 1)
                        nc.gpsimd.tensor_tensor(h_lo[s][:, m, :], h[s][:, m, :], h_hi[s][:, m, :].bitcast(F32),
                                                ALU.subtract).then_inc(h_lo_ready[s].sem, 1)

                def mid(it):
                    for step in range(STEPS):
                        h_low(B, step, it)
                        if step < STEPS - 1:
                            h_low(A, step + 1, it)

                def tail(it):
                    for s in SLOTS:
                        norm.root(pool, it, s)

                staged(pool, (NOW, mid), (NEXT, lambda it: h_low(A, 0, it)), (NOW, tail))

            @block.vector
            def _(dve):
                def a_low(s, step, it):
                    for k in range(CH):
                        wait(dve, a_hi_ready, s, it, CH * step + k + 1)
                        nc.vector.tensor_tensor(a_lo[s][:, k, :], HV[s][:, k, :], a_hi[s][:, k, :].bitcast(F32),
                                                ALU.subtract).then_inc(a_lo_ready[s].sem, 1)

                def reset(s, step, it):
                    for m in range(CH):
                        wait(dve, r_ready, s, it, CH * step + m + 1)
                        nc.vector.tensor_tensor(r[s][:, m, :], r[s][:, m, :], h[s][:, m, :],
                                                ALU.mult).then_inc(rh_ready[s].sem, 1)
                    for m in range(CH):
                        wait(dve, rh_hi_ready, s, it, CH * step + m + 1)
                        nc.vector.tensor_tensor(rh_lo[s][:, m, :], r[s][:, m, :], rh_hi[s][:, m, :].bitcast(F32),
                                                ALU.subtract).then_inc(rh_lo_ready[s].sem, 1)

                def update(s, step, it):
                    for m in range(CH):
                        wait(dve, hv_ready, s, it, CH * step + m + 1)
                        ins = nc.vector.tensor_tensor(d[s][:, m, :], HV[s][:, m, :], h[s][:, m, :], ALU.subtract)
                    mid_chain.link(ins)
                    for m in range(CH):
                        wait(dve, z_ready, s, it, CH * step + m + 1)
                        ins = nc.vector.tensor_tensor(d[s][:, m, :], RZ[s][:, m, :], d[s][:, m, :], ALU.mult)
                    mid_chain.link(ins)
                    for m in range(CH):
                        nc.vector.tensor_tensor(h[s][:, m, :], h[s][:, m, :], d[s][:, m, :],
                                                ALU.add).then_inc(h_new[s].sem, 1)

                def residual(s, it):
                    wait(dve, y_ready, s, it, 0)
                    for b in range(2):
                        wait(dve, tok_done, s, it, 2 * (STEPS - 1) + b + 1)
                        nc.vector.tensor_tensor(z[s][:, 2 * b:2 * b + 2, :],
                                                RZ[s][:, b, :].rearrange("p (t f) -> p t f", t=2),
                                                x_tok[s][:, 2 * b:2 * b + 2, :], ALU.add).then_inc(x_free[s].sem, 1)

                def mid(it):
                    mid_chain.start(dve, it)
                    for step in range(STEPS):
                        if step:
                            update(B, step - 1, it)
                        reset(A, step, it)
                        a_low(B, step, it)
                        update(A, step, it)
                        reset(B, step, it)
                        if step < STEPS - 1:
                            a_low(A, step + 1, it)
                    residual(A, it)
                    update(B, STEPS - 1, it)

                def tail(it):
                    tail_chain.start(dve, it)
                    residual(B, it)
                    for s in SLOTS:
                        wait(dve, x_free, s, it, CH)
                        norm.statistics(tail_chain, s, z[s])
                    for s in SLOTS:
                        wait(dve, stored, s, it, 0)
                        norm.apply(dve, it, s, z[s], y_tok[s]).then_inc(y_ready[s].sem, 1)

                staged(dve, (NOW, mid), (NEXT, lambda it: a_low(A, 0, it)), (NOW, tail))


def build(nc, a, out):
    with ExitStack() as stack:
        p = Program(nc, a, out, stack)
        p.stream = Stream(p)
        p.weights = Weights(p)
        tokens = [a["x"].rearrange("b n d -> (b n) d")]
        tokens += [nc.dram_tensor(f"x_after_{n}", (GRAPHS * NODES, DIM), F32, kind="Internal").ap() for n in range(3)]
        tokens += [out.rearrange("b n d -> (b n) d")]
        x = [p.view(t) for t in tokens]
        with ExitStack() as own, nc.Block() as block:
            constants(p, block, own)
            raw = load_weights(p, block, own)
            p.operand = [[p.sb(f"operand_{q}{s}", [P, CH, GROUP], F32R, stack=own) for s in SLOTS] for q in ("hi", "lo")]
            gate_sums(p, block, raw)
            layer0(p, block, own, raw, x[0], x[1])
            split_gates(p, block)
            layer1(p, block, own, raw, x[1], x[2])
            split_attention(p, block, raw)
        p.clear_semaphores()
        layer2(p, x[2], x[3])
        p.clear_semaphores()
        layer3(p, x[3], x[4])
        p.clear_semaphores()


_OUT = ((GRAPHS, NODES, DIM), "float32")


def kernel(**inputs):
    import numpy as _np
    import concourse.bacc as _bacc
    from concourse import mybir as _mybir
    from concourse.bass_utils import run_bass_kernel_spmd as _run

    nc = _bacc.Bacc("TRN2", target_bir_lowering=False, num_devices=1)
    arrays, args = {}, {}
    for name in inputs:
        a = _np.ascontiguousarray(inputs[name])
        arrays[f"in_{name}_dram"] = a
        args[name] = nc.dram_tensor(f"in_{name}_dram", a.shape, _mybir.dt.from_np(a.dtype), kind="ExternalInput").ap()
    out = nc.dram_tensor("out_0_dram", _OUT[0], _mybir.dt.from_np(_np.dtype(_OUT[1])), kind="ExternalOutput").ap()
    build(nc, args, out)
    r = _run(nc, [arrays], core_ids=[0])
    return r.results[0]["out_0_dram"]
```
